# Optimizing a Trainium2 kernel written in Bass

```python
import numpy as np
import jax
import jax.numpy as jnp

def _softmax(x, axis=-1):
    return jax.nn.softmax(x, axis=axis)

def _gelu(x):
    return jax.nn.gelu(x, approximate=True)

def _silu(x):
    return jax.nn.silu(x)

def _sigmoid(x):
    return jax.nn.sigmoid(x)

def _layernorm(x, axis=-1, eps=1e-05):
    m = jnp.mean(x, axis=axis, keepdims=True)
    v = jnp.var(x, axis=axis, keepdims=True)
    return (x - m) / jnp.sqrt(v + eps)

def _scatter_add(tgt, idx, src, axis=0):
    return tgt.at[idx].add(src)

def _segment_sum(src, seg, n):
    return jax.ops.segment_sum(src, seg, n)
kernel_name = 'mk_flamingo_gated_d2_seqx_r8_d0606f'

def setup_inputs(seed: int=0):
    np.random.seed(seed)
    _w = jnp.asarray

    def _rec_inputs():
        import jax
        import jax.numpy as jnp
        _rk = jax.random.key(seed)
        x = -0.000125 + 0.9999 * jax.random.normal(jax.random.fold_in(_rk, 1), (32, 128, 128), jnp.float32)
        _lenS = 128 - jax.random.randint(jax.random.fold_in(_rk, 7), (32,), 0, max(1, 128 // 4) + 1, jnp.int32)
        _lenS2 = 77 - jax.random.randint(jax.random.fold_in(_rk, 8), (32,), 0, max(1, 77 // 4) + 1, jnp.int32)
        _ctx_2048P = jax.random.normal(jax.random.fold_in(_rk, 11), (32, 16, 256), jnp.float32)
        _ctx_2048c = jax.random.dirichlet(jax.random.fold_in(_rk, 511), 0.3 * jnp.ones((16,), jnp.float32), (32, 77))
        _ctx_2048t = jnp.einsum('bsk,bkd->bsd', _ctx_2048c, _ctx_2048P)
        _ctx_2048t = _ctx_2048t * jax.lax.rsqrt(jnp.mean(jnp.square(_ctx_2048t)) + 1e-12) * 0.953939
        ctx_2048 = -1.39393e-06 + 0.999914 * (_ctx_2048t + 0.3 * jax.random.normal(jax.random.fold_in(_rk, 611), (32, 77, 256), jnp.float32))
        _validS = jnp.arange(128)[None, :] < _lenS[:, None]
        _validS2 = jnp.arange(77)[None, :] < _lenS2[:, None]
        _causal = jnp.tril(jnp.ones((128, 128), dtype=bool))
        mask_BxS2_if0 = jnp.where(jnp.ones((32, 77), dtype=bool), 4, 0).astype(jnp.int32)
        _g = jax.random.normal(jax.random.fold_in(_rk, 9001), (2, 2), jnp.float32)
        _g = jnp.sign(_g) * jnp.maximum(jnp.abs(_g), 1.0) + (_g == 0) * 1.0
        g_xattn = _g[0]
        g_ffn = _g[1]
        return (x, ctx_2048, mask_BxS2_if0, g_xattn, g_ffn)
    x, ctx_2048, mask_BxS2_if0, g_xattn, g_ffn = _rec_inputs()

    def _L0_xattn_setup():
        import jax, jax.numpy as jnp
        import numpy as np
        B, N, DIM = (8, 512, 128)
        M, CTX = (32, 256)
        HEADS, DH = (16, 64)
        INNER = HEADS * DH
        EPS = 1e-06

        def _split_heads(t):
            b, n, _ = t.shape
            return t.reshape(b, n, HEADS, DH).transpose(0, 2, 1, 3)
        key = jax.random.key(seed)
        ks = jax.random.split(key, 6)
        x = jax.random.normal(ks[0], (B, N, DIM), dtype=jnp.float32)
        context = jax.random.normal(ks[1], (B, M, CTX), dtype=jnp.float32)
        Wq = jax.random.normal(ks[2], (DIM, INNER), dtype=jnp.float32) / np.sqrt(DIM)
        Wkv = jax.random.normal(ks[3], (CTX, 2 * INNER), dtype=jnp.float32) / np.sqrt(CTX)
        null_kv = jax.random.normal(ks[4], (2, DH), dtype=jnp.float32) / np.sqrt(2.0)
        Wout = jax.random.normal(ks[5], (INNER, DIM), dtype=jnp.float32) / np.sqrt(INNER)
        ln_scale = jnp.ones((DIM,), dtype=jnp.float32)
        ln_bias = jnp.zeros((DIM,), dtype=jnp.float32)
        return {'x': x, 'context': context, 'Wq': Wq, 'Wkv': Wkv, 'null_kv': null_kv, 'Wout': Wout, 'ln_scale': ln_scale, 'ln_bias': ln_bias}
    _L0_xattn_all = _L0_xattn_setup()
    _L0_xattn_in = {k: v for k, v in _L0_xattn_all.items() if k in ('Wq', 'Wkv', 'null_kv', 'Wout', 'ln_scale', 'ln_bias')}
    del _L0_xattn_all

    def _L0_ffn_setup():
        import jax, jax.numpy as jnp
        import numpy as np
        B, S, D_MODEL, D_HIDDEN = (4, 256, 128, 512)

        def act_quant(x):
            scale = 127.0 / jnp.clip(jnp.max(jnp.abs(x), axis=-1, keepdims=True), 1e-05)
            return jnp.clip(jnp.round(x * scale), -128, 127) / scale

        def weight_quant(w):
            scale = 1.0 / jnp.clip(jnp.mean(jnp.abs(w)), 1e-05)
            return jnp.clip(jnp.round(w * scale), -1, 1) / scale

        def bit_linear(x, w):
            xq = x + jax.lax.stop_gradient(act_quant(x) - x)
            wq = w + jax.lax.stop_gradient(weight_quant(w) - w)
            return jnp.einsum('bsd,hd->bsh', xq, wq)

        def depthwise_conv1d(x_bcl, w, b):
            y = jax.lax.conv_general_dilated(x_bcl, w, window_strides=(1,), padding=[(1, 1)], dimension_numbers=('NCH', 'OIH', 'NCH'), feature_group_count=x_bcl.shape[1])
            return y + b[None, :, None]
        key = jax.random.key(seed)
        ks = jax.random.split(key, 5)
        lim1 = 1.0 / np.sqrt(D_MODEL)
        lim2 = 1.0 / np.sqrt(D_HIDDEN)
        limc = 1.0 / np.sqrt(3.0)
        return {'x': jax.random.normal(ks[0], (B, S, D_MODEL), dtype=jnp.float32), 'w1': jax.random.uniform(ks[1], (D_HIDDEN, D_MODEL), jnp.float32, -lim1, lim1), 'conv_w': jax.random.uniform(ks[2], (D_HIDDEN, 1, 3), jnp.float32, -limc, limc), 'conv_b': jax.random.uniform(ks[3], (D_HIDDEN,), jnp.float32, -limc, limc), 'w2': jax.random.uniform(ks[4], (D_MODEL, D_HIDDEN), jnp.float32, -lim2, lim2)}
    _L0_ffn_all = _L0_ffn_setup()
    _L0_ffn_in = {k: v for k, v in _L0_ffn_all.items() if k in ('w1', 'conv_w', 'conv_b', 'w2')}
    del _L0_ffn_all

    def _L1_xattn_setup():
        import jax, jax.numpy as jnp
        import numpy as np
        B, L, P = (4, 512, 128)
        D_MODEL = 128
        D_GLOBAL = 256
        HEADDIM = 32
        EPSILON = 0.001
        RMS_EPS = 1e-05

        def rmsnorm(x, g, eps=RMS_EPS):
            var = jnp.mean(jnp.square(x), axis=-1, keepdims=True)
            return x * jax.lax.rsqrt(var + eps) * g

        def _hnet_depool(h, h_patch_full, patch_lens):
            h_patch = h_patch_full[..., :D_MODEL]
            bsz, plen = (h_patch.shape[0], h_patch.shape[1])
            seqlen = h.shape[1]
            logp = jnp.full((bsz, plen), -EPSILON, dtype=jnp.float32)
            bidx = jnp.cumsum(patch_lens, axis=1) - 1
            boundary_mask = jnp.zeros((bsz, seqlen), dtype=jnp.int32)
            boundary_mask = boundary_mask.at[jnp.arange(bsz)[:, None], bidx].set(1)
            dt = (-jnp.log(-jnp.expm1(logp))).astype(h_patch.dtype)
            x = h_patch / dt[..., None]
            n_heads = D_MODEL // HEADDIM
            A = -jnp.ones((n_heads,), dtype=jnp.float32)
            bcoef = jnp.exp(logp).astype(h_patch.dtype)
            x4 = x.reshape(bsz, plen, n_heads, HEADDIM)
            a = jnp.exp(dt[:, :, None] * A[None, None, :])
            u = (dt * bcoef)[:, :, None, None] * x4
            a_b = jnp.broadcast_to(a[..., None], u.shape)

            def comb(lft, rgt):
                aL, uL = lft
                aR, uR = rgt
                return (aL * aR, uL * aR + uR)
            _, s = jax.lax.associative_scan(comb, (a_b, u), axis=1)
            depool = s.reshape(bsz, plen, D_MODEL)
            plug = jnp.clip(jnp.cumsum(boundary_mask, axis=1) - 1, 0, plen - 1)
            depool_out = depool[jnp.arange(bsz)[:, None], plug]
            return depool_out + h
        key = jax.random.key(seed)
        k1, k2, k3, k4 = jax.random.split(key, 4)
        embeds = jax.random.normal(k1, (B, L, D_MODEL), dtype=jnp.float32)
        patch_embeds = jax.random.normal(k2, (B, P, D_GLOBAL), dtype=jnp.float32)
        patch_lens = jnp.full((B, P), L // P, dtype=jnp.int64)
        W_in = jax.random.normal(k3, (D_MODEL, D_MODEL), dtype=jnp.float32) * 0.02
        b_in = jnp.zeros((D_MODEL,), dtype=jnp.float32)
        g_res = jnp.ones((D_MODEL,), dtype=jnp.float32)
        g_init = jnp.ones((D_GLOBAL,), dtype=jnp.float32)
        return {'embeds': embeds, 'patch_embeds': patch_embeds, 'patch_lens': patch_lens, 'W_in': W_in, 'b_in': b_in, 'g_res': g_res, 'g_init': g_init}
    _L1_xattn_all = _L1_xattn_setup()
    _L1_xattn_in = {k: v for k, v in _L1_xattn_all.items() if k in ('W_in', 'b_in', 'g_res', 'g_init')}
    del _L1_xattn_all

    def _L1_ffn_setup():
        import jax, jax.numpy as jnp
        import numpy as np
        D_MODEL, D_FF, N_EXPERTS, TOP_K = (128, 512, 8, 2)
        key = jax.random.key(seed)
        k0, k1, k2, k3 = jax.random.split(key, 4)
        x = jax.random.normal(k0, (2, 256, D_MODEL), dtype=jnp.float32)
        Wg = jax.random.normal(k1, (D_MODEL, N_EXPERTS), dtype=jnp.float32) * 0.02
        W1 = jax.random.normal(k2, (N_EXPERTS, D_MODEL, D_FF), dtype=jnp.float32) * 0.02
        b1 = jnp.zeros((N_EXPERTS, D_FF), dtype=jnp.float32)
        W2 = jax.random.normal(k3, (N_EXPERTS, D_FF, D_MODEL), dtype=jnp.float32) * 0.02
        b2 = jnp.zeros((N_EXPERTS, D_MODEL), dtype=jnp.float32)
        return {'x': x, 'Wg': Wg, 'W1': W1, 'b1': b1, 'W2': W2, 'b2': b2}
    _L1_ffn_all = _L1_ffn_setup()
    _L1_ffn_in = {k: v for k, v in _L1_ffn_all.items() if k in ('Wg', 'W1', 'b1', 'W2', 'b2')}
    del _L1_ffn_all
    return {'x': x, 'ctx_2048': ctx_2048, 'mask_BxS2_if0': mask_BxS2_if0, 'g_xattn': g_xattn, 'g_ffn': g_ffn, 'L0_xattn_Wq': _L0_xattn_in['Wq'], 'L0_xattn_Wkv': _L0_xattn_in['Wkv'], 'L0_xattn_null_kv': _L0_xattn_in['null_kv'], 'L0_xattn_Wout': _L0_xattn_in['Wout'], 'L0_xattn_ln_scale': _L0_xattn_in['ln_scale'], 'L0_xattn_ln_bias': _L0_xattn_in['ln_bias'], 'L0_ffn_w1': _L0_ffn_in['w1'], 'L0_ffn_conv_w': _L0_ffn_in['conv_w'], 'L0_ffn_conv_b': _L0_ffn_in['conv_b'], 'L0_ffn_w2': _L0_ffn_in['w2'], 'L1_xattn_W_in': _L1_xattn_in['W_in'], 'L1_xattn_b_in': _L1_xattn_in['b_in'], 'L1_xattn_g_res': _L1_xattn_in['g_res'], 'L1_xattn_g_init': _L1_xattn_in['g_init'], 'L1_ffn_Wg': _L1_ffn_in['Wg'], 'L1_ffn_W1': _L1_ffn_in['W1'], 'L1_ffn_b1': _L1_ffn_in['b1'], 'L1_ffn_W2': _L1_ffn_in['W2'], 'L1_ffn_b2': _L1_ffn_in['b2']}

def reference(x, ctx_2048, mask_BxS2_if0, g_xattn, g_ffn, L0_xattn_Wq, L0_xattn_Wkv, L0_xattn_null_kv, L0_xattn_Wout, L0_xattn_ln_scale, L0_xattn_ln_bias, L0_ffn_w1, L0_ffn_conv_w, L0_ffn_conv_b, L0_ffn_w2, L1_xattn_W_in, L1_xattn_b_in, L1_xattn_g_res, L1_xattn_g_init, L1_ffn_Wg, L1_ffn_W1, L1_ffn_b1, L1_ffn_W2, L1_ffn_b2):
    import jax
    import jax.numpy as jnp

    def _L0_xattn_ref(x, context, Wq, Wkv, null_kv, Wout, ln_scale, ln_bias):
        import jax, jax.numpy as jnp
        import numpy as np
        B, N, DIM = (8, 512, 128)
        M, CTX = (32, 256)
        HEADS, DH = (16, 64)
        INNER = HEADS * DH
        EPS = 1e-06

        def _split_heads(t):
            b, n, _ = t.shape
            return t.reshape(b, n, HEADS, DH).transpose(0, 2, 1, 3)
        scale = DH ** (-0.5)
        b = x.shape[0]
        q = _split_heads(jnp.einsum('bnd,df->bnf', x, Wq))
        kv = jnp.einsum('bmc,cf->bmf', context, Wkv)
        k, v = jnp.split(kv, 2, axis=-1)
        k, v = (_split_heads(k), _split_heads(v))
        nk = jnp.broadcast_to(null_kv[0], (b, HEADS, 1, DH))
        nv = jnp.broadcast_to(null_kv[1], (b, HEADS, 1, DH))
        k = jnp.concatenate((nk, k), axis=-2)
        v = jnp.concatenate((nv, v), axis=-2)
        q = q * scale
        sim = jnp.einsum('bhid,bhjd->bhij', q, k)
        attn = jax.nn.softmax(sim, axis=-1)
        out = jnp.einsum('bhij,bhjd->bhid', attn, v)
        out = out.transpose(0, 2, 1, 3).reshape(b, -1, INNER)
        out = jnp.einsum('bnf,fd->bnd', out, Wout)
        mu = jnp.mean(out, axis=-1, keepdims=True)
        var = jnp.var(out, axis=-1, keepdims=True)
        out = (out - mu) * jax.lax.rsqrt(var + EPS) * ln_scale + ln_bias
        return out

    def _L0_ffn_ref(x, w1, conv_w, conv_b, w2):
        import jax, jax.numpy as jnp
        import numpy as np
        B, S, D_MODEL, D_HIDDEN = (4, 256, 128, 512)

        def act_quant(x):
            scale = 127.0 / jnp.clip(jnp.max(jnp.abs(x), axis=-1, keepdims=True), 1e-05)
            return jnp.clip(jnp.round(x * scale), -128, 127) / scale

        def weight_quant(w):
            scale = 1.0 / jnp.clip(jnp.mean(jnp.abs(w)), 1e-05)
            return jnp.clip(jnp.round(w * scale), -1, 1) / scale

        def bit_linear(x, w):
            xq = x + jax.lax.stop_gradient(act_quant(x) - x)
            wq = w + jax.lax.stop_gradient(weight_quant(w) - w)
            return jnp.einsum('bsd,hd->bsh', xq, wq)

        def depthwise_conv1d(x_bcl, w, b):
            y = jax.lax.conv_general_dilated(x_bcl, w, window_strides=(1,), padding=[(1, 1)], dimension_numbers=('NCH', 'OIH', 'NCH'), feature_group_count=x_bcl.shape[1])
            return y + b[None, :, None]
        h = bit_linear(x, w1)
        h = depthwise_conv1d(h.transpose(0, 2, 1), conv_w, conv_b)
        h = h.transpose(0, 2, 1)
        h = jax.nn.silu(h)
        return bit_linear(h, w2)

    def _L1_xattn_ref(embeds, patch_embeds, patch_lens, W_in, b_in, g_res, g_init):
        import jax, jax.numpy as jnp
        import numpy as np
        B, L, P = (4, 512, 128)
        D_MODEL = 128
        D_GLOBAL = 256
        HEADDIM = 32
        EPSILON = 0.001
        RMS_EPS = 1e-05

        def rmsnorm(x, g, eps=RMS_EPS):
            var = jnp.mean(jnp.square(x), axis=-1, keepdims=True)
            return x * jax.lax.rsqrt(var + eps) * g

        def _hnet_depool(h, h_patch_full, patch_lens):
            h_patch = h_patch_full[..., :D_MODEL]
            bsz, plen = (h_patch.shape[0], h_patch.shape[1])
            seqlen = h.shape[1]
            logp = jnp.full((bsz, plen), -EPSILON, dtype=jnp.float32)
            bidx = jnp.cumsum(patch_lens, axis=1) - 1
            boundary_mask = jnp.zeros((bsz, seqlen), dtype=jnp.int32)
            boundary_mask = boundary_mask.at[jnp.arange(bsz)[:, None], bidx].set(1)
            dt = (-jnp.log(-jnp.expm1(logp))).astype(h_patch.dtype)
            x = h_patch / dt[..., None]
            n_heads = D_MODEL // HEADDIM
            A = -jnp.ones((n_heads,), dtype=jnp.float32)
            bcoef = jnp.exp(logp).astype(h_patch.dtype)
            x4 = x.reshape(bsz, plen, n_heads, HEADDIM)
            a = jnp.exp(dt[:, :, None] * A[None, None, :])
            u = (dt * bcoef)[:, :, None, None] * x4
            a_b = jnp.broadcast_to(a[..., None], u.shape)

            def comb(lft, rgt):
                aL, uL = lft
                aR, uR = rgt
                return (aL * aR, uL * aR + uR)
            _, s = jax.lax.associative_scan(comb, (a_b, u), axis=1)
            depool = s.reshape(bsz, plen, D_MODEL)
            plug = jnp.clip(jnp.cumsum(boundary_mask, axis=1) - 1, 0, plen - 1)
            depool_out = depool[jnp.arange(bsz)[:, None], plug]
            return depool_out + h
        h = rmsnorm(embeds, g_res)
        h = jnp.einsum('bld,ed->ble', h, W_in) + b_in
        h_patch = rmsnorm(patch_embeds, g_init)
        return _hnet_depool(h, h_patch, patch_lens)

    def _L1_ffn_ref(x, Wg, W1, b1, W2, b2):
        import jax, jax.numpy as jnp
        import numpy as np
        D_MODEL, D_FF, N_EXPERTS, TOP_K = (128, 512, 8, 2)
        B = x.shape[:-1]
        xs = x.reshape(-1, x.shape[-1])
        T = xs.shape[0]
        gate_logits = xs @ Wg
        weights, sel = jax.lax.top_k(gate_logits, TOP_K)
        weights = jax.nn.softmax(weights.astype(jnp.float32), axis=1).astype(x.dtype)
        h = jax.nn.relu(jnp.einsum('td,edf->etf', xs, W1) + b1[:, None, :])
        out_e = jnp.einsum('etf,efd->etd', h, W2) + b2[:, None, :]
        tok = jnp.arange(T)
        picked = out_e[sel, tok[:, None]]
        out = jnp.einsum('tk,tkd->td', weights, picked)
        return out.reshape(*B, x.shape[-1])
    x = x + jnp.tanh(g_xattn[0]) * _L0_xattn_ref(_layernorm(x, axis=-1), ctx_2048, L0_xattn_Wq, L0_xattn_Wkv, L0_xattn_null_kv, L0_xattn_Wout, L0_xattn_ln_scale, L0_xattn_ln_bias)
    x = x + jnp.tanh(g_ffn[0]) * _L0_ffn_ref(_layernorm(x, axis=-1), L0_ffn_w1, L0_ffn_conv_w, L0_ffn_conv_b, L0_ffn_w2)
    x = x + jnp.tanh(g_xattn[1]) * _L1_xattn_ref(_layernorm(x, axis=-1), ctx_2048, mask_BxS2_if0, L1_xattn_W_in, L1_xattn_b_in, L1_xattn_g_res, L1_xattn_g_init)
    x = x + jnp.tanh(g_ffn[1]) * _L1_ffn_ref(_layernorm(x, axis=-1), L1_ffn_Wg, L1_ffn_W1, L1_ffn_b1, L1_ffn_W2, L1_ffn_b2)
    return x

_drawn_inputs = setup_inputs


def setup_inputs(seed=0):
    import zlib

    import numpy as np

    out = dict(_drawn_inputs(seed))
    spreads = {'g_ffn': (-1.0, 0.6),
     'L0_xattn_ln_scale': (1.0, 0.2),
     'L0_xattn_ln_bias': (0.0, 0.1),
     'L1_xattn_b_in': (0.0, 0.1),
     'L1_xattn_g_res': (1.0, 0.58),
     'L1_xattn_g_init': (1.0, 0.2),
     'L1_ffn_b1': (0.0, 0.714),
     'L1_ffn_b2': (0.0, 0.1)}
    factors = {'L0_xattn_null_kv': 4.307}
    for name, (base, spread) in spreads.items():
        noise = np.random.default_rng([zlib.crc32(name.encode()), seed]).standard_normal(out[name].shape)
        drawn = base * np.exp(spread * noise) if base else spread * noise
        out[name] = jnp.asarray(drawn.astype(out[name].dtype))
    for name, factor in factors.items():
        out[name] = (out[name] * factor).astype(out[name].dtype)
    return out
```

```python
from contextlib import ExitStack

import numpy as np

import concourse.bass as bass
from concourse import mybir

F32 = mybir.dt.float32
F32R = mybir.dt.float32r
BF16 = mybir.dt.bfloat16
I32 = mybir.dt.int32
U32 = mybir.dt.uint32
ALU = mybir.AluOpType
ACT = mybir.ActivationFunctionType
AX = mybir.AxisListType

MAGIC = 1.5 * 2.0**23
LN_EPS = 1e-5
XATTN_EPS = 1e-6
QUANT_FLOOR = 1e-5
PATCH_CLIP = 65536.0


def need(eng, sem, count):
    if isinstance(count, int) and count <= 0:
        return
    eng.wait_ge(sem, count)


def chain(eng, sem, count):
    done = [0]

    def link(ins, wait=need):
        done[0] += 1
        ins.then_inc(sem, 1)
        wait(eng, sem, count + done[0])

    return link


def build(nc, a, out):
    B, S, D = a["x"].shape
    J, C = a["ctx_2048"].shape[1:]
    INNER = a["L0_xattn_Wq"].shape[1]
    DH = a["L0_xattn_null_kv"].shape[1]
    H = INNER // DH
    F = a["L0_ffn_w1"].shape[0]
    E = a["L1_ffn_Wg"].shape[1]
    FF = a["L1_ffn_W1"].shape[2]
    assert S == 128 and D == 128 and C == 256 and DH == 64 and B % 4 == 0
    GB = 4
    NG = B // GB
    QH = H // 4
    JN = J + 1
    CC = C // 128
    FC = F // 128
    FFC = FF // 128
    SCALE = DH**-0.5
    POWERS = 12
    CT_LAST = 4 * (NG - 2) + 3 + 8 + 1

    logp = np.float32(-0.001)
    dt = np.float32(-np.log(-np.expm1(logp)))
    decay = float(np.exp(-dt))
    gain = float(np.exp(logp))

    ctx = ExitStack()
    with ctx:
        def sb(name, shape, dtype=F32):
            return ctx.enter_context(nc.sbuf_tensor(name, shape, dtype))

        def sem(name):
            return ctx.enter_context(nc.semaphore(name))

        x_res = sb("x_res", [128, B, D])
        G = sb("G", [128, 2, GB, H, JN])
        A_hi = sb("A_hi", [128, CC, H, D], F32R)
        A_lo = sb("A_lo", [128, CC, H, D], F32R)
        wv_hi = sb("wv_hi", [128, CC, INNER], F32R)
        wv_lo = sb("wv_lo", [128, CC, INNER], F32R)
        ctxT_hi = sb("ctxT_hi", [128, 2, CC, GB * J], F32R)
        ctxT_lo = sb("ctxT_lo", [128, 2, CC, GB * J], F32R)
        ctxv_hi = sb("ctxv_hi", [128, 2, CC, J], F32R)
        ctxv_lo = sb("ctxv_lo", [128, 2, CC, J], F32R)
        tap_hi = sb("tap_hi", [128, 3, F], F32R)
        tap_lo = sb("tap_lo", [128, 3, F], F32R)
        w_out = sb("w_out", [128, INNER // 128, D])
        w2q = sb("w2q", [128, FC, D], BF16)
        w_inT = sb("w_inT", [128, D])
        w_gate = sb("w_gate", [128, E])
        plug_rows = sb("plug_rows", [J, B, S], BF16)
        xsT_in = sb("xsT_in", [128, 2, GB, S])
        ident = sb("ident", [128, 128])
        ident_bf = sb("ident_bf", [128, 128], BF16)
        ones = sb("ones", [128, 128])
        scanT = sb("scanT", [J, J])
        patch_no = sb("patch_no", [J, 1])
        conv_b = sb("conv_b", [128, F])
        ln_gain = sb("ln_gain", [128, D])
        ln_shift = sb("ln_shift", [128, D])
        b_in = sb("b_in", [J, D])
        g_init = sb("g_init", [J, D])
        g_res = sb("g_res", [128, 1])
        gates = sb("gates", [128, 4])
        w2_gain = sb("w2_gain", [128, 1])
        wsum = sb("wsum", [128, 2])
        wmean = sb("wmean", [128, 2])
        winv = sb("winv", [128, 2])
        half = sb("half", [128, 1])
        tap_gain = sb("tap_gain", [128, FC, 3])
        nullk = sb("nullk", [128, 2])
        gnull = sb("gnull", [128, H])
        b1c = sb("b1c", [128, E, FFC])
        expert_no = sb("expert_no", [128, E])
        gp = sb("gp", [128, 5, B])

        rows = sb("rows", [J, 2, C])
        patch = sb("patch", [J, 2, C])
        h1 = sb("h1", [128, D])
        hT = sb("hT", [128, 2, S])
        top = sb("top", [128, 2, QH])
        shifted = sb("shifted", [128, 2, QH, JN])
        probs = sb("probs", [128, 2, QH, JN])
        probsT = sb("probsT", [JN, 2, QH, S])
        V = sb("V", [JN, 2, H, DH + 1])
        rden = sb("rden", [128, 2, QH])
        attn = sb("attn", [128, 2, QH * DH])
        attnT = sb("attnT", [128, 2, INNER // 128, S])
        xb = sb("xb", [128, D])
        y1 = sb("y1", [128, D])
        y2 = sb("y2", [128, D])
        h2 = sb("h2", [128, D])
        z2 = sb("z2", [128, D])
        xq = sb("xq", [128, D])
        xqT_hi = sb("xqT_hi", [128, S + 2], F32R)
        xqT_lo = sb("xqT_lo", [128, S + 2], F32R)
        ffn = sb("ffn", [128, 4, F])
        conv, tanh_c, act2, z3 = (ffn[:, i, :] for i in range(4))
        q3 = sb("q3", [128, F], BF16)
        q3T = sb("q3T", [128, FC, S], BF16)
        h3 = sb("h3", [128, D])
        h3T = sb("h3T", [128, S])
        hp = sb("hp", [J, D])
        dep = sb("dep", [J, D])
        pick = sb("pick", [J, S])
        xs = sb("xs", [128, D])
        xsT = sb("xsT", [128, S])
        raw1, raw2, raw3, raw4, rawy = (sb(f"raw_{n}", [128, 6]) for n in ("x", "x2", "x3", "x4", "y"))
        mv1, mv2, mv3, mv4, mvy = (sb(f"mv_{n}", [128, 2]) for n in ("x", "x2", "x3", "x4", "y"))
        var1, var2, var3, var4, vary = (sb(f"var_{n}", [128, 1]) for n in ("x", "x2", "x3", "x4", "y"))
        r1, r2, r3, r4, ry = (sb(f"rstd_{n}", [128, 1]) for n in ("x", "x2", "x3", "x4", "y"))
        ratio3 = sb("ratio3", [128, 3])
        rawc = sb("raw_c", [J, 6])
        mvc = sb("mv_c", [J, 2])
        msc = sb("ms_c", [J, 2])
        rc = sb("rstd_c", [J, 1])
        qs2 = sb("qs2", [128, 3])
        qs3 = sb("qs3", [128, 3])
        back3 = sb("back3", [128, 2])
        best = sb("best", [128, 8])
        best_at = sb("best_at", [128, 8], U32)
        best_all = sb("best_all", [128, B, 2])
        at_all = sb("at_all", [128, B, 2])

        flat = G[:, :, :, :, :].rearrange("p a b h j -> p (a b h j)")
        taken = [0]

        def part(n):
            taken[0] += n
            assert taken[0] <= 2 * GB * H * JN
            return flat[:, taken[0] - n:taken[0]]

        wq = part(INNER)
        wk = part(CC * INNER).rearrange("p (c n) -> p c n", c=CC)
        wqT = part(INNER).rearrange("p (h d) -> p h d", d=D)
        wkT = part(CC * INNER).rearrange("p (h c) -> p h c", c=C)
        w1 = part(FC * D).rearrange("p (c d) -> p c d", c=FC)
        w2 = part(F)
        wtap = part(FC * 3 * D).rearrange("p (c t d) -> p c t d", c=FC, t=3)
        w_in = part(D)
        w2t = part(F // 2).bitcast(BF16)
        eW1 = flat[:, 0:E * FF].rearrange("p (e f) -> p e f", e=E)
        b2r = flat[:, 2 * E * FF:2 * E * FF + E * D].rearrange("p (e d) -> p e d", e=E)
        gw = flat[:, 2 * E * FF + E * D:2 * E * FF + E * D + 3 * B * E].rearrange("p (i b e) -> p i b e", i=3, b=B)
        moe = w_out[:, :, :].rearrange("p (a t) d -> p a t d", a=2)
        eW2 = flat[:, E * FF:2 * E * FF].rearrange("p (e c d) -> p e c d", e=E, c=FFC)
        wv = ffn[:, :, :].rearrange("p (c a) n -> p c (a n)", c=CC)
        eq = attnT[:, :, :, :].rearrange("p a c s -> p (a c s)")[:, 0:16 * J].bitcast(BF16).rearrange(
            "p (t j) -> p t j", t=32)
        hid = [ffn[:, :, :], attnT[:, :, :, :].rearrange("p a (c e) s -> p (a c) (e s)", e=4)]
        len_i = sb("len_i", [128, J], I32)
        len_f = sb("len_f", [128, J])
        len_sum = sb("len_sum", [128, J])
        len_wrap = sb("len_wrap", [128, J])
        token_no = sb("token_no", [128, 32])
        edge = sb("edge", [128, 32])
        edges = sb("edges", [B, S])
        edge_sum = sb("edge_sum", [B, S])
        zero_row = sb("zero_row", [128, 128])
        plug = sb("plug", [B, S], BF16)

        bank = [ctx.enter_context(nc.psum_tensor(f"bank{i}", [128, 512], F32)) for i in range(8)]
        SC, PT, AV, YH, GC, VO, T1, T2 = bank

        edge_d = nc.dram_tensor("edge_d", (B, S), F32, kind="Internal").ap()
        xsT_d = nc.dram_tensor("xsT_d", (B, 128, S), F32, kind="Internal").ap()
        plug_d = nc.dram_tensor("plug_d", (B, S), BF16, kind="Internal").ap()

        ld_names = ["wq", "wk", "x0", "x1", "wv", "wout", "len", "small", "row", "edge", "plug_st", "plug", "moe"]
        ld = {n: sem(f"loaded_{n}") for n in ld_names}
        ld_rows = [sem(f"loaded_rows{i}") for i in range(2)]
        ld_patch = [sem(f"loaded_patch{i}") for i in range(2)]
        prep_pe = sem("prep_pe")
        prep_act = sem("prep_act")
        prep_dve = sem("prep_dve")
        prep_pool = sem("prep_pool")
        prep_chain = sem("prep_chain")
        prep_split = sem("prep_split")
        edge_ready = sem("edge_ready")
        plug_ready = sem("plug_ready")
        wsum_ready = sem("wsum_ready")
        wtap_ready = sem("wtap_ready")
        w2t_ready = sem("w2t_ready")
        gates_ready = sem("gates_ready")
        shift_ready = sem("shift_ready")
        main_ready = sem("main_ready")
        names = """s_done pT_done av_done oT_done G_done V_done xT_done conv_done qT_done w2_done hT_done
            T3_done L1_done T4_done gate_done dep_done cT_done y_done
            exp_ready oT_ready pT_ready G_ready xThi_ready T3_ready cThi_ready hT_ready tanh_ready qT_ready xsT_ready
            norm_ready sub_ready V_ready h1_ready h3_ready xTlo_ready cTlo_ready pick_ready conv_ready z_ready
            xq_ready x3_ready x4_ready xs_ready hp_ready dep_ready gate_taken y_taken x2_ready
            st1 st2 st3 st4 sty stc rs1 rs2 rs3 rs4 rsy rsc q_ready xb_ready cv_ready
            c_soft c_norm c_y c_st c_h2 c_conv c_gate c_pool1 c_pool2 c_pool3 c_pool4 c_pooly c_poolc
            g_exp gw_ready h_done hid_ready o_done moe_taken moe_sum stored c_moe g_in xsT_stored xsT_in0 xsT_in1 xsT_used""".split()
        m = {n: sem(n) for n in names}

        raw_sem = [sem(f"raw_{n}") for n in ("y", "x", "x2", "x3", "x4", "c")]

        def valid(b, n=B):
            return not isinstance(b, int) or 0 <= b < n

        def apart(eng, sem, count):
            if isinstance(count, int) and count <= 0:
                return
            if not isinstance(count, int):
                at = counts[eng.engine]
                eng.reg_mov(at, count)
                count = at
            eng.wait_ge(main_ready, 1)
            eng.wait_ge(sem, count)

        def upto(n, last):
            return min(n, last) if isinstance(n, int) else n

        def back(b, q, k, d):
            return b + (q - d) // 4, (q - d) % 4, (k + (q - d) // 4) % 4

        def program(eng, slot):
            def group(g):
                for j in range(16):
                    slot(g, j // 4, j % 4, 4 * g + j // 4, 16 * g + j)

            for g in (-2, -1, 0, 1):
                group(g)
            with eng.Fori(2, NG - 1) as g:
                group(g)
            for g in (NG - 1, NG):
                group(g)

        counts = {e.engine: e.alloc_register(f"count_{i}") for i, e in enumerate((nc.vector, nc.gpsimd))}
        block = ctx.enter_context(nc.Block())

        SMALL = 17
        LEN_LOADS = 4
        NULL_LOADS = 4

        @block.sync
        def _(sp):
            kv = a["L0_xattn_Wkv"].rearrange("(c p) n -> p c n", p=128)
            sp.dma_start(rows[:, 0, :], a["ctx_2048"][0]).then_inc(ld_rows[0], 16)
            sp.dma_start(wq, a["L0_xattn_Wq"]).then_inc(ld["wq"], 16)
            sp.dma_start(wk, kv[:, :, 0:INNER]).then_inc(ld["wk"], 16)
            sp.dma_start(x_res[:, 0:8, :], a["x"][0:8].rearrange("b s d -> s b d")).then_inc(ld["x0"], 16)
            sp.dma_start(wv, kv[:, :, INNER:2 * INNER]).then_inc(ld["wv"], 16)
            sp.dma_start(x_res[:, 8:B, :], a["x"][8:B].rearrange("b s d -> s b d")).then_inc(ld["x1"], 16)
            sp.dma_start(w_out[:, :, :], a["L0_xattn_Wout"].rearrange("(c p) n -> p c n", p=128)).then_inc(ld["wout"], 16)
            nk = a["L0_xattn_null_kv"]
            sp.wait_ge(prep_pool, 2)
            for i in range(2):
                sp.dma_start(nullk[64 * i:64 * i + 64, i:i + 1], nk[0:1, :].rearrange("o d -> d o")).then_inc(ld["small"], 16)
                sp.dma_start(V[J:JN, i, :, 0:DH], nk[1:2, :].unsqueeze(1).broadcast_to([1, H, DH])).then_inc(ld["small"], 16)
            sp.wait_ge(edge_ready, 1)
            for i in range(4):
                sp.dma_start(edge_d[:, 32 * i:32 * i + 32], edge[B * i:B * i + B, :]).then_inc(ld["edge"], 16)
            sp.wait_ge(ld["edge"], 64)
            sp.dma_start(edges[:, :], edge_d).then_inc(ld["row"], 16)
            sp.wait_ge(plug_ready, 1)
            sp.dma_start(plug_d, plug[:, :]).then_inc(ld["plug_st"], 16)
            sp.wait_ge(ld["plug_st"], 16)
            sp.dma_start(plug_rows[:, :, :], plug_d.partition_broadcast(J)).then_inc(ld["plug"], 16)

            def slot(g, k, q, b, s):
                if q == 0:
                    if not isinstance(b, int) or 0 <= b + 9 < CT_LAST:
                        need(sp, m["cT_done"], b + 8)
                        sp.dma_start(rows[:, (k + 1) % 2, :], a["ctx_2048"][(b + 9) % B]).then_inc(ld_rows[(k + 1) % 2], 16)
                    if valid(b - 1):
                        need(sp, m["hp_ready"], b - 2)
                        sp.dma_start(patch[:, (k + 1) % 2, :], a["ctx_2048"][b - 1]).then_inc(ld_patch[(k + 1) % 2], 16)

                if q == 1 and valid(b - 4):
                    sp.wait_ge(m["xsT_ready"], b - 3)
                    sp.dma_start(xsT_d[b - 4], xsT[:, :]).then_inc(m["xsT_stored"], 16)

            program(sp, slot)
            for i in range(2):
                sp.wait_ge(ld_rows[i], 16 * ((CT_LAST + 2 - i) // 2))
            sp.wait_ge(m["s_done"], 4 * B)
            sp.dma_start(eW1, a["L1_ffn_W1"].rearrange("e p f -> p e f")).then_inc(ld["moe"], 16)
            sp.dma_start(eW2, a["L1_ffn_W2"].rearrange("e (c p) d -> p e c d", p=128)).then_inc(ld["moe"], 16)
            sp.dma_start(b2r, a["L1_ffn_b2"].partition_broadcast(128)).then_inc(ld["moe"], 16)
            sp.wait_ge(m["xsT_stored"], 16 * B)
            xsT_v = xsT_d.rearrange("(t b) p s -> t p b s", b=GB)
            out_v = out.rearrange("(t b) s d -> t s b d", b=GB)

            def load_x(t, i):
                sp.dma_start(xsT_in[:, i, :, :], xsT_v[t]).then_inc(m[f"xsT_in{i}"], 16)

            def store(t):
                sp.wait_ge(m["moe_sum"], 4 * E * (t + 1))
                sp.dma_start(out_v[t], x_res[:, bass.ds(4 * t, 4), :]).then_inc(m["stored"], 16)

            load_x(0, 0)
            load_x(1, 1)
            with sp.Fori(0, NG // 2 - 1) as u:
                for i in range(2):
                    store(2 * u + i)
                    sp.wait_ge(m["h_done"], FFC * E * (2 * u + i + 1))
                    load_x(2 * u + i + 2, i)
            for i in range(2):
                store(NG - 2 + i)
            sp.wait_ge(m["stored"], 16 * NG)

        @block.gpsimd
        def _(pool):
            pool.memset(nullk[:, :], 0.0).then_inc(prep_pool, 1)
            pool.memset(V[:, :, :, :], 1.0).then_inc(prep_pool, 1)
            pool.memset(ident[:, :], 0.0).then_inc(prep_pool, 1)
            pool.memset(ones[:, :], 1.0).then_inc(prep_pool, 1)
            pool.memset(half[:, :], -0.5).then_inc(prep_pool, 1)
            pool.memset(xqT_hi[:, :].bitcast(F32), 0.0).then_inc(prep_pool, 1)
            pool.memset(xqT_lo[:, :].bitcast(F32), 0.0).then_inc(prep_pool, 1)
            pool.memset(scanT[:, :], 0.0).then_inc(prep_pool, 1)
            pool.memset(zero_row[:, :], 0.0).then_inc(prep_pool, 1)
            pool.wait_ge(prep_pool, 9)
            step = chain(pool, prep_pool, 9)
            step(pool.affine_select(out=ident[:, :], in_=ident[:, :], compare_op=ALU.not_equal, fill=1.0, base=0,
                                    pattern=[[-1, 128]], channel_multiplier=1))
            for i in range(4):
                step(pool.iota(token_no[32 * i:32 * i + 32, :], pattern=[[1, 32]], base=32 * i, channel_multiplier=0,
                               allow_small_or_imprecise_dtypes=True))
            step(pool.iota(patch_no[:, :], pattern=[[0, 1]], base=1, channel_multiplier=1,
                           allow_small_or_imprecise_dtypes=True))
            step(pool.iota(expert_no[:, :], pattern=[[1, E]], base=0, channel_multiplier=0,
                           allow_small_or_imprecise_dtypes=True))
            pool.tensor_copy(ident_bf[:, :], ident[:, :]).then_inc(prep_pool, 1)
            k = 0
            while k < POWERS:
                pool.wait_ge(prep_pool, 17 + k)
                pool.affine_select(out=scanT[:, :], in_=scanT[:, :], compare_op=ALU.not_equal,
                                   fill=gain * decay**k, base=k, pattern=[[-1, J]], channel_multiplier=1)\
                    .then_inc(prep_pool, 1)
                k += 1

            def rstd(b, var, root, ready, sem_c, src, eps, stat):
                apart(pool, stat, b + 1)
                step = chain(pool, sem_c, b)
                step(pool.tensor_scalar(var[:, :], src, eps, None, ALU.add))
                pool.tensor_tensor(root[:, :], var[:, :], half[0:root.shape[0], :], ALU.pow).then_inc(ready, 1)

            def slot(g, k, q, b, s):
                if q == 0:
                    if valid(b - 4):
                        rstd(b - 4, var4, r4, m["rs4"], m["c_pool4"], mv4[:, 1:2], LN_EPS, m["st4"])
                    if valid(b - 2):
                        rstd(b - 2, vary, ry, m["rsy"], m["c_pooly"], mvy[:, 1:2], XATTN_EPS, m["sty"])
                    if valid(b + 1):
                        rstd(b + 1, var1, r1, m["rs1"], m["c_pool1"], mv1[:, 1:2], LN_EPS, m["st1"])
                if q == 1:
                    if valid(b - 2):
                        rstd(b - 2, var2, r2, m["rs2"], m["c_pool2"], mv2[:, 1:2], LN_EPS, m["st2"])
                    if valid(b - 1):
                        need(pool, m["x2_ready"], b - 1)
                        pool.tensor_tensor(xb[:, :], x_res[:, b - 1, :], ln_shift[:, :], ALU.add)\
                            .then_inc(m["xb_ready"], 1)
                    if valid(b + 2):
                        grp = g + (k + 2) // 4
                        kk = (k + 2) % 4
                        need(pool, m["cThi_ready"], b + 3)
                        need(pool, m["cTlo_ready"], b + 3)
                        need(pool, m["V_done"], 4 * (b + 1))
                        for to, of in ((ctxv_hi, ctxT_hi), (ctxv_lo, ctxT_lo)):
                            pool.tensor_copy(to[:, k % 2, :, :], of[:, grp % 2, :, kk * J:kk * J + J].bitcast(F32))\
                                .then_inc(m["cv_ready"], 1)
                if q == 2:
                    if valid(b - 2):
                        need(pool, m["stc"], b - 1)
                        step = chain(pool, m["c_poolc"], 3 * (b - 2))
                        step(pool.tensor_tensor(msc[:, 0:1], mvc[:, 0:1], mvc[:, 0:1], ALU.mult))
                        step(pool.tensor_tensor(msc[:, 1:2], msc[:, 0:1], mvc[:, 1:2], ALU.add), apart)
                        step(pool.tensor_scalar(msc[:, 0:1], msc[:, 1:2], LN_EPS, None, ALU.add))
                        pool.tensor_tensor(rc[:, :], msc[:, 0:1], half[0:J, :], ALU.pow).then_inc(m["rsc"], 1)
                    if valid(b - 3):
                        apart(pool, m["st3"], b - 2)
                        step = chain(pool, m["c_pool3"], 5 * (b - 3))
                        step(pool.tensor_scalar(var3[:, :], mv3[:, 1:2], LN_EPS, None, ALU.add))
                        step(pool.tensor_tensor(ratio3[:, 0:1], var3[:, :], half[:, :], ALU.pow))
                        step(pool.tensor_tensor(ratio3[:, 1:2], ratio3[:, 0:1], ratio3[:, 0:1], ALU.mult), apart)
                        step(pool.tensor_scalar(ratio3[:, 2:3], ratio3[:, 1:2], mv3[:, 1:2], LN_EPS, ALU.mult, ALU.add))
                        step(pool.tensor_tensor(var3[:, :], ratio3[:, 2:3], half[:, :], ALU.pow))
                        pool.tensor_tensor(r3[:, :], var3[:, :], ratio3[:, 0:1], ALU.mult).then_inc(m["rs3"], 1)
                if q == 3 and valid(b - 2):
                    apart(pool, m["z_ready"], b - 1)
                    need(pool, m["qT_done"], b - 2)
                    pool.tensor_scalar(q3[:, :], z3, -MAGIC, None, ALU.add).then_inc(m["q_ready"], 1)

            pool.wait_ge(ld["x0"], 16)
            pool.wait_ge(ld["x1"], 16)
            pool.wait_ge(shift_ready, 1)
            program(pool, slot)

        JOBS = 21
        A_JOBS = range(6, 14)
        TAP_JOBS = range(17, 20)

        def a_job(n):
            r = (n - 6) % 4
            return (n - 6) // 4, 8 * (r // 2) + r % 2

        def low_parts(n):
            return sum(j in A_JOBS or j in TAP_JOBS for j in range(n))

        @block.tensor
        def _(pe):
            for n in range(JOBS):
                b8 = bank[n % 8]
                need(pe, prep_act, n - 7)
                need(pe, prep_dve, low_parts(max(n - 7, 0)))
                if n < 2:
                    if n == 0:
                        pe.wait_ge(prep_pool, 17)
                        pe.wait_ge(ld["wq"], 16)
                    for i in range(4):
                        mm = pe.transpose(b8[:, 128 * i:128 * i + 128], wq[:, 128 * (4 * n + i):128 * (4 * n + i) + 128], ident[:, :])
                elif n < 6:
                    if n == 2:
                        pe.wait_ge(ld["wk"], 16)
                    for i in range(4):
                        h2_, c = 2 * (n - 2) + i // 2, i % 2
                        mm = pe.transpose(b8[:, 128 * i:128 * i + 128], wk[:, c, 128 * h2_:128 * h2_ + 128], ident[:, :])
                elif n < 14:
                    if n == 6:
                        pe.wait_ge(prep_act, 6)
                    c, h0 = a_job(n)
                    r = 64 * (h0 % 2)
                    for i in range(4):
                        h = h0 + 2 * i
                        mm = pe.matmul(b8[:, 128 * i:128 * i + 128], wkT[r:r + 64, h // 2, 128 * c:128 * c + 128],
                                       wqT[r:r + 64, h // 2, :], start=True, stop=True)
                elif n == 14:
                    pe.wait_ge(ld["small"], 16 * SMALL)
                    for i in range(H // 2):
                        mm = pe.matmul(b8[:, 2 * i:2 * i + 2], wqT[:, i, :], nullk[:, :], start=True, stop=True)
                elif n == 15:
                    pe.wait_ge(wsum_ready, 2)
                    mm = pe.matmul(b8[:, 0:2], ones[:, :], wsum[:, :], start=True, stop=True)
                elif n == 16:
                    mm = pe.transpose(b8[:, 0:128], w_in, ident[:, :])
                elif n < 20:
                    if n == 17:
                        pe.wait_ge(wtap_ready, 3 * FC)
                    for i in range(FC):
                        mm = pe.transpose(b8[:, 128 * i:128 * i + 128], wtap[:, i, n - 17, :], ident[:, :])
                else:
                    pe.wait_ge(w2t_ready, 1)
                    for i in range(FC):
                        mm = pe.transpose(b8[:, 64 * i:64 * i + 64].bitcast(BF16), w2t[:, 128 * i:128 * i + 128], ident_bf[:, :])
                mm.then_inc(prep_pe, 1)
            pe.wait_ge(prep_act, JOBS)
            pe.wait_ge(prep_dve, low_parts(JOBS))
            pe.wait_ge(ld["wout"], 16)
            pe.wait_ge(prep_split, 2)
            pe.wait_ge(main_ready, 1)
            pe.wait_ge(prep_pool, 17 + POWERS)

            def split3(o, w_hi, w_lo, x_hi, x_lo, first, last):
                pe.matmul(o, w_lo, x_hi, start=first, stop=False)
                pe.matmul(o, w_hi, x_lo, start=False, stop=False)
                return pe.matmul(o, w_hi, x_hi, start=False, stop=last)

            def slot(g, k, q, b, s):
                if valid(s - 2, 4 * B):
                    t = s - 2
                    bt, qt, kt = back(b, q, k, 2)
                    need(pe, m["pT_ready"], t + 1)
                    need(pe, m["V_ready"], t + 1)
                    need(pe, m["norm_ready"], t)
                    for i in range(QH):
                        mm = pe.matmul(AV[:, i * (DH + 1):(i + 1) * (DH + 1)], probsT[:, qt % 2, i, :],
                                       V[:, kt % 2, QH * qt + i, :], start=True, stop=True)
                    mm.then_inc(m["av_done"], 1)
                if valid(b):
                    need(pe, m["G_ready"], 16 * g + QH * (q + 1))
                    need(pe, m["hT_ready"], b + 1)
                    need(pe, m["sub_ready"], s)
                    pe.matmul(SC[:, 0:QH * JN], hT[:, k % 2, :],
                              G[:, g % 2, k, QH * q:QH * q + QH, :].rearrange("p h j -> p (h j)"),
                              start=True, stop=True).then_inc(m["s_done"], 1)
                if valid(b + 1):
                    need(pe, m["cv_ready"], 2 * (b + 2))
                    need(pe, m["V_ready"], s + 4)
                    need(pe, m["oT_ready"], s - 3)
                    for c in range(CC):
                        mm = split3(VO[0:J, 0:QH * DH], ctxv_hi[:, (k + 1) % 2, c, :], ctxv_lo[:, (k + 1) % 2, c, :],
                                    wv_hi[:, c, QH * DH * q:QH * DH * (q + 1)], wv_lo[:, c, QH * DH * q:QH * DH * (q + 1)],
                                    c == 0, c == CC - 1)
                    mm.then_inc(m["V_done"], 1)
                if q == 0 and valid(b - 3):
                    need(pe, m["q_ready"], b - 2)
                    need(pe, m["dep_ready"], b - 2)
                    for i in range(FC):
                        mm = pe.transpose(T1[:, 64 * i:64 * i + 64].bitcast(BF16), q3[:, 128 * i:128 * i + 128], ident_bf[:, :])
                    mm.then_inc(m["qT_done"], 1)
                if q == 1 and valid(b - 3):
                    need(pe, m["qT_ready"], b - 2)
                    for i in range(FC):
                        mm = pe.matmul(T1[:, 0:D], q3T[:, i, :], w2q[:, i, :], start=(i == 0), stop=(i == FC - 1))
                    mm.then_inc(m["w2_done"], 1)
                if q == 2 and valid(b - 2):
                    need(pe, m["xq_ready"], b - 1)
                    need(pe, m["x3_ready"], b - 2)
                    pe.transpose(T1[:, 0:S], xq[:, :], ident[:, :]).then_inc(m["xT_done"], 1)
                if q == 3:
                    if valid(b - 3):
                        need(pe, m["T3_ready"], b - 2)
                        need(pe, m["pick_ready"], b - 2)
                        need(pe, m["dep_ready"], b - 2)
                        pe.matmul(T2[:, 0:D], h3T[:, :], w_inT[:, :], start=True, stop=False)
                        pe.matmul(T2[:, 0:D], pick[:, :], dep[:, :], start=False, stop=True).then_inc(m["L1_done"], 1)
                    if valid(b - 2):
                        need(pe, m["hp_ready"], b - 1)
                        need(pe, m["conv_ready"], b - 1)
                        pe.matmul(T1[0:J, 0:D], scanT[:, :], hp[:, :], start=True, stop=True).then_inc(m["dep_done"], 1)
                if valid(s - 1, 4 * B):
                    t = s - 1
                    bt, qt, kt = back(b, q, k, 1)
                    need(pe, m["exp_ready"], t + 1)
                    need(pe, m["pT_ready"], t)
                    for i in range(QH):
                        mm = pe.transpose(PT[0:JN, 128 * i:128 * i + 128], probs[:, qt % 2, i, :], ident[:, :])
                    mm.then_inc(m["pT_done"], 1)
                if valid(g + 1, NG):
                    h = 4 * k + q
                    n = 16 * (g + 1) + h
                    need(pe, m["G_ready"], n)
                    need(pe, m["cThi_ready"], 4 * (g + 2))
                    need(pe, m["cTlo_ready"], 4 * (g + 2))
                    for c in range(CC):
                        mm = split3(GC[:, 0:GB * J], A_hi[:, c, h, :], A_lo[:, c, h, :],
                                    ctxT_hi[:, (g + 1) % 2, c, :], ctxT_lo[:, (g + 1) % 2, c, :], c == 0, c == CC - 1)
                    mm.then_inc(m["G_done"], 1)
                if q == 0 and valid(b - 4):
                    need(pe, m["xs_ready"], b - 3)
                    need(pe, m["x4_ready"], b - 3)
                    pe.transpose(T2[:, 0:S], xs[:, :], ident[:, :]).then_inc(m["T4_done"], 1)
                if q == 1:
                    if valid(b - 4):
                        need(pe, m["xsT_ready"], b - 3)
                        pe.matmul(T2[:, 0:E], xsT[:, :], w_gate[:, :], start=True, stop=True).then_inc(m["gate_done"], 1)
                    if not isinstance(b, int) or 0 <= b + 8 < CT_LAST:
                        need(pe, ld_rows[k % 2], 16 * (2 * g + (k + 8) // 2 + 1))
                        need(pe, m["y_taken"], b - 1)
                        need(pe, m["hT_ready"], b + 1)
                        need(pe, m["cThi_ready"], b + 8)
                        need(pe, m["cTlo_ready"], b + 8)
                        for c in range(CC):
                            mm = pe.transpose(YH[:, J * c:J * c + J], rows[:, k % 2, 128 * c:128 * c + 128], ident[0:J, 0:J])
                        mm.then_inc(m["cT_done"], 1)
                if q == 2:
                    if valid(b - 2):
                        need(pe, m["xThi_ready"], b - 1)
                        need(pe, m["xTlo_ready"], b - 1)
                        for i in range(3):
                            mm = split3(T1[:, :], xqT_hi[:, i:i + S], xqT_lo[:, i:i + S], tap_hi[:, i, :], tap_lo[:, i, :],
                                        i == 0, i == 2)
                        mm.then_inc(m["conv_done"], 1)
                    if valid(b + 1):
                        need(pe, m["h1_ready"], b + 2)
                        need(pe, m["cThi_ready"], upto(b + 9, CT_LAST))
                        need(pe, m["cTlo_ready"], upto(b + 9, CT_LAST))
                        need(pe, m["y_taken"], b - 1)
                        pe.transpose(YH[:, 0:S], h1[:, :], ident[:, :]).then_inc(m["hT_done"], 1)
                    if valid(b - 3):
                        need(pe, m["h3_ready"], b - 2)
                        need(pe, m["gate_taken"], b - 3)
                        pe.transpose(T2[:, 0:S], h3[:, :], ident[:, :]).then_inc(m["T3_done"], 1)
                if q == 3 and valid(b - 1):
                    need(pe, m["oT_ready"], 4 * b)
                    need(pe, m["hT_ready"], upto(b + 2, B))
                    need(pe, m["y_taken"], b - 1)
                    for i in range(INNER // 128):
                        mm = pe.matmul(YH[:, 0:D], attnT[:, (k + 1) % 2, i, :], w_out[:, i, :],
                                       start=(i == 0), stop=(i == INNER // 128 - 1))
                    mm.then_inc(m["y_done"], 1)
                if valid(s - 3, 4 * B):
                    t = s - 3
                    bt, qt, kt = back(b, q, k, 3)
                    need(pe, m["norm_ready"], t + 1)
                    need(pe, m["oT_ready"], t)
                    need(pe, m["V_ready"], upto(s + 5, 4 * B))
                    for i in range(2):
                        mm = pe.transpose(VO[:, 256 + 128 * i:384 + 128 * i], attn[:, qt % 2, 128 * i:128 * i + 128], ident[:, :])
                    mm.then_inc(m["oT_done"], 1)

            program(pe, slot)

            pe.wait_ge(ld["moe"], 48)
            pe.wait_ge(m["gate_taken"], B)

            def second(t, e):
                n = E * t + e
                need(pe, m["hid_ready"], FFC * (n + 1))
                if e >= 2:
                    pe.wait_ge(m["moe_taken"], n - 1)
                for i in range(4):
                    for c in range(FFC):
                        mm = pe.matmul(bank[4 + e % 2][:, 128 * i:128 * i + 128], hid[e % 2][:, c, 128 * i:128 * i + 128],
                                       eW2[:, e, c, :], start=(c == 0), stop=(c == FFC - 1))
                mm.then_inc(m["o_done"], 1)

            with pe.Fori(0, NG // 2) as u:
                for i2 in range(2):
                    t = 2 * u + i2
                    pe.wait_ge(m[f"xsT_in{i2}"], 16 * (u + 1))
                    for e in range(E):
                        for c in range(FFC):
                            if e:
                                pe.wait_ge(m["hid_ready"], FFC * (E * t + e) + c - 3)
                            pe.matmul(bank[c][:, :], eW1[:, e, 128 * c:128 * c + 128],
                                      xsT_in[:, i2, :, :].rearrange("p b s -> p (b s)"), start=True, stop=True)\
                                .then_inc(m["h_done"], 1)
                        if e:
                            second(t, e - 1)
                    second(t, E - 1)
                    pe.wait_ge(m["moe_taken"], E * (t + 1))

        @block.scalar
        def _(act):
            for i in range(LEN_LOADS):
                act.dma_start(len_i[B * i:B * i + B, :], a["mask_BxS2_if0"]).then_inc(ld["len"], 16)
            n = NULL_LOADS
            for dst, src in (
                (w1, a["L0_ffn_w1"].rearrange("(c p) d -> p c d", p=128)),
                (w2, a["L0_ffn_w2"]),
                (gates[:, 0:2], a["g_xattn"].partition_broadcast(128)),
                (gates[:, 2:4], a["g_ffn"].partition_broadcast(128)),
                (w_in, a["L1_xattn_W_in"]),
                (w_gate[:, :], a["L1_ffn_Wg"]),
                (tap_gain[:, :, :], a["L0_ffn_conv_w"].rearrange("(c p) o t -> p c (o t)", p=128)),
                (conv_b[:, :], a["L0_ffn_conv_b"].partition_broadcast(128)),
                (ln_gain[:, :], a["L0_xattn_ln_scale"].partition_broadcast(128)),
                (ln_shift[:, :], a["L0_xattn_ln_bias"].partition_broadcast(128)),
                (b_in[:, :], a["L1_xattn_b_in"].partition_broadcast(J)),
                (g_init[:, :], a["L1_xattn_g_init"][0:D].partition_broadcast(J)),
                (g_res[:, :], a["L1_xattn_g_res"].rearrange("(p o) -> p o", o=1)),
            ):
                act.dma_start(dst, src).then_inc(ld["small"], 16)
                n += 1
            assert n == SMALL
            act.dma_start(b1c[:, :, :], a["L1_ffn_b1"].rearrange("e (c p) -> p e c", p=128), allow_slow_non_contiguous=True).then_inc(m["g_in"], 16)
            act.wait_ge(ld["small"], 16 * SMALL)
            act.activation(gates[:, :], gates[:, :], ACT.Tanh).then_inc(gates_ready, 1)
            for n in range(JOBS):
                b8 = bank[n % 8]
                act.wait_ge(prep_pe, n + 1)
                if n < 2:
                    ins = act.activation(wqT[:, 4 * n:4 * n + 4, :].rearrange("p h d -> p (h d)"), b8[:, :], ACT.Copy, scale=SCALE)
                elif n < 6:
                    ins = act.activation(wkT[:, 2 * (n - 2):2 * (n - 2) + 2, :].rearrange("p h c -> p (h c)"), b8[:, :], ACT.Copy)
                elif n < 14:
                    c, h0 = a_job(n)
                    ins = act.activation(A_hi[:, c, h0:h0 + 7:2, :], b8[:, :].rearrange("p (h d) -> p h d", h=4), ACT.Copy)
                elif n == 14:
                    ins = act.activation(gnull[:, :], b8[:, 0:H], ACT.Copy)
                elif n == 15:
                    ins = act.activation(wmean[:, :], b8[:, 0:2], ACT.Copy, scale=1.0 / (F * D))
                elif n == 16:
                    ins = act.activation(w_inT[:, :], b8[:, 0:128], ACT.Copy, scale=g_res[:, :])
                elif n < 20:
                    ins = act.activation(tap_hi[:, n - 17, :], b8[:, :], ACT.Copy)
                else:
                    ins = act.activation(w2q[:, :, :].rearrange("p c d -> p (c d)"), b8[:, 0:256].bitcast(BF16), ACT.Copy)
                ins.then_inc(prep_act, 1)
                if n == 13:
                    act.wait_ge(ld["wv"], 16)
                    act.activation(wv_hi[:, :, :], wv, ACT.Copy).then_inc(prep_split, 1)
            act.wait_ge(main_ready, 1)

            def slot(g, k, q, b, s):
                if valid(s - 4, 4 * B):
                    t = s - 4
                    bt, qt, kt = back(b, q, k, 4)
                    need(act, m["oT_done"], t + 1)
                    need(act, m["y_done"], bt - 1)
                    act.activation(attnT[:, kt % 2, 2 * qt:2 * qt + 2, :].rearrange("p c s -> p (c s)"), VO[:, 256:512], ACT.Copy)\
                        .then_inc(m["oT_ready"], 1)
                if valid(b + 1):
                    need(act, m["V_done"], s + 5)
                    need(act, m["av_done"], s - 3)
                    act.activation(V[0:J, (k + 1) % 2, QH * q:QH * q + QH, 0:DH],
                                   VO[0:J, 0:QH * DH].rearrange("p (h d) -> p h d", h=QH), ACT.Copy).then_inc(m["V_ready"], 1)
                if q == 2 and valid(b - 2):
                    need(act, m["xT_done"], b - 1)
                    need(act, m["conv_done"], b - 2)
                    act.activation(xqT_hi[:, 1:S + 1], T1[:, 0:S], ACT.Copy).then_inc(m["xThi_ready"], 1)
                if q == 1 and valid(b - 4):
                    need(act, m["T4_done"], b - 3)
                    need(act, m["gate_done"], b - 4)
                    need(act, m["xsT_stored"], 16 * (b - 4))
                    act.activation(xsT[:, :], T2[:, 0:S], ACT.Copy).then_inc(m["xsT_ready"], 1)
                if valid(b):
                    need(act, m["sub_ready"], s + 1)
                    need(act, m["pT_done"], s - 1)
                    act.activation(probs[:, q % 2, :, :], shifted[:, q % 2, :, :], ACT.Exp).then_inc(m["exp_ready"], 1)
                if q == 0 and valid(b - 3):
                    need(act, m["qT_done"], b - 2)
                    need(act, m["w2_done"], b - 3)
                    act.activation(q3T[:, :, :].rearrange("p c s -> p (c s)"), T1[:, 0:256].bitcast(BF16), ACT.Copy)\
                        .then_inc(m["qT_ready"], 1)
                if q == 3 and valid(b - 2):
                    need(act, m["conv_ready"], b - 1)
                    need(act, m["c_conv"], 5 * (b - 2))
                    act.activation(tanh_c, conv, ACT.Tanh, scale=0.5).then_inc(m["tanh_ready"], 1)
                if valid(s - 1, 4 * B):
                    t = s - 1
                    bt, qt, kt = back(b, q, k, 1)
                    need(act, m["pT_done"], t + 1)
                    need(act, m["av_done"], t - 1)
                    act.activation(probsT[:, qt % 2, :, :].rearrange("p h s -> p (h s)"), PT[0:JN, :], ACT.Copy)\
                        .then_inc(m["pT_ready"], 1)
                if valid(g + 1, NG):
                    h = 4 * k + q
                    n = 16 * (g + 1) + h
                    need(act, m["G_done"], n + 1)
                    need(act, m["s_done"], 16 * g)
                    act.activation(G[:, (g + 1) % 2, :, h, 0:J], GC[:, 0:GB * J].rearrange("p (b j) -> p b j", b=GB), ACT.Copy)\
                        .then_inc(m["G_ready"], 1)
                if q == 1 and (not isinstance(b, int) or 0 <= b + 8 < CT_LAST):
                    need(act, m["cT_done"], b + 9)
                    need(act, m["G_done"], 16 * (g + 1))
                    need(act, m["cv_ready"], upto(2 * (b + 1), 2 * B))
                    act.activation(ctxT_hi[:, g % 2, :, k * J:k * J + J], YH[:, 0:CC * J].rearrange("p (c j) -> p c j", c=CC), ACT.Copy)\
                        .then_inc(m["cThi_ready"], 1)
                if q == 2:
                    if valid(b + 1):
                        need(act, m["hT_done"], b + 2)
                        need(act, m["s_done"], 4 * b)
                        act.activation(hT[:, (k + 1) % 2, :], YH[:, 0:S], ACT.Copy).then_inc(m["hT_ready"], 1)
                    if valid(b - 3):
                        need(act, m["T3_done"], b - 2)
                        need(act, m["L1_done"], b - 3)
                        act.activation(h3T[:, :], T2[:, 0:S], ACT.Copy).then_inc(m["T3_ready"], 1)

            program(act, slot)
            act.wait_ge(m["c_moe"], 1)
            act.activation(gp[:, 1, :], gp[:, 0, :], ACT.Exp).then_inc(m["g_exp"], 1)
            act.wait_ge(m["g_in"], 16)
            with act.Fori(0, B // 4) as t:
                for e in range(E):
                    for c in range(FFC):
                        n = FFC * (E * t + e) + c
                        act.wait_ge(m["h_done"], n + 1)
                        if e >= 2:
                            act.wait_ge(m["o_done"], E * t + e - 1)
                        act.activation(hid[e % 2][:, c, :], bank[c][:, :], ACT.Relu, bias=b1c[:, e, c:c + 1])\
                            .then_inc(m["hid_ready"], 1)
                act.wait_ge(m["o_done"], E * (t + 1))

        @block.vector
        def _(dve):
            step = chain(dve, prep_chain, 0)
            dve.wait_ge(ld["len"], 16 * LEN_LOADS)
            dve.wait_ge(prep_pool, 16)
            step(dve.tensor_scalar(len_f[:, :], len_i[:, :], PATCH_CLIP, -PATCH_CLIP, ALU.min, ALU.max))
            step(dve.tensor_tensor_scan(len_sum[:, :], len_f[:, :], zero_row[:, 0:J], 0.0, ALU.add, ALU.add))
            step(dve.tensor_scalar(len_f[:, :], len_sum[:, :], -1.0, None, ALU.add))
            step(dve.tensor_scalar(len_wrap[:, :], len_f[:, :], 0.0, float(S), ALU.is_lt, ALU.mult))
            step(dve.tensor_tensor(len_sum[:, :], len_f[:, :], len_wrap[:, :], ALU.add))
            step(dve.tensor_tensor(eq, len_sum[:, :].unsqueeze(1).broadcast_to([128, 32, J]),
                                   token_no[:, :].unsqueeze(2).broadcast_to([128, 32, J]), ALU.is_equal))
            dve.tensor_reduce(edge[:, :], eq, AX.X, ALU.max).then_inc(edge_ready, 1)
            dve.wait_ge(ld["small"], 16 * SMALL)
            dve.tensor_reduce(wsum[:, 0:1], w1, AX.XY, ALU.add, apply_absolute_value=True).then_inc(wsum_ready, 1)
            dve.tensor_reduce(wsum[:, 1:2], w2, AX.X, ALU.add, apply_absolute_value=True).then_inc(wsum_ready, 1)
            for n in A_JOBS:
                c, h0 = a_job(n)
                dve.wait_ge(prep_act, n + 1)
                dve.tensor_tensor(A_lo[:, c, h0:h0 + 7:2, :], bank[n % 8][:, :].rearrange("p (h d) -> p h d", h=4),
                                  A_hi[:, c, h0:h0 + 7:2, :].bitcast(F32), ALU.subtract).then_inc(prep_dve, 1)
            dve.wait_ge(ld["row"], 16)
            step(dve.tensor_tensor_scan(edge_sum[:, :], edges[:, :], zero_row[0:B, :], 0.0, ALU.add, ALU.add))
            dve.tensor_scalar(plug[:, :], edge_sum[:, :], 1.0, None, ALU.max).then_inc(plug_ready, 1)
            dve.wait_ge(prep_act, 16)
            dve.wait_ge(gates_ready, 1)
            step(dve.tensor_scalar(wsum[:, :], wmean[:, :], QUANT_FLOOR, None, ALU.max))
            step(dve.reciprocal(winv[:, :], wsum[:, :]))
            step(dve.tensor_scalar(w1, w1, winv[:, 0:1], -1.0, ALU.mult, ALU.max))
            step(dve.tensor_scalar(w1, w1, 1.0, MAGIC, ALU.min, ALU.add))
            step(dve.tensor_scalar(w1, w1, -MAGIC, wsum[:, 0:1], ALU.add, ALU.mult))
            for c in range(FC):
                for t in range(3):
                    dve.tensor_scalar(wtap[:, c, t, :], w1[:, c, :], tap_gain[:, c, t:t + 1], None, ALU.mult).then_inc(wtap_ready, 1)
            step(dve.tensor_scalar(w2, w2, winv[:, 1:2], -1.0, ALU.mult, ALU.max))
            step(dve.tensor_scalar(w2, w2, 1.0, MAGIC, ALU.min, ALU.add))
            dve.tensor_scalar(w2t, w2, -MAGIC, None, ALU.add).then_inc(w2t_ready, 1)
            step(dve.tensor_scalar(w2_gain[:, :], wsum[:, 1:2], gates[:, 2:3], 0.5, ALU.mult, ALU.mult))
            step(dve.tensor_scalar(ln_gain[:, :], ln_gain[:, :], gates[:, 0:1], None, ALU.mult))
            dve.tensor_scalar(ln_shift[:, :], ln_shift[:, :], gates[:, 0:1], None, ALU.mult).then_inc(shift_ready, 1)
            dve.wait_ge(prep_split, 1)
            dve.tensor_tensor(wv_lo[:, :, :], wv, wv_hi[:, :, :].bitcast(F32), ALU.subtract).then_inc(prep_split, 1)
            for n in TAP_JOBS:
                dve.wait_ge(prep_act, n + 1)
                dve.tensor_tensor(tap_lo[:, n - 17, :], bank[n % 8][:, :], tap_hi[:, n - 17, :].bitcast(F32), ALU.subtract)\
                    .then_inc(prep_dve, 1)
            dve.wait_ge(prep_act, JOBS)
            for i in range(2):
                ins = dve.tensor_copy(G[:, i, :, :, J], gnull[:, :].unsqueeze(1).broadcast_to([128, GB, H]))
            ins.then_inc(main_ready, 1)
            dve.wait_ge(ld["x0"], 16)
            dve.wait_ge(ld["x1"], 16)
            dve.wait_ge(ld["plug"], 16)
            dve.wait_ge(prep_pool, 17)

            def stats(b, src, raw, mv, ready, written=None):
                if written:
                    apart(dve, written, b + 1)
                dve.bn_stats(raw[:, :], src).then_inc(ready[0], 1)
                apart(dve, ready[0], b + 1)
                dve.bn_aggr(mv[:, :], raw[:, :]).then_inc(ready[1], 1)

            def norm_by(dst, src, mv, root):
                return dve.tensor_scalar(dst, src, mv[:, 0:1], root[:, 0:1], ALU.subtract, ALU.mult)

            def slot(g, k, q, b, s):
                if q == 0 and valid(b - 2):
                    stats(b - 2, YH[:, 0:D], rawy, mvy, (raw_sem[0], m["sty"]), m["y_done"])
                if q == 3 and valid(b - 2):
                    need(dve, m["conv_done"], b - 1)
                    dve.tensor_tensor(conv, T1[:, :], conv_b[:, :], ALU.add).then_inc(m["conv_ready"], 1)
                if valid(s - 2, 4 * B):
                    t = s - 2
                    bt, qt, kt = back(b, q, k, 2)
                    need(dve, m["av_done"], t + 1)
                    need(dve, m["oT_done"], t - 1)
                    av = AV[:, 0:QH * (DH + 1)].rearrange("p (h d) -> p h d", h=QH)
                    dve.reciprocal(rden[:, qt % 2, :], av[:, :, DH]).then_inc(m["c_norm"], 1)
                    dve.wait_ge(m["c_norm"], t + 1)
                    dve.tensor_tensor(attn[:, qt % 2, :].rearrange("p (h d) -> p h d", h=QH), av[:, :, 0:DH],
                                      rden[:, qt % 2, :].unsqueeze(2).broadcast_to([128, QH, DH]), ALU.mult)\
                        .then_inc(m["norm_ready"], 1)
                if valid(b):
                    sc = SC[:, 0:QH * JN].rearrange("p (h j) -> p h j", h=QH)
                    need(dve, m["s_done"], s + 1)
                    need(dve, m["exp_ready"], s - 1)
                    dve.tensor_reduce(top[:, q % 2, :], sc, AX.X, ALU.max).then_inc(m["c_soft"], 1)
                    dve.wait_ge(m["c_soft"], s + 1)
                    dve.tensor_tensor(shifted[:, q % 2, :, :], sc, top[:, q % 2, :].unsqueeze(2).broadcast_to([128, QH, JN]),
                                      ALU.subtract).then_inc(m["sub_ready"], 1)
                if q == 0:
                    if valid(b + 1):
                        stats(b + 1, x_res[:, b + 1, :], raw1, mv1, (raw_sem[1], m["st1"]))
                    if valid(b - 4):
                        need(dve, m["rs4"], b - 3)
                        need(dve, m["T4_done"], b - 4)
                        norm_by(xs[:, :], x_res[:, b - 4, :], mv4, r4).then_inc(m["xs_ready"], 1)
                    if valid(b - 2):
                        need(dve, m["rsy"], b - 1)
                        need(dve, m["xb_ready"], b - 1)
                        norm_by(y1[:, :], YH[:, 0:D], mvy, ry).then_inc(m["y_taken"], 1)
                        dve.wait_ge(m["y_taken"], b - 1)
                        dve.tensor_tensor(y2[:, :], y1[:, :], ln_gain[:, :], ALU.mult).then_inc(m["c_y"], 1)
                        dve.wait_ge(m["c_y"], b - 1)
                        dve.tensor_tensor(x_res[:, b - 2, :], y2[:, :], xb[:, :], ALU.add).then_inc(m["x2_ready"], 1)
                        stats(b - 2, x_res[:, b - 2, :], raw2, mv2, (raw_sem[2], m["st2"]), m["x2_ready"])
                if q == 1:
                    if valid(b + 1):
                        need(dve, m["rs1"], b + 2)
                        need(dve, m["hT_done"], b + 1)
                        norm_by(h1[:, :], x_res[:, b + 1, :], mv1, r1).then_inc(m["h1_ready"], 1)
                    if valid(b - 3):
                        need(dve, m["w2_done"], b - 2)
                        need(dve, m["c_conv"], 5 * (b - 2))
                        dve.scalar_tensor_tensor(x_res[:, b - 3, :], T1[:, 0:D], back3[:, (k + 1) % 2:(k + 1) % 2 + 1],
                                                 x_res[:, b - 3, :], ALU.mult, ALU.add).then_inc(m["x3_ready"], 1)
                        stats(b - 3, x_res[:, b - 3, :], raw3, mv3, (raw_sem[3], m["st3"]), m["x3_ready"])
                    if valid(b - 2):
                        apart(dve, ld_patch[k % 2], 16 * (2 * g + (k - 2) // 2 + 1))
                        dve.bn_stats(rawc[:, :], patch[:, k % 2, :]).then_inc(raw_sem[5], 1)
                        apart(dve, raw_sem[5], b - 1)
                        dve.bn_aggr(mvc[:, :], rawc[:, :]).then_inc(m["stc"], 1)
                        need(dve, m["rs2"], b - 1)
                        need(dve, m["xT_done"], b - 2)
                        step = chain(dve, m["c_h2"], 5 * (b - 2))
                        step(norm_by(h2[:, :], x_res[:, b - 2, :], mv2, r2))
                        step(dve.tensor_reduce(qs2[:, 0:1], h2[:, :], AX.X, ALU.max, apply_absolute_value=True))
                        step(dve.tensor_scalar(qs2[:, 1:2], qs2[:, 0:1], QUANT_FLOOR, 1.0 / 127.0, ALU.max, ALU.mult))
                        step(dve.reciprocal(qs2[:, 2:3], qs2[:, 1:2]))
                        step(dve.tensor_scalar(z2[:, :], h2[:, :], qs2[:, 2:3], MAGIC, ALU.mult, ALU.add))
                        dve.tensor_scalar(xq[:, :], z2[:, :], -MAGIC, qs2[:, 1:2], ALU.add, ALU.mult).then_inc(m["xq_ready"], 1)
                    if not isinstance(b, int) or 0 <= b + 8 < CT_LAST:
                        need(dve, m["cThi_ready"], b + 9)
                        dve.tensor_tensor(ctxT_lo[:, g % 2, :, k * J:k * J + J], YH[:, 0:CC * J].rearrange("p (c j) -> p c j", c=CC),
                                          ctxT_hi[:, g % 2, :, k * J:k * J + J].bitcast(F32), ALU.subtract).then_inc(m["cTlo_ready"], 1)
                if q == 2:
                    if valid(b - 2):
                        need(dve, m["xThi_ready"], b - 1)
                        dve.tensor_tensor(xqT_lo[:, 1:S + 1], T1[:, 0:S], xqT_hi[:, 1:S + 1].bitcast(F32), ALU.subtract)\
                            .then_inc(m["xTlo_ready"], 1)
                    if valid(b - 4):
                        apart(dve, m["gate_done"], b - 3)
                        dve.max(best[:, :], T2[:, 0:E]).then_inc(m["c_gate"], 1)
                        apart(dve, m["c_gate"], 3 * (b - 4) + 1)
                        dve.max_index(best_at[:, :], best[:, :], T2[:, 0:E]).then_inc(m["gate_taken"], 1)
                        dve.tensor_copy(best_all[:, b - 4, :], best[:, 0:2]).then_inc(m["c_gate"], 1)
                        dve.wait_ge(m["gate_taken"], b - 3)
                        dve.tensor_copy(at_all[:, b - 4, :], best_at[:, 0:2]).then_inc(m["c_gate"], 1)
                        dve.wait_ge(m["c_gate"], 3 * (b - 4) + 3)
                    if valid(b - 3):
                        need(dve, m["rs3"], b - 2)
                        need(dve, m["T3_done"], b - 3)
                        norm_by(h3[:, :], x_res[:, b - 3, :], mv3, r3).then_inc(m["h3_ready"], 1)
                        need(dve, m["L1_done"], b - 3)
                        dve.tensor_scalar(pick[:, :], plug_rows[:, b - 3, :], patch_no[:, :], None, ALU.is_equal)\
                            .then_inc(m["pick_ready"], 1)
                    if valid(b - 2):
                        need(dve, m["rsc"], b - 1)
                        need(dve, m["dep_done"], b - 2)
                        dve.scalar_tensor_tensor(hp[:, :], patch[:, k % 2, 0:D], rc[:, 0:1], g_init[:, :], ALU.mult, ALU.mult)\
                            .then_inc(m["hp_ready"], 1)
                if q == 3:
                    if valid(b - 3):
                        need(dve, m["L1_done"], b - 2)
                        dve.scalar_tensor_tensor(x_res[:, b - 3, :], T2[:, 0:D], gates[:, 1:2], x_res[:, b - 3, :],
                                                 ALU.mult, ALU.add).then_inc(m["x4_ready"], 1)
                        stats(b - 3, x_res[:, b - 3, :], raw4, mv4, (raw_sem[4], m["st4"]), m["x4_ready"])
                    if valid(b - 2):
                        need(dve, m["dep_done"], b - 1)
                        need(dve, m["L1_done"], b - 2)
                        dve.tensor_tensor(dep[:, :], T1[0:J, 0:D], b_in[:, :], ALU.add).then_inc(m["dep_ready"], 1)
                        need(dve, m["tanh_ready"], b - 1)
                        need(dve, m["q_ready"], b - 2)
                        step = chain(dve, m["c_conv"], 5 * (b - 2))
                        step(dve.scalar_tensor_tensor(act2, tanh_c, 1.0, conv, ALU.add, ALU.mult))
                        step(dve.tensor_reduce(qs3[:, 0:1], act2, AX.X, ALU.max, apply_absolute_value=True))
                        step(dve.tensor_scalar(qs3[:, 1:2], qs3[:, 0:1], 2 * QUANT_FLOOR, 1.0 / 127.0, ALU.max, ALU.mult))
                        step(dve.reciprocal(qs3[:, 2:3], qs3[:, 1:2]))
                        dve.tensor_scalar(z3, act2, qs3[:, 2:3], MAGIC, ALU.mult, ALU.add).then_inc(m["z_ready"], 1)
                        dve.tensor_scalar(back3[:, k % 2:k % 2 + 1], qs3[:, 1:2], w2_gain[:, :], None, ALU.mult)\
                            .then_inc(m["c_conv"], 1)

            program(dve, slot)

            dve.tensor_tensor(gp[:, 0, :], best_all[:, :, 1], best_all[:, :, 0], ALU.subtract).then_inc(m["c_moe"], 1)
            dve.wait_ge(m["g_exp"], 1)
            step = chain(dve, m["c_moe"], 1)
            step(dve.tensor_scalar(gp[:, 2, :], gp[:, 1, :], 1.0, None, ALU.add))
            step(dve.reciprocal(gp[:, 3, :], gp[:, 2, :]))
            step(dve.tensor_scalar(gp[:, 3, :], gp[:, 3, :], gates[:, 3:4], None, ALU.mult))
            step(dve.tensor_tensor(gp[:, 4, :], gp[:, 1, :], gp[:, 3, :], ALU.mult))
            for i in range(2):
                step(dve.tensor_tensor(gw[:, i, :, :], expert_no[:, :].unsqueeze(1).broadcast_to([128, B, E]),
                                       at_all[:, :, i].unsqueeze(2).broadcast_to([128, B, E]), ALU.is_equal))
                step(dve.tensor_tensor(gw[:, i, :, :], gw[:, i, :, :],
                                       gp[:, 3 + i, :].unsqueeze(2).broadcast_to([128, B, E]), ALU.mult))
            step(dve.tensor_tensor(gw[:, 2, :, :], gw[:, 0, :, :], gw[:, 1, :, :], ALU.add))
            dve.wait_ge(ld["moe"], 48)
            dve.wait_ge(m["y_done"], B)
            with dve.Fori(0, B // 4) as t:
                for e in range(E):
                    n = E * t + e
                    dve.wait_ge(m["o_done"], n + 1)
                    dve.tensor_tensor(moe[:, e % 2, :, :], bank[4 + e % 2][:, :].rearrange("p (t d) -> p t d", t=4),
                                      b2r[:, e, :].unsqueeze(1).broadcast_to([128, 4, D]), ALU.add).then_inc(m["moe_taken"], 1)
                    dve.wait_ge(m["moe_taken"], n + 1)
                    for i in range(4):
                        dve.scalar_tensor_tensor(x_res[:, 4 * t + i, :], moe[:, e % 2, i, :], gw[:, 2, 4 * t + i, e:e + 1],
                                                 x_res[:, 4 * t + i, :], ALU.mult, ALU.add).then_inc(m["moe_sum"], 1)
                    dve.wait_ge(m["moe_sum"], 4 * (n + 1))


_INS = ["x", "ctx_2048", "mask_BxS2_if0", "g_xattn", "g_ffn", "L0_xattn_Wq", "L0_xattn_Wkv", "L0_xattn_null_kv",
        "L0_xattn_Wout", "L0_xattn_ln_scale", "L0_xattn_ln_bias", "L0_ffn_w1", "L0_ffn_conv_w", "L0_ffn_conv_b",
        "L0_ffn_w2", "L1_xattn_W_in", "L1_xattn_b_in", "L1_xattn_g_res", "L1_xattn_g_init", "L1_ffn_Wg", "L1_ffn_W1",
        "L1_ffn_b1", "L1_ffn_W2", "L1_ffn_b2"]


def kernel(**inputs):
    import concourse.bacc as bacc
    from concourse.bass_utils import run_bass_kernel_spmd

    nc = bacc.Bacc("TRN2", target_bir_lowering=False, num_devices=1)
    arrays, handles = {}, {}
    for name in _INS:
        arr = np.ascontiguousarray(inputs[name])
        arrays[name] = arr
        handles[name] = nc.dram_tensor(name, arr.shape, mybir.dt.from_np(arr.dtype), kind="ExternalInput").ap()
    out = nc.dram_tensor("out", arrays["x"].shape, F32, kind="ExternalOutput").ap()
    build(nc, handles, out)
    r = run_bass_kernel_spmd(nc, [arrays], core_ids=[0])
    return r.results[0]["out"]
```

```python
from contextlib import ExitStack

import numpy as np

import concourse.bass as bass
from concourse import mybir

F32 = mybir.dt.float32
F32R = mybir.dt.float32r
BF16 = mybir.dt.bfloat16
I32 = mybir.dt.int32
U32 = mybir.dt.uint32
ALU = mybir.AluOpType
ACT = mybir.ActivationFunctionType
AX = mybir.AxisListType

MAGIC = 1.5 * 2.0**23
LN_EPS = 1e-5
XATTN_EPS = 1e-6
QUANT_FLOOR = 1e-5
PATCH_CLIP = 65536.0


def need(eng, sem, count):
    if isinstance(count, int) and count <= 0:
        return
    eng.wait_ge(sem, count)


def chain(eng, sem, count):
    done = [0]

    def link(ins, wait=need):
        done[0] += 1
        ins.then_inc(sem, 1)
        wait(eng, sem, count + done[0])

    return link


def build(nc, a, out):
    B, S, D = a["x"].shape
    J, C = a["ctx_2048"].shape[1:]
    INNER = a["L0_xattn_Wq"].shape[1]
    DH = a["L0_xattn_null_kv"].shape[1]
    H = INNER // DH
    F = a["L0_ffn_w1"].shape[0]
    E = a["L1_ffn_Wg"].shape[1]
    FF = a["L1_ffn_W1"].shape[2]
    assert S == 128 and D == 128 and C == 256 and DH == 64 and B % 4 == 0
    GB = 4
    NG = B // GB
    QH = H // 4
    JN = J + 1
    CC = C // 128
    FC = F // 128
    FFC = FF // 128
    SCALE = DH**-0.5
    CAP = B * S + 128
    TILES = 2 * B * S // 128 + E
    POWERS = 12
    CT_LAST = 4 * (NG - 2) + 3 + 8 + 1

    logp = np.float32(-0.001)
    dt = np.float32(-np.log(-np.expm1(logp)))
    decay = float(np.exp(-dt))
    gain = float(np.exp(logp))

    ctx = ExitStack()
    with ctx:
        def sb(name, shape, dtype=F32):
            return ctx.enter_context(nc.sbuf_tensor(name, shape, dtype))

        def sem(name):
            return ctx.enter_context(nc.semaphore(name))

        x_res = sb("x_res", [128, B, D])
        G = sb("G", [128, 2, GB, H, JN])
        wv_lo = sb("wv_lo", [128, CC, INNER], F32R)
        ctxT_hi = sb("ctxT_hi", [128, 2, CC, GB * J], F32R)
        ctxT_lo = sb("ctxT_lo", [128, 2, CC, GB * J], F32R)
        ctxv_hi = sb("ctxv_hi", [128, 2, CC, J], F32R)
        ctxv_lo = sb("ctxv_lo", [128, 2, CC, J], F32R)
        tap_hi = sb("tap_hi", [128, 3, F], F32R)
        tap_lo = sb("tap_lo", [128, 3, F], F32R)
        w_out = sb("w_out", [128, INNER // 128, D])
        w2q = sb("w2q", [128, FC, D], BF16)
        w_inT = sb("w_inT", [128, D])
        w_gate = sb("w_gate", [128, E])
        plug_rows = sb("plug_rows", [J, B, S], BF16)
        before = sb("before", [128, 128], BF16)
        ones_bf = sb("ones_bf", [128, 128], BF16)
        ident = sb("ident", [128, 128])
        ident_bf = sb("ident_bf", [128, 128], BF16)
        ones = sb("ones", [128, 128])
        scanT = sb("scanT", [J, J])
        patch_no = sb("patch_no", [J, 1])
        conv_b = sb("conv_b", [128, F])
        ln_gain = sb("ln_gain", [128, D])
        ln_shift = sb("ln_shift", [128, D])
        b_in = sb("b_in", [J, D])
        g_init = sb("g_init", [J, D])
        g_res = sb("g_res", [128, 1])
        gates = sb("gates", [128, 4])
        w2_gain = sb("w2_gain", [128, 1])
        wsum = sb("wsum", [128, 2])
        wmean = sb("wmean", [128, 2])
        winv = sb("winv", [128, 2])
        half = sb("half", [128, 1])
        tap_gain = sb("tap_gain", [128, FC, 3])
        nullk = sb("nullk", [128, 2])
        gnull = sb("gnull", [128, H])
        expert_no = sb("expert_no", [128, E])
        gp = sb("gp", [128, 5, B])

        rows = sb("rows", [J, 2, C])
        patch = sb("patch", [J, 2, C])
        h1 = sb("h1", [128, D])
        hT = sb("hT", [128, 2, S])
        top = sb("top", [128, 2, QH])
        shifted = sb("shifted", [128, 2, QH, JN])
        probs = sb("probs", [128, 2, QH, JN])
        probsT = sb("probsT", [JN, 2, QH, S])
        V = sb("V", [JN, 2, H, DH + 1])
        rden = sb("rden", [128, 2, QH])
        attn = sb("attn", [128, 2, QH * DH])
        attnT = sb("attnT", [128, 2, INNER // 128, S])
        xb = sb("xb", [128, D])
        y1 = sb("y1", [128, D])
        y2 = sb("y2", [128, D])
        h2 = sb("h2", [128, D])
        z2 = sb("z2", [128, D])
        xq = sb("xq", [128, D])
        xqT_hi = sb("xqT_hi", [128, S + 2], F32R)
        xqT_lo = sb("xqT_lo", [128, S + 2], F32R)
        ffn = sb("ffn", [128, 4, F])
        conv, tanh_c, act2, z3 = (ffn[:, i, :] for i in range(4))
        q3 = sb("q3", [128, F], BF16)
        q3T = sb("q3T", [128, FC, S], BF16)
        h3 = sb("h3", [128, D])
        h3T = sb("h3T", [128, S])
        hp = sb("hp", [J, D])
        dep = sb("dep", [J, D])
        pick = sb("pick", [J, S])
        xs = sb("xs", [128, 2, D])
        xsT = sb("xsT", [128, S])
        raw1, raw2, raw3, raw4, rawy = (sb(f"raw_{n}", [128, 6]) for n in ("x", "x2", "x3", "x4", "y"))
        mv1, mv2, mv3, mv4, mvy = (sb(f"mv_{n}", [128, 2]) for n in ("x", "x2", "x3", "x4", "y"))
        var1, var2, var3, var4, vary = (sb(f"var_{n}", [128, 1]) for n in ("x", "x2", "x3", "x4", "y"))
        r1, r2, r3, r4, ry = (sb(f"rstd_{n}", [128, 1]) for n in ("x", "x2", "x3", "x4", "y"))
        ratio3 = sb("ratio3", [128, 3])
        rawc = sb("raw_c", [J, 6])
        mvc = sb("mv_c", [J, 2])
        msc = sb("ms_c", [J, 2])
        rc = sb("rstd_c", [J, 1])
        qs2 = sb("qs2", [128, 3])
        qs3 = sb("qs3", [128, 3])
        back3 = sb("back3", [128, 2])
        best = sb("best", [128, 8])
        best_at = sb("best_at", [128, 8], U32)
        chosen = sb("chosen", [128, 2, E])
        mask = sb("mask", [128, E], BF16)
        so_far = sb("so_far", [128, E], BF16)
        first_row = sb("first_row", [128, E])
        row_of = sb("row_of", [128, E])
        row_pick = sb("row_pick", [128, 2, E])
        row_now = sb("row_now", [128, 2, 2], U32)
        row_all = sb("row_all", [128, B, 2])
        row_idx = sb("row_idx", [128, 2, GB * 2], U32)
        pad_row = sb("pad_row", [1, E], I32)
        tile_no = sb("tile_no", [1, TILES])
        tile_at = sb("tile_at", [1, 2, TILES], I32)
        n_rows = sb("n_rows", [128, 6, E])
        best_all = sb("best_all", [128, B, 2])
        at_all = sb("at_all", [128, B, 2])

        flat = G[:, :, :, :, :].rearrange("p a b h j -> p (a b h j)")
        taken = [0]

        def part(n):
            taken[0] += n
            assert taken[0] <= 2 * GB * H * JN
            return flat[:, taken[0] - n:taken[0]]

        wq = part(INNER)
        wk = part(CC * INNER).rearrange("p (c n) -> p c n", c=CC)
        wqT = part(INNER).rearrange("p (h d) -> p h d", d=D)
        wkT = part(CC * INNER).rearrange("p (h c) -> p h c", c=C)
        w1 = part(FC * D).rearrange("p (c d) -> p c d", c=FC)
        w2 = part(F)
        wtap = part(FC * 3 * D).rearrange("p (c t d) -> p c t d", c=FC, t=3)
        w_in = part(D)
        w2t = part(F // 2).bitcast(BF16)
        eW1 = flat[:, 0:E * FF].rearrange("p (e f) -> p e f", e=E)
        b2r = flat[:, 2 * E * FF:2 * E * FF + E * D].rearrange("p (e d) -> p e d", e=E)
        eW2 = flat[:, E * FF:2 * E * FF].rearrange("p (e c d) -> p e c d", e=E, c=FFC)
        wv = ffn[:, :, :].rearrange("p (c a) n -> p c (a n)", c=CC)
        eq = attnT[:, :, :, :].rearrange("p a c s -> p (a c s)")[:, 0:16 * J].bitcast(BF16).rearrange(
            "p (t j) -> p t j", t=32)
        at_most = ffn[0:1, :, :].rearrange("p a n -> p (a n)")[:, 0:TILES * E].rearrange("p (t e) -> p t e", e=E)
        at_most_n = ffn[0:1, :, :].rearrange("p a n -> p (a n)")[:, TILES * E:2 * TILES * E].rearrange("p (t e) -> p t e", e=E)
        tile_f = ffn[0:1, :, :].rearrange("p a n -> p (a n)")[:, 2 * TILES * E:2 * TILES * E + 6 * TILES].rearrange("p (i t) -> p i t", i=6)
        len_i = sb("len_i", [128, J], I32)
        len_f = sb("len_f", [128, J])
        len_sum = sb("len_sum", [128, J])
        len_wrap = sb("len_wrap", [128, J])
        token_no = sb("token_no", [128, 32])
        edge = sb("edge", [128, 32])
        edges = sb("edges", [B, S])
        edge_sum = sb("edge_sum", [B, S])
        zero_row = sb("zero_row", [128, 128])
        plug = sb("plug", [B, S], BF16)

        with ExitStack() as first:
            def weights(name, shape):
                return first.enter_context(nc.sbuf_tensor(name, shape, F32R))

            A_hi = weights("A_hi", [128, CC, H, D])
            A_lo = weights("A_lo", [128, CC, H, D])
            wv_hi = weights("wv_hi", [128, CC, INNER])
        eb1 = sb("eb1", [128, E, FF])
        xt = sb("xt", [128, 4, D])
        xtT = sb("xtT", [128, 2, 128])
        hb = sb("hb", [128, 2, FF])
        hbT = sb("hbT", [128, 2, FFC, 128])
        ye = sb("ye", [128, 4, D])
        yg = sb("yg", [128, 2, GB, 2, D])

        move = yg[:, 0, :, :, :].rearrange("p b k d -> p (b k d)")[:, 0:2 * B * E].rearrange("p (r e) -> p r e", e=E)
        move_by = sb("move_by", [128, 2 * B])

        bank = [ctx.enter_context(nc.psum_tensor(f"bank{i}", [128, 512], F32)) for i in range(8)]
        SC, PT, AV, YH, GC, VO, T1, T2 = bank

        edge_d = nc.dram_tensor("edge_d", (B, S), F32, kind="Internal").ap()
        xe_d = nc.dram_tensor("xe_d", (E * CAP + 128, D), F32, kind="Internal").ap()
        ye_d = nc.dram_tensor("ye_d", (128 * TILES, D), F32, kind="Internal").ap()
        plug_d = nc.dram_tensor("plug_d", (B, S), BF16, kind="Internal").ap()

        ld_names = ["wq", "wk", "x0", "x1", "wv", "wout", "len", "small", "row", "edge", "plug_st", "plug", "moe"]
        ld = {n: sem(f"loaded_{n}") for n in ld_names}
        ld_rows = [sem(f"loaded_rows{i}") for i in range(2)]
        ld_patch = [sem(f"loaded_patch{i}") for i in range(2)]
        prep_pe = sem("prep_pe")
        prep_act = sem("prep_act")
        prep_dve = sem("prep_dve")
        prep_pool = sem("prep_pool")
        prep_chain = sem("prep_chain")
        prep_split = sem("prep_split")
        edge_ready = sem("edge_ready")
        plug_ready = sem("plug_ready")
        wsum_ready = sem("wsum_ready")
        wtap_ready = sem("wtap_ready")
        w2t_ready = sem("w2t_ready")
        gates_ready = sem("gates_ready")
        shift_ready = sem("shift_ready")
        main_ready = sem("main_ready")
        names = """s_done pT_done av_done oT_done G_done V_done xT_done conv_done qT_done w2_done hT_done
            T3_done L1_done T4_done gate_done dep_done cT_done y_done
            exp_ready oT_ready pT_ready G_ready xThi_ready T3_ready cThi_ready hT_ready tanh_ready qT_ready xsT_ready
            norm_ready sub_ready V_ready h1_ready h3_ready xTlo_ready cTlo_ready pick_ready conv_ready z_ready
            xq_ready x3_ready x4_ready xs_ready hp_ready dep_ready gate_taken y_taken x2_ready
            st1 st2 st3 st4 sty stc rs1 rs2 rs3 rs4 rsy rsc q_ready xb_ready cv_ready
            c_soft c_norm c_y c_st c_h2 c_conv c_gate c_pool1 c_pool2 c_pool3 c_pool4 c_pooly c_poolc
            g_exp stored c_moe moe_sum mask_ready pos_done pos_taken row_ready so_far_ready c_row
            scattered0 scattered1 n_done rows_known tiles_known padded xt_in0 xt_in1 xt_in2 xt_in3 xT_out xT_in
            h_out hb_in hbT_out hbT_in y_out ye_in ye_st0 ye_st1 ye_st2 ye_st3 idx_ready got0 got1""".split()
        m = {n: sem(n) for n in names}

        raw_sem = [sem(f"raw_{n}") for n in ("y", "x", "x2", "x3", "x4", "c")]

        def valid(b, n=B):
            return not isinstance(b, int) or 0 <= b < n

        def apart(eng, sem, count):
            if isinstance(count, int) and count <= 0:
                return
            if not isinstance(count, int):
                at = counts[eng.engine]
                eng.reg_mov(at, count)
                count = at
            eng.wait_ge(main_ready, 1)
            eng.wait_ge(sem, count)

        def upto(n, last):
            return min(n, last) if isinstance(n, int) else n

        def back(b, q, k, d):
            return b + (q - d) // 4, (q - d) % 4, (k + (q - d) // 4) % 4

        def program(eng, slot):
            def group(g):
                for j in range(16):
                    slot(g, j // 4, j % 4, 4 * g + j // 4, 16 * g + j)

            for g in (-2, -1, 0, 1):
                group(g)
            with eng.Fori(2, NG - 1) as g:
                group(g)
            for g in (NG - 1, NG):
                group(g)

        counts = {e.engine: e.alloc_register(f"count_{i}") for i, e in enumerate((nc.vector, nc.gpsimd))}
        block = ctx.enter_context(nc.Block())

        SMALL = 17
        LEN_LOADS = 4
        NULL_LOADS = 4

        @block.sync
        def _(sp):
            kv = a["L0_xattn_Wkv"].rearrange("(c p) n -> p c n", p=128)
            sp.dma_start(rows[:, 0, :], a["ctx_2048"][0]).then_inc(ld_rows[0], 16)
            sp.dma_start(wq, a["L0_xattn_Wq"]).then_inc(ld["wq"], 16)
            sp.dma_start(wk, kv[:, :, 0:INNER]).then_inc(ld["wk"], 16)
            sp.dma_start(x_res[:, 0:8, :], a["x"][0:8].rearrange("b s d -> s b d")).then_inc(ld["x0"], 16)
            sp.dma_start(wv, kv[:, :, INNER:2 * INNER]).then_inc(ld["wv"], 16)
            sp.dma_start(x_res[:, 8:B, :], a["x"][8:B].rearrange("b s d -> s b d")).then_inc(ld["x1"], 16)
            sp.dma_start(w_out[:, :, :], a["L0_xattn_Wout"].rearrange("(c p) n -> p c n", p=128)).then_inc(ld["wout"], 16)
            nk = a["L0_xattn_null_kv"]
            sp.wait_ge(prep_pool, 2)
            for i in range(2):
                sp.dma_start(nullk[64 * i:64 * i + 64, i:i + 1], nk[0:1, :].rearrange("o d -> d o")).then_inc(ld["small"], 16)
                sp.dma_start(V[J:JN, i, :, 0:DH], nk[1:2, :].unsqueeze(1).broadcast_to([1, H, DH])).then_inc(ld["small"], 16)
            sp.wait_ge(edge_ready, 1)
            for i in range(4):
                sp.dma_start(edge_d[:, 32 * i:32 * i + 32], edge[B * i:B * i + B, :]).then_inc(ld["edge"], 16)
            sp.wait_ge(ld["edge"], 64)
            sp.dma_start(edges[:, :], edge_d).then_inc(ld["row"], 16)
            sp.wait_ge(plug_ready, 1)
            sp.dma_start(plug_d, plug[:, :]).then_inc(ld["plug_st"], 16)
            sp.wait_ge(ld["plug_st"], 16)
            sp.dma_start(plug_rows[:, :, :], plug_d.partition_broadcast(J)).then_inc(ld["plug"], 16)

            def slot(g, k, q, b, s):
                if q == 0:
                    if not isinstance(b, int) or 0 <= b + 9 < CT_LAST:
                        need(sp, m["cT_done"], b + 8)
                        sp.dma_start(rows[:, (k + 1) % 2, :], a["ctx_2048"][(b + 9) % B]).then_inc(ld_rows[(k + 1) % 2], 16)
                    if valid(b - 1):
                        need(sp, m["hp_ready"], b - 2)
                        sp.dma_start(patch[:, (k + 1) % 2, :], a["ctx_2048"][b - 1]).then_inc(ld_patch[(k + 1) % 2], 16)

            program(sp, slot)
            for i in range(2):
                sp.wait_ge(ld_rows[i], 16 * ((CT_LAST + 2 - i) // 2))
            sp.wait_ge(m["s_done"], 4 * B)
            sp.dma_start(eW1, a["L1_ffn_W1"].rearrange("e p f -> p e f")).then_inc(ld["moe"], 16)
            sp.dma_start(eW2, a["L1_ffn_W2"].rearrange("e (c p) d -> p e c d", p=128)).then_inc(ld["moe"], 16)
            sp.dma_start(b2r, a["L1_ffn_b2"].partition_broadcast(128)).then_inc(ld["moe"], 16)
            sp.wait_ge(m["G_done"], 16 * NG)
            sp.dma_start(eb1[:, :, :], a["L1_ffn_b1"].partition_broadcast(128)).then_inc(ld["moe"], 16)
            for i in range(2):
                sp.wait_ge(m[f"scattered{i}"], 16 * B)
            sp.dma_start(xe_d[E * CAP:E * CAP + 128, :], zero_row[:, :]).then_inc(m["padded"], 16)
            sp.wait_ge(m["rows_known"], 1)
            for e in range(E):
                at = sp.value_load(pad_row[0:1, e:e + 1], min_val=0, max_val=E * CAP - 128)
                sp.dma_start(xe_d[bass.ds(at, 128), :], zero_row[:, :]).then_inc(m["padded"], 16)
            sp.wait_ge(m["tiles_known"], 1)
            sp.wait_ge(m["padded"], 16 * (E + 1))

            def load_tile(u, j):
                at = sp.value_load(tile_at[0:1, 0, bass.ds(4 * u + j, 1)], min_val=0, max_val=E * CAP)
                sp.dma_start(xt[:, j, :], xe_d[bass.ds(at, 128), :]).then_inc(m[f"xt_in{j}"], 16)

            for j in range(4):
                load_tile(0, j)
            with sp.Fori(1, TILES // 4) as u:
                for j in range(4):
                    sp.wait_ge(m["xT_out"], 4 * u - 3 + j)
                    load_tile(u, j)

            out_v = out.rearrange("(t b) s d -> t s b d", b=GB)
            with sp.Fori(0, NG) as t:
                sp.wait_ge(m["moe_sum"], 2 * GB * (t + 1))
                sp.dma_start(out_v[t], x_res[:, bass.ds(GB * t, GB), :]).then_inc(m["stored"], 16)
            sp.wait_ge(m["stored"], 16 * NG)

        @block.gpsimd
        def _(pool):
            pool.memset(nullk[:, :], 0.0).then_inc(prep_pool, 1)
            pool.memset(V[:, :, :, :], 1.0).then_inc(prep_pool, 1)
            pool.memset(ident[:, :], 0.0).then_inc(prep_pool, 1)
            pool.memset(ones[:, :], 1.0).then_inc(prep_pool, 1)
            pool.memset(half[:, :], -0.5).then_inc(prep_pool, 1)
            pool.memset(xqT_hi[:, :].bitcast(F32), 0.0).then_inc(prep_pool, 1)
            pool.memset(xqT_lo[:, :].bitcast(F32), 0.0).then_inc(prep_pool, 1)
            pool.memset(scanT[:, :], 0.0).then_inc(prep_pool, 1)
            pool.memset(zero_row[:, :], 0.0).then_inc(prep_pool, 1)
            pool.wait_ge(prep_pool, 9)
            step = chain(pool, prep_pool, 9)
            step(pool.affine_select(out=ident[:, :], in_=ident[:, :], compare_op=ALU.not_equal, fill=1.0, base=0,
                                    pattern=[[-1, 128]], channel_multiplier=1))
            for i in range(4):
                step(pool.iota(token_no[32 * i:32 * i + 32, :], pattern=[[1, 32]], base=32 * i, channel_multiplier=0,
                               allow_small_or_imprecise_dtypes=True))
            step(pool.iota(patch_no[:, :], pattern=[[0, 1]], base=1, channel_multiplier=1,
                           allow_small_or_imprecise_dtypes=True))
            step(pool.iota(expert_no[:, :], pattern=[[1, E]], base=0, channel_multiplier=0,
                           allow_small_or_imprecise_dtypes=True))
            step(pool.tensor_copy(ident_bf[:, :], ident[:, :]))
            k = 0
            while k < POWERS:
                step(pool.affine_select(out=scanT[:, :], in_=scanT[:, :], compare_op=ALU.not_equal,
                                        fill=gain * decay**k, base=k, pattern=[[-1, J]], channel_multiplier=1))
                k += 1
            step(pool.memset(so_far[:, :], 0.0))
            step(pool.memset(ones_bf[:, :], 1.0))
            step(pool.affine_select(out=before[:, :], in_=ones_bf[:, :], compare_op=ALU.is_ge, fill=0.0, base=-1,
                                    pattern=[[1, 128]], channel_multiplier=-1))
            step(pool.iota(first_row[:, :], pattern=[[CAP, E]], base=0, channel_multiplier=0,
                           allow_small_or_imprecise_dtypes=True))
            step(pool.iota(tile_no[:, :], pattern=[[1, TILES]], base=0, channel_multiplier=0,
                           allow_small_or_imprecise_dtypes=True))

            def rstd(b, var, root, ready, sem_c, src, eps, stat):
                apart(pool, stat, b + 1)
                step = chain(pool, sem_c, b)
                step(pool.tensor_scalar(var[:, :], src, eps, None, ALU.add))
                pool.tensor_tensor(root[:, :], var[:, :], half[0:root.shape[0], :], ALU.pow).then_inc(ready, 1)

            def slot(g, k, q, b, s):
                if q == 0:
                    if valid(b - 4):
                        rstd(b - 4, var4, r4, m["rs4"], m["c_pool4"], mv4[:, 1:2], LN_EPS, m["st4"])
                    if valid(b - 2):
                        rstd(b - 2, vary, ry, m["rsy"], m["c_pooly"], mvy[:, 1:2], XATTN_EPS, m["sty"])
                    if valid(b + 1):
                        rstd(b + 1, var1, r1, m["rs1"], m["c_pool1"], mv1[:, 1:2], LN_EPS, m["st1"])
                if q == 1:
                    if valid(b - 2):
                        rstd(b - 2, var2, r2, m["rs2"], m["c_pool2"], mv2[:, 1:2], LN_EPS, m["st2"])
                    if valid(b - 1):
                        need(pool, m["x2_ready"], b - 1)
                        pool.tensor_tensor(xb[:, :], x_res[:, b - 1, :], ln_shift[:, :], ALU.add)\
                            .then_inc(m["xb_ready"], 1)
                    if valid(b + 2):
                        grp = g + (k + 2) // 4
                        kk = (k + 2) % 4
                        need(pool, m["cThi_ready"], b + 3)
                        need(pool, m["cTlo_ready"], b + 3)
                        need(pool, m["V_done"], 4 * (b + 1))
                        for to, of in ((ctxv_hi, ctxT_hi), (ctxv_lo, ctxT_lo)):
                            pool.tensor_copy(to[:, k % 2, :, :], of[:, grp % 2, :, kk * J:kk * J + J].bitcast(F32))\
                                .then_inc(m["cv_ready"], 1)
                if q == 2:
                    if valid(b - 2):
                        need(pool, m["stc"], b - 1)
                        step = chain(pool, m["c_poolc"], 3 * (b - 2))
                        step(pool.tensor_tensor(msc[:, 0:1], mvc[:, 0:1], mvc[:, 0:1], ALU.mult))
                        step(pool.tensor_tensor(msc[:, 1:2], msc[:, 0:1], mvc[:, 1:2], ALU.add), apart)
                        step(pool.tensor_scalar(msc[:, 0:1], msc[:, 1:2], LN_EPS, None, ALU.add))
                        pool.tensor_tensor(rc[:, :], msc[:, 0:1], half[0:J, :], ALU.pow).then_inc(m["rsc"], 1)
                    if valid(b - 3):
                        apart(pool, m["st3"], b - 2)
                        step = chain(pool, m["c_pool3"], 5 * (b - 3))
                        step(pool.tensor_scalar(var3[:, :], mv3[:, 1:2], LN_EPS, None, ALU.add))
                        step(pool.tensor_tensor(ratio3[:, 0:1], var3[:, :], half[:, :], ALU.pow))
                        step(pool.tensor_tensor(ratio3[:, 1:2], ratio3[:, 0:1], ratio3[:, 0:1], ALU.mult), apart)
                        step(pool.tensor_scalar(ratio3[:, 2:3], ratio3[:, 1:2], mv3[:, 1:2], LN_EPS, ALU.mult, ALU.add))
                        step(pool.tensor_tensor(var3[:, :], ratio3[:, 2:3], half[:, :], ALU.pow))
                        pool.tensor_tensor(r3[:, :], var3[:, :], ratio3[:, 0:1], ALU.mult).then_inc(m["rs3"], 1)
                if q == 3 and valid(b - 4):
                    apart(pool, m["row_ready"], b - 3)
                    for i in range(2):
                        pool.indirect_dma_start(xe_d, bass.IndirectOffsetOnAxis(ap=row_now[:, k % 2, i:i + 1], axis=0),
                                                xs[:, k % 2, :], None).then_inc(m[f"scattered{k % 2}"], 16)
                if q == 3 and valid(b - 2):
                    apart(pool, m["z_ready"], b - 1)
                    need(pool, m["qT_done"], b - 2)
                    pool.tensor_scalar(q3[:, :], z3, -MAGIC, None, ALU.add).then_inc(m["q_ready"], 1)

            pool.wait_ge(ld["x0"], 16)
            pool.wait_ge(ld["x1"], 16)
            pool.wait_ge(shift_ready, 1)
            program(pool, slot)

            with pool.Fori(0, TILES // 4) as u:
                for j in range(4):
                    pool.wait_ge(m["ye_in"], 4 * u + j + 1)
                    pool.dma_start(ye_d.rearrange("(t r) d -> t r d", r=128)[4 * u + j], ye[:, j, :])\
                        .then_inc(m[f"ye_st{j}"], 16)
            for j in range(4):
                pool.wait_ge(m[f"ye_st{j}"], 16 * (TILES // 4))
            with pool.Fori(0, NG // 2) as u:
                for i in range(2):
                    apart(pool, m["idx_ready"], 2 * u + i + 1)
                    for jb in range(GB):
                        for kk in range(2):
                            pool.indirect_dma_start(yg[:, i, jb, kk, :], None, ye_d,
                                                    bass.IndirectOffsetOnAxis(ap=row_idx[:, i, 2 * jb + kk:2 * jb + kk + 1], axis=0))\
                                .then_inc(m[f"got{i}"], 16)

        JOBS = 21
        A_JOBS = range(6, 14)
        TAP_JOBS = range(17, 20)

        def a_job(n):
            r = (n - 6) % 4
            return (n - 6) // 4, 8 * (r // 2) + r % 2

        def low_parts(n):
            return sum(j in A_JOBS or j in TAP_JOBS for j in range(n))

        @block.tensor
        def _(pe):
            for n in range(JOBS):
                b8 = bank[n % 8]
                need(pe, prep_act, n - 7)
                need(pe, prep_dve, low_parts(max(n - 7, 0)))
                if n < 2:
                    if n == 0:
                        pe.wait_ge(prep_pool, 17)
                        pe.wait_ge(ld["wq"], 16)
                    for i in range(4):
                        mm = pe.transpose(b8[:, 128 * i:128 * i + 128], wq[:, 128 * (4 * n + i):128 * (4 * n + i) + 128], ident[:, :])
                elif n < 6:
                    if n == 2:
                        pe.wait_ge(ld["wk"], 16)
                    for i in range(4):
                        h2_, c = 2 * (n - 2) + i // 2, i % 2
                        mm = pe.transpose(b8[:, 128 * i:128 * i + 128], wk[:, c, 128 * h2_:128 * h2_ + 128], ident[:, :])
                elif n < 14:
                    if n == 6:
                        pe.wait_ge(prep_act, 6)
                    c, h0 = a_job(n)
                    r = 64 * (h0 % 2)
                    for i in range(4):
                        h = h0 + 2 * i
                        mm = pe.matmul(b8[:, 128 * i:128 * i + 128], wkT[r:r + 64, h // 2, 128 * c:128 * c + 128],
                                       wqT[r:r + 64, h // 2, :], start=True, stop=True)
                elif n == 14:
                    pe.wait_ge(ld["small"], 16 * SMALL)
                    for i in range(H // 2):
                        mm = pe.matmul(b8[:, 2 * i:2 * i + 2], wqT[:, i, :], nullk[:, :], start=True, stop=True)
                elif n == 15:
                    pe.wait_ge(wsum_ready, 2)
                    mm = pe.matmul(b8[:, 0:2], ones[:, :], wsum[:, :], start=True, stop=True)
                elif n == 16:
                    mm = pe.transpose(b8[:, 0:128], w_in, ident[:, :])
                elif n < 20:
                    if n == 17:
                        pe.wait_ge(wtap_ready, 3 * FC)
                    for i in range(FC):
                        mm = pe.transpose(b8[:, 128 * i:128 * i + 128], wtap[:, i, n - 17, :], ident[:, :])
                else:
                    pe.wait_ge(w2t_ready, 1)
                    for i in range(FC):
                        mm = pe.transpose(b8[:, 64 * i:64 * i + 64].bitcast(BF16), w2t[:, 128 * i:128 * i + 128], ident_bf[:, :])
                mm.then_inc(prep_pe, 1)
            pe.wait_ge(prep_act, JOBS)
            pe.wait_ge(prep_dve, low_parts(JOBS))
            pe.wait_ge(ld["wout"], 16)
            pe.wait_ge(prep_split, 2)
            pe.wait_ge(main_ready, 1)
            pe.wait_ge(prep_pool, 17 + POWERS + 5)

            def split3(o, w_hi, w_lo, x_hi, x_lo, first, last):
                pe.matmul(o, w_lo, x_hi, start=first, stop=False)
                pe.matmul(o, w_hi, x_lo, start=False, stop=False)
                return pe.matmul(o, w_hi, x_hi, start=False, stop=last)

            def slot(g, k, q, b, s):
                if q == 3 and valid(b - 4):
                    need(pe, m["mask_ready"], b - 3)
                    need(pe, m["so_far_ready"], b - 4)
                    need(pe, m["norm_ready"], upto(s - 2, 4 * B))
                    pe.matmul(AV[:, 264:264 + E], before[:, :], mask[:, :], start=True, stop=False)
                    pe.matmul(AV[:, 264:264 + E], ones_bf[:, :], so_far[:, :], start=False, stop=True).then_inc(m["pos_done"], 1)
                if valid(s - 2, 4 * B):
                    t = s - 2
                    if q == 0 and valid(b - 5):
                        need(pe, m["pos_taken"], b - 4)
                    bt, qt, kt = back(b, q, k, 2)
                    need(pe, m["pT_ready"], t + 1)
                    need(pe, m["V_ready"], t + 1)
                    need(pe, m["norm_ready"], t)
                    for i in range(QH):
                        mm = pe.matmul(AV[:, i * (DH + 1):(i + 1) * (DH + 1)], probsT[:, qt % 2, i, :],
                                       V[:, kt % 2, QH * qt + i, :], start=True, stop=True)
                    mm.then_inc(m["av_done"], 1)
                if valid(b):
                    need(pe, m["G_ready"], 16 * g + QH * (q + 1))
                    need(pe, m["hT_ready"], b + 1)
                    need(pe, m["sub_ready"], s)
                    pe.matmul(SC[:, 0:QH * JN], hT[:, k % 2, :],
                              G[:, g % 2, k, QH * q:QH * q + QH, :].rearrange("p h j -> p (h j)"),
                              start=True, stop=True).then_inc(m["s_done"], 1)
                if valid(b + 1):
                    need(pe, m["cv_ready"], 2 * (b + 2))
                    need(pe, m["V_ready"], s + 4)
                    need(pe, m["oT_ready"], s - 3)
                    for c in range(CC):
                        mm = split3(VO[0:J, 0:QH * DH], ctxv_hi[:, (k + 1) % 2, c, :], ctxv_lo[:, (k + 1) % 2, c, :],
                                    wv_hi[:, c, QH * DH * q:QH * DH * (q + 1)], wv_lo[:, c, QH * DH * q:QH * DH * (q + 1)],
                                    c == 0, c == CC - 1)
                    mm.then_inc(m["V_done"], 1)
                if q == 0 and valid(b - 3):
                    need(pe, m["q_ready"], b - 2)
                    need(pe, m["dep_ready"], b - 2)
                    for i in range(FC):
                        mm = pe.transpose(T1[:, 64 * i:64 * i + 64].bitcast(BF16), q3[:, 128 * i:128 * i + 128], ident_bf[:, :])
                    mm.then_inc(m["qT_done"], 1)
                if q == 1 and valid(b - 3):
                    need(pe, m["qT_ready"], b - 2)
                    for i in range(FC):
                        mm = pe.matmul(T1[:, 0:D], q3T[:, i, :], w2q[:, i, :], start=(i == 0), stop=(i == FC - 1))
                    mm.then_inc(m["w2_done"], 1)
                if q == 2 and valid(b - 2):
                    need(pe, m["xq_ready"], b - 1)
                    need(pe, m["x3_ready"], b - 2)
                    pe.transpose(T1[:, 0:S], xq[:, :], ident[:, :]).then_inc(m["xT_done"], 1)
                if q == 3:
                    if valid(b - 3):
                        need(pe, m["T3_ready"], b - 2)
                        need(pe, m["pick_ready"], b - 2)
                        need(pe, m["dep_ready"], b - 2)
                        pe.matmul(T2[:, 0:D], h3T[:, :], w_inT[:, :], start=True, stop=False)
                        pe.matmul(T2[:, 0:D], pick[:, :], dep[:, :], start=False, stop=True).then_inc(m["L1_done"], 1)
                    if valid(b - 2):
                        need(pe, m["hp_ready"], b - 1)
                        need(pe, m["conv_ready"], b - 1)
                        pe.matmul(T1[0:J, 0:D], scanT[:, :], hp[:, :], start=True, stop=True).then_inc(m["dep_done"], 1)
                if valid(s - 1, 4 * B):
                    t = s - 1
                    bt, qt, kt = back(b, q, k, 1)
                    need(pe, m["exp_ready"], t + 1)
                    need(pe, m["pT_ready"], t)
                    for i in range(QH):
                        mm = pe.transpose(PT[0:JN, 128 * i:128 * i + 128], probs[:, qt % 2, i, :], ident[:, :])
                    mm.then_inc(m["pT_done"], 1)
                if valid(g + 1, NG):
                    h = 4 * k + q
                    n = 16 * (g + 1) + h
                    need(pe, m["G_ready"], n)
                    need(pe, m["cThi_ready"], 4 * (g + 2))
                    need(pe, m["cTlo_ready"], 4 * (g + 2))
                    for c in range(CC):
                        mm = split3(GC[:, 0:GB * J], A_hi[:, c, h, :], A_lo[:, c, h, :],
                                    ctxT_hi[:, (g + 1) % 2, c, :], ctxT_lo[:, (g + 1) % 2, c, :], c == 0, c == CC - 1)
                    mm.then_inc(m["G_done"], 1)
                if q == 0 and valid(b - 4):
                    need(pe, m["xs_ready"], b - 3)
                    need(pe, m["x4_ready"], b - 3)
                    pe.transpose(T2[:, 0:S], xs[:, k % 2, :], ident[:, :]).then_inc(m["T4_done"], 1)
                if q == 1:
                    if valid(b - 4):
                        need(pe, m["xsT_ready"], b - 3)
                        pe.matmul(T2[:, 0:E], xsT[:, :], w_gate[:, :], start=True, stop=True).then_inc(m["gate_done"], 1)
                    if not isinstance(b, int) or 0 <= b + 8 < CT_LAST:
                        need(pe, ld_rows[k % 2], 16 * (2 * g + (k + 8) // 2 + 1))
                        need(pe, m["y_taken"], b - 1)
                        need(pe, m["hT_ready"], b + 1)
                        need(pe, m["cThi_ready"], b + 8)
                        need(pe, m["cTlo_ready"], b + 8)
                        for c in range(CC):
                            mm = pe.transpose(YH[:, J * c:J * c + J], rows[:, k % 2, 128 * c:128 * c + 128], ident[0:J, 0:J])
                        mm.then_inc(m["cT_done"], 1)
                if q == 2:
                    if valid(b - 2):
                        need(pe, m["xThi_ready"], b - 1)
                        need(pe, m["xTlo_ready"], b - 1)
                        for i in range(3):
                            mm = split3(T1[:, :], xqT_hi[:, i:i + S], xqT_lo[:, i:i + S], tap_hi[:, i, :], tap_lo[:, i, :],
                                        i == 0, i == 2)
                        mm.then_inc(m["conv_done"], 1)
                    if valid(b + 1):
                        need(pe, m["h1_ready"], b + 2)
                        need(pe, m["cThi_ready"], upto(b + 9, CT_LAST))
                        need(pe, m["cTlo_ready"], upto(b + 9, CT_LAST))
                        need(pe, m["y_taken"], b - 1)
                        pe.transpose(YH[:, 0:S], h1[:, :], ident[:, :]).then_inc(m["hT_done"], 1)
                    if valid(b - 3):
                        need(pe, m["h3_ready"], b - 2)
                        need(pe, m["gate_taken"], b - 3)
                        pe.transpose(T2[:, 0:S], h3[:, :], ident[:, :]).then_inc(m["T3_done"], 1)
                if q == 3 and valid(b - 1):
                    need(pe, m["oT_ready"], 4 * b)
                    need(pe, m["hT_ready"], upto(b + 2, B))
                    need(pe, m["y_taken"], b - 1)
                    for i in range(INNER // 128):
                        mm = pe.matmul(YH[:, 0:D], attnT[:, (k + 1) % 2, i, :], w_out[:, i, :],
                                       start=(i == 0), stop=(i == INNER // 128 - 1))
                    mm.then_inc(m["y_done"], 1)
                if valid(s - 3, 4 * B):
                    t = s - 3
                    bt, qt, kt = back(b, q, k, 3)
                    need(pe, m["norm_ready"], t + 1)
                    need(pe, m["oT_ready"], t)
                    need(pe, m["V_ready"], upto(s + 5, 4 * B))
                    for i in range(2):
                        mm = pe.transpose(VO[:, 256 + 128 * i:384 + 128 * i], attn[:, qt % 2, 128 * i:128 * i + 128], ident[:, :])
                    mm.then_inc(m["oT_done"], 1)

            program(pe, slot)

            pe.wait_ge(m["so_far_ready"], B)
            pe.wait_ge(m["pos_taken"], B)
            pe.matmul(AV[:, 264:264 + E], ones_bf[:, :], so_far[:, :], start=True, stop=True).then_inc(m["n_done"], 1)
            pe.wait_ge(ld["moe"], 64)
            pe.wait_ge(m["tiles_known"], 1)

            def transpose_rows(i, j):
                pe.wait_ge(m[f"xt_in{j % 4}"], 4 * (i - j % 4) + 16)
                need(pe, m["xT_in"], i - 1)
                pe.transpose(bank[j % 2][:, 0:128], xt[:, j % 4, :], ident[:, :]).then_inc(m["xT_out"], 1)

            def tile(i, j, n=TILES):
                def expert(lag):
                    return pe.value_load(tile_at[0:1, 1, bass.ds(i - lag, 1)] if not isinstance(i, int)
                                         else tile_at[0:1, 1, i - lag:i - lag + 1], min_val=0, max_val=E - 1)

                if valid(i, n):
                    e = expert(0)
                    pe.wait_ge(m["xT_in"], i + 1)
                    need(pe, m["hb_in"], i - 1)
                    pe.matmul(bank[2 + j % 2][:, :], xtT[:, j % 2, :], eW1[:, e, :], start=True, stop=True)\
                        .then_inc(m["h_out"], 1)
                if valid(i + 1, n):
                    transpose_rows(i + 1, j + 1)
                if valid(i - 2, n):
                    w = eW2[:, expert(2), :, :]
                    pe.wait_ge(m["hbT_in"], i - 1)
                    need(pe, m["ye_in"], i - 3)
                    for c in range(FFC):
                        mm = pe.matmul(bank[6 + j % 2][:, 0:D], hbT[:, j % 2, c, :], w[:, c, :], start=(c == 0), stop=(c == FFC - 1))
                    mm.then_inc(m["y_out"], 1)
                if valid(i - 1, n):
                    pe.wait_ge(m["hb_in"], i)
                    need(pe, m["hbT_in"], i - 2)
                    for c in range(FFC):
                        mm = pe.transpose(bank[4 + (j + 1) % 2][:, 128 * c:128 * c + 128], hb[:, (j + 1) % 2, 128 * c:128 * c + 128], ident[:, :])
                    mm.then_inc(m["hbT_out"], 1)

            transpose_rows(0, 0)
            for j in range(4):
                tile(j, j)
            with pe.Fori(1, TILES // 4 - 1) as u:
                for j in range(4):
                    tile(4 * u + j, j)
            for j in range(6):
                tile(TILES - 4 + j, j)

        @block.scalar
        def _(act):
            for i in range(LEN_LOADS):
                act.dma_start(len_i[B * i:B * i + B, :], a["mask_BxS2_if0"]).then_inc(ld["len"], 16)
            n = NULL_LOADS
            for dst, src in (
                (w1, a["L0_ffn_w1"].rearrange("(c p) d -> p c d", p=128)),
                (w2, a["L0_ffn_w2"]),
                (gates[:, 0:2], a["g_xattn"].partition_broadcast(128)),
                (gates[:, 2:4], a["g_ffn"].partition_broadcast(128)),
                (w_in, a["L1_xattn_W_in"]),
                (w_gate[:, :], a["L1_ffn_Wg"]),
                (tap_gain[:, :, :], a["L0_ffn_conv_w"].rearrange("(c p) o t -> p c (o t)", p=128)),
                (conv_b[:, :], a["L0_ffn_conv_b"].partition_broadcast(128)),
                (ln_gain[:, :], a["L0_xattn_ln_scale"].partition_broadcast(128)),
                (ln_shift[:, :], a["L0_xattn_ln_bias"].partition_broadcast(128)),
                (b_in[:, :], a["L1_xattn_b_in"].partition_broadcast(J)),
                (g_init[:, :], a["L1_xattn_g_init"][0:D].partition_broadcast(J)),
                (g_res[:, :], a["L1_xattn_g_res"].rearrange("(p o) -> p o", o=1)),
            ):
                act.dma_start(dst, src).then_inc(ld["small"], 16)
                n += 1
            assert n == SMALL
            act.wait_ge(ld["small"], 16 * SMALL)
            act.activation(gates[:, :], gates[:, :], ACT.Tanh).then_inc(gates_ready, 1)
            for n in range(JOBS):
                b8 = bank[n % 8]
                act.wait_ge(prep_pe, n + 1)
                if n < 2:
                    ins = act.activation(wqT[:, 4 * n:4 * n + 4, :].rearrange("p h d -> p (h d)"), b8[:, :], ACT.Copy, scale=SCALE)
                elif n < 6:
                    ins = act.activation(wkT[:, 2 * (n - 2):2 * (n - 2) + 2, :].rearrange("p h c -> p (h c)"), b8[:, :], ACT.Copy)
                elif n < 14:
                    c, h0 = a_job(n)
                    ins = act.activation(A_hi[:, c, h0:h0 + 7:2, :], b8[:, :].rearrange("p (h d) -> p h d", h=4), ACT.Copy)
                elif n == 14:
                    ins = act.activation(gnull[:, :], b8[:, 0:H], ACT.Copy)
                elif n == 15:
                    ins = act.activation(wmean[:, :], b8[:, 0:2], ACT.Copy, scale=1.0 / (F * D))
                elif n == 16:
                    ins = act.activation(w_inT[:, :], b8[:, 0:128], ACT.Copy, scale=g_res[:, :])
                elif n < 20:
                    ins = act.activation(tap_hi[:, n - 17, :], b8[:, :], ACT.Copy)
                else:
                    ins = act.activation(w2q[:, :, :].rearrange("p c d -> p (c d)"), b8[:, 0:256].bitcast(BF16), ACT.Copy)
                ins.then_inc(prep_act, 1)
                if n == 13:
                    act.wait_ge(ld["wv"], 16)
                    act.activation(wv_hi[:, :, :], wv, ACT.Copy).then_inc(prep_split, 1)
            act.wait_ge(main_ready, 1)

            def slot(g, k, q, b, s):
                if valid(s - 4, 4 * B):
                    t = s - 4
                    bt, qt, kt = back(b, q, k, 4)
                    need(act, m["oT_done"], t + 1)
                    need(act, m["y_done"], bt - 1)
                    act.activation(attnT[:, kt % 2, 2 * qt:2 * qt + 2, :].rearrange("p c s -> p (c s)"), VO[:, 256:512], ACT.Copy)\
                        .then_inc(m["oT_ready"], 1)
                if valid(b + 1):
                    need(act, m["V_done"], s + 5)
                    need(act, m["av_done"], s - 3)
                    act.activation(V[0:J, (k + 1) % 2, QH * q:QH * q + QH, 0:DH],
                                   VO[0:J, 0:QH * DH].rearrange("p (h d) -> p h d", h=QH), ACT.Copy).then_inc(m["V_ready"], 1)
                if q == 2 and valid(b - 2):
                    need(act, m["xT_done"], b - 1)
                    need(act, m["conv_done"], b - 2)
                    act.activation(xqT_hi[:, 1:S + 1], T1[:, 0:S], ACT.Copy).then_inc(m["xThi_ready"], 1)
                if q == 1 and valid(b - 4):
                    need(act, m["T4_done"], b - 3)
                    need(act, m["gate_done"], b - 4)
                    act.activation(xsT[:, :], T2[:, 0:S], ACT.Copy).then_inc(m["xsT_ready"], 1)
                if valid(b):
                    need(act, m["sub_ready"], s + 1)
                    need(act, m["pT_done"], s - 1)
                    act.activation(probs[:, q % 2, :, :], shifted[:, q % 2, :, :], ACT.Exp).then_inc(m["exp_ready"], 1)
                if q == 0 and valid(b - 3):
                    need(act, m["qT_done"], b - 2)
                    need(act, m["w2_done"], b - 3)
                    act.activation(q3T[:, :, :].rearrange("p c s -> p (c s)"), T1[:, 0:256].bitcast(BF16), ACT.Copy)\
                        .then_inc(m["qT_ready"], 1)
                if q == 3 and valid(b - 2):
                    need(act, m["conv_ready"], b - 1)
                    need(act, m["c_conv"], 5 * (b - 2))
                    act.activation(tanh_c, conv, ACT.Tanh, scale=0.5).then_inc(m["tanh_ready"], 1)
                if valid(s - 1, 4 * B):
                    t = s - 1
                    bt, qt, kt = back(b, q, k, 1)
                    need(act, m["pT_done"], t + 1)
                    need(act, m["av_done"], t - 1)
                    act.activation(probsT[:, qt % 2, :, :].rearrange("p h s -> p (h s)"), PT[0:JN, :], ACT.Copy)\
                        .then_inc(m["pT_ready"], 1)
                if valid(g + 1, NG):
                    h = 4 * k + q
                    n = 16 * (g + 1) + h
                    need(act, m["G_done"], n + 1)
                    need(act, m["s_done"], 16 * g)
                    act.activation(G[:, (g + 1) % 2, :, h, 0:J], GC[:, 0:GB * J].rearrange("p (b j) -> p b j", b=GB), ACT.Copy)\
                        .then_inc(m["G_ready"], 1)
                if q == 1 and (not isinstance(b, int) or 0 <= b + 8 < CT_LAST):
                    need(act, m["cT_done"], b + 9)
                    need(act, m["G_done"], 16 * (g + 1))
                    need(act, m["cv_ready"], upto(2 * (b + 1), 2 * B))
                    act.activation(ctxT_hi[:, g % 2, :, k * J:k * J + J], YH[:, 0:CC * J].rearrange("p (c j) -> p c j", c=CC), ACT.Copy)\
                        .then_inc(m["cThi_ready"], 1)
                if q == 2:
                    if valid(b + 1):
                        need(act, m["hT_done"], b + 2)
                        need(act, m["s_done"], 4 * b)
                        act.activation(hT[:, (k + 1) % 2, :], YH[:, 0:S], ACT.Copy).then_inc(m["hT_ready"], 1)
                    if valid(b - 3):
                        need(act, m["T3_done"], b - 2)
                        need(act, m["L1_done"], b - 3)
                        act.activation(h3T[:, :], T2[:, 0:S], ACT.Copy).then_inc(m["T3_ready"], 1)

            program(act, slot)
            act.wait_ge(m["c_moe"], 1)
            act.activation(gp[:, 1, :], gp[:, 0, :], ACT.Exp).then_inc(m["g_exp"], 1)


            def tile(i, j, n=TILES):
                if valid(i, n):
                    act.wait_ge(m["xT_out"], i + 1)
                    need(act, m["h_out"], i - 1)
                    act.activation(xtT[:, j % 2, :], bank[j % 2][:, 0:128], ACT.Copy).then_inc(m["xT_in"], 1)
                if valid(i - 2, n):
                    act.wait_ge(m["hbT_out"], i - 1)
                    need(act, m["y_out"], i - 3)
                    act.activation(hbT[:, j % 2, :, :].rearrange("p c t -> p (c t)"), bank[4 + j % 2][:, :], ACT.Relu)\
                        .then_inc(m["hbT_in"], 1)

            for j in range(4):
                tile(j, j)
            with act.Fori(1, TILES // 4) as u:
                for j in range(4):
                    tile(4 * u + j, j)
            for j in range(2):
                tile(TILES + j, j)

        @block.vector
        def _(dve):
            step = chain(dve, prep_chain, 0)
            dve.wait_ge(ld["len"], 16 * LEN_LOADS)
            dve.wait_ge(prep_pool, 16)
            step(dve.tensor_scalar(len_f[:, :], len_i[:, :], PATCH_CLIP, -PATCH_CLIP, ALU.min, ALU.max))
            step(dve.tensor_tensor_scan(len_sum[:, :], len_f[:, :], zero_row[:, 0:J], 0.0, ALU.add, ALU.add))
            step(dve.tensor_scalar(len_f[:, :], len_sum[:, :], -1.0, None, ALU.add))
            step(dve.tensor_scalar(len_wrap[:, :], len_f[:, :], 0.0, float(S), ALU.is_lt, ALU.mult))
            step(dve.tensor_tensor(len_sum[:, :], len_f[:, :], len_wrap[:, :], ALU.add))
            step(dve.tensor_tensor(eq, len_sum[:, :].unsqueeze(1).broadcast_to([128, 32, J]),
                                   token_no[:, :].unsqueeze(2).broadcast_to([128, 32, J]), ALU.is_equal))
            dve.tensor_reduce(edge[:, :], eq, AX.X, ALU.max).then_inc(edge_ready, 1)
            dve.wait_ge(ld["small"], 16 * SMALL)
            dve.tensor_reduce(wsum[:, 0:1], w1, AX.XY, ALU.add, apply_absolute_value=True).then_inc(wsum_ready, 1)
            dve.tensor_reduce(wsum[:, 1:2], w2, AX.X, ALU.add, apply_absolute_value=True).then_inc(wsum_ready, 1)
            for n in A_JOBS:
                c, h0 = a_job(n)
                dve.wait_ge(prep_act, n + 1)
                dve.tensor_tensor(A_lo[:, c, h0:h0 + 7:2, :], bank[n % 8][:, :].rearrange("p (h d) -> p h d", h=4),
                                  A_hi[:, c, h0:h0 + 7:2, :].bitcast(F32), ALU.subtract).then_inc(prep_dve, 1)
            dve.wait_ge(ld["row"], 16)
            step(dve.tensor_tensor_scan(edge_sum[:, :], edges[:, :], zero_row[0:B, :], 0.0, ALU.add, ALU.add))
            dve.tensor_scalar(plug[:, :], edge_sum[:, :], 1.0, None, ALU.max).then_inc(plug_ready, 1)
            dve.wait_ge(prep_act, 16)
            dve.wait_ge(gates_ready, 1)
            step(dve.tensor_scalar(wsum[:, :], wmean[:, :], QUANT_FLOOR, None, ALU.max))
            step(dve.reciprocal(winv[:, :], wsum[:, :]))
            step(dve.tensor_scalar(w1, w1, winv[:, 0:1], -1.0, ALU.mult, ALU.max))
            step(dve.tensor_scalar(w1, w1, 1.0, MAGIC, ALU.min, ALU.add))
            step(dve.tensor_scalar(w1, w1, -MAGIC, wsum[:, 0:1], ALU.add, ALU.mult))
            for c in range(FC):
                for t in range(3):
                    dve.tensor_scalar(wtap[:, c, t, :], w1[:, c, :], tap_gain[:, c, t:t + 1], None, ALU.mult).then_inc(wtap_ready, 1)
            step(dve.tensor_scalar(w2, w2, winv[:, 1:2], -1.0, ALU.mult, ALU.max))
            step(dve.tensor_scalar(w2, w2, 1.0, MAGIC, ALU.min, ALU.add))
            dve.tensor_scalar(w2t, w2, -MAGIC, None, ALU.add).then_inc(w2t_ready, 1)
            step(dve.tensor_scalar(w2_gain[:, :], wsum[:, 1:2], gates[:, 2:3], 0.5, ALU.mult, ALU.mult))
            step(dve.tensor_scalar(ln_gain[:, :], ln_gain[:, :], gates[:, 0:1], None, ALU.mult))
            dve.tensor_scalar(ln_shift[:, :], ln_shift[:, :], gates[:, 0:1], None, ALU.mult).then_inc(shift_ready, 1)
            dve.wait_ge(prep_split, 1)
            dve.tensor_tensor(wv_lo[:, :, :], wv, wv_hi[:, :, :].bitcast(F32), ALU.subtract).then_inc(prep_split, 1)
            for n in TAP_JOBS:
                dve.wait_ge(prep_act, n + 1)
                dve.tensor_tensor(tap_lo[:, n - 17, :], bank[n % 8][:, :], tap_hi[:, n - 17, :].bitcast(F32), ALU.subtract)\
                    .then_inc(prep_dve, 1)
            dve.wait_ge(prep_act, JOBS)
            for i in range(2):
                ins = dve.tensor_copy(G[:, i, :, :, J], gnull[:, :].unsqueeze(1).broadcast_to([128, GB, H]))
            ins.then_inc(main_ready, 1)
            dve.wait_ge(ld["x0"], 16)
            dve.wait_ge(ld["x1"], 16)
            dve.wait_ge(ld["plug"], 16)
            dve.wait_ge(prep_pool, 17)

            def stats(b, src, raw, mv, ready, written=None):
                if written:
                    apart(dve, written, b + 1)
                dve.bn_stats(raw[:, :], src).then_inc(ready[0], 1)
                apart(dve, ready[0], b + 1)
                dve.bn_aggr(mv[:, :], raw[:, :]).then_inc(ready[1], 1)

            def norm_by(dst, src, mv, root):
                return dve.tensor_scalar(dst, src, mv[:, 0:1], root[:, 0:1], ALU.subtract, ALU.mult)

            def slot(g, k, q, b, s):
                if q == 0 and valid(b - 2):
                    stats(b - 2, YH[:, 0:D], rawy, mvy, (raw_sem[0], m["sty"]), m["y_done"])
                if q == 3 and valid(b - 2):
                    need(dve, m["conv_done"], b - 1)
                    dve.tensor_tensor(conv, T1[:, :], conv_b[:, :], ALU.add).then_inc(m["conv_ready"], 1)
                if valid(s - 2, 4 * B):
                    t = s - 2
                    bt, qt, kt = back(b, q, k, 2)
                    need(dve, m["av_done"], t + 1)
                    need(dve, m["oT_done"], t - 1)
                    av = AV[:, 0:QH * (DH + 1)].rearrange("p (h d) -> p h d", h=QH)
                    dve.reciprocal(rden[:, qt % 2, :], av[:, :, DH]).then_inc(m["c_norm"], 1)
                    dve.wait_ge(m["c_norm"], t + 1)
                    dve.tensor_tensor(attn[:, qt % 2, :].rearrange("p (h d) -> p h d", h=QH), av[:, :, 0:DH],
                                      rden[:, qt % 2, :].unsqueeze(2).broadcast_to([128, QH, DH]), ALU.mult)\
                        .then_inc(m["norm_ready"], 1)
                if valid(b):
                    sc = SC[:, 0:QH * JN].rearrange("p (h j) -> p h j", h=QH)
                    need(dve, m["s_done"], s + 1)
                    need(dve, m["exp_ready"], s - 1)
                    dve.tensor_reduce(top[:, q % 2, :], sc, AX.X, ALU.max).then_inc(m["c_soft"], 1)
                    dve.wait_ge(m["c_soft"], s + 1)
                    dve.tensor_tensor(shifted[:, q % 2, :, :], sc, top[:, q % 2, :].unsqueeze(2).broadcast_to([128, QH, JN]),
                                      ALU.subtract).then_inc(m["sub_ready"], 1)
                if q == 0:
                    if valid(b + 1):
                        stats(b + 1, x_res[:, b + 1, :], raw1, mv1, (raw_sem[1], m["st1"]))
                    if valid(b - 4):
                        need(dve, m["rs4"], b - 3)
                        need(dve, m["T4_done"], b - 5)
                        need(dve, m[f"scattered{k % 2}"], 32 * (2 * g + k // 2 - 2))
                        norm_by(xs[:, k % 2, :], x_res[:, b - 4, :], mv4, r4).then_inc(m["xs_ready"], 1)
                    if valid(b - 2):
                        need(dve, m["rsy"], b - 1)
                        need(dve, m["xb_ready"], b - 1)
                        norm_by(y1[:, :], YH[:, 0:D], mvy, ry).then_inc(m["y_taken"], 1)
                        dve.wait_ge(m["y_taken"], b - 1)
                        dve.tensor_tensor(y2[:, :], y1[:, :], ln_gain[:, :], ALU.mult).then_inc(m["c_y"], 1)
                        dve.wait_ge(m["c_y"], b - 1)
                        dve.tensor_tensor(x_res[:, b - 2, :], y2[:, :], xb[:, :], ALU.add).then_inc(m["x2_ready"], 1)
                        stats(b - 2, x_res[:, b - 2, :], raw2, mv2, (raw_sem[2], m["st2"]), m["x2_ready"])
                if q == 1:
                    if valid(b + 1):
                        need(dve, m["rs1"], b + 2)
                        need(dve, m["hT_done"], b + 1)
                        norm_by(h1[:, :], x_res[:, b + 1, :], mv1, r1).then_inc(m["h1_ready"], 1)
                    if valid(b - 3):
                        need(dve, m["w2_done"], b - 2)
                        need(dve, m["c_conv"], 5 * (b - 2))
                        dve.scalar_tensor_tensor(x_res[:, b - 3, :], T1[:, 0:D], back3[:, (k + 1) % 2:(k + 1) % 2 + 1],
                                                 x_res[:, b - 3, :], ALU.mult, ALU.add).then_inc(m["x3_ready"], 1)
                        stats(b - 3, x_res[:, b - 3, :], raw3, mv3, (raw_sem[3], m["st3"]), m["x3_ready"])
                    if valid(b - 2):
                        apart(dve, ld_patch[k % 2], 16 * (2 * g + (k - 2) // 2 + 1))
                        dve.bn_stats(rawc[:, :], patch[:, k % 2, :]).then_inc(raw_sem[5], 1)
                        apart(dve, raw_sem[5], b - 1)
                        dve.bn_aggr(mvc[:, :], rawc[:, :]).then_inc(m["stc"], 1)
                        need(dve, m["rs2"], b - 1)
                        need(dve, m["xT_done"], b - 2)
                        step = chain(dve, m["c_h2"], 5 * (b - 2))
                        step(norm_by(h2[:, :], x_res[:, b - 2, :], mv2, r2))
                        step(dve.tensor_reduce(qs2[:, 0:1], h2[:, :], AX.X, ALU.max, apply_absolute_value=True))
                        step(dve.tensor_scalar(qs2[:, 1:2], qs2[:, 0:1], QUANT_FLOOR, 1.0 / 127.0, ALU.max, ALU.mult))
                        step(dve.reciprocal(qs2[:, 2:3], qs2[:, 1:2]))
                        step(dve.tensor_scalar(z2[:, :], h2[:, :], qs2[:, 2:3], MAGIC, ALU.mult, ALU.add))
                        dve.tensor_scalar(xq[:, :], z2[:, :], -MAGIC, qs2[:, 1:2], ALU.add, ALU.mult).then_inc(m["xq_ready"], 1)
                    if not isinstance(b, int) or 0 <= b + 8 < CT_LAST:
                        need(dve, m["cThi_ready"], b + 9)
                        dve.tensor_tensor(ctxT_lo[:, g % 2, :, k * J:k * J + J], YH[:, 0:CC * J].rearrange("p (c j) -> p c j", c=CC),
                                          ctxT_hi[:, g % 2, :, k * J:k * J + J].bitcast(F32), ALU.subtract).then_inc(m["cTlo_ready"], 1)
                if q == 2:
                    if valid(b - 2):
                        need(dve, m["xThi_ready"], b - 1)
                        dve.tensor_tensor(xqT_lo[:, 1:S + 1], T1[:, 0:S], xqT_hi[:, 1:S + 1].bitcast(F32), ALU.subtract)\
                            .then_inc(m["xTlo_ready"], 1)
                    if valid(b - 4):
                        apart(dve, m["gate_done"], b - 3)
                        dve.max(best[:, :], T2[:, 0:E]).then_inc(m["c_gate"], 1)
                        apart(dve, m["c_gate"], 3 * (b - 4) + 1)
                        dve.max_index(best_at[:, :], best[:, :], T2[:, 0:E]).then_inc(m["gate_taken"], 1)
                        dve.tensor_copy(best_all[:, b - 4, :], best[:, 0:2]).then_inc(m["c_gate"], 1)
                        dve.wait_ge(m["gate_taken"], b - 3)
                        dve.tensor_copy(at_all[:, b - 4, :], best_at[:, 0:2]).then_inc(m["c_gate"], 1)
                        dve.wait_ge(m["c_gate"], 3 * (b - 4) + 3)
                        dve.tensor_tensor(chosen[:, :, :], expert_no[:, :].unsqueeze(1).broadcast_to([128, 2, E]),
                                          at_all[:, b - 4, :].unsqueeze(2).broadcast_to([128, 2, E]), ALU.is_equal)\
                            .then_inc(m["c_row"], 1)
                        dve.wait_ge(m["c_row"], 3 * (b - 4) + 1)
                        need(dve, m["pos_done"], b - 4)
                        dve.tensor_tensor(mask[:, :], chosen[:, 0, :], chosen[:, 1, :], ALU.add).then_inc(m["mask_ready"], 1)
                    if valid(b - 3):
                        need(dve, m["rs3"], b - 2)
                        need(dve, m["T3_done"], b - 3)
                        norm_by(h3[:, :], x_res[:, b - 3, :], mv3, r3).then_inc(m["h3_ready"], 1)
                        need(dve, m["L1_done"], b - 3)
                        dve.tensor_scalar(pick[:, :], plug_rows[:, b - 3, :], patch_no[:, :], None, ALU.is_equal)\
                            .then_inc(m["pick_ready"], 1)
                    if valid(b - 2):
                        need(dve, m["rsc"], b - 1)
                        need(dve, m["dep_done"], b - 2)
                        dve.scalar_tensor_tensor(hp[:, :], patch[:, k % 2, 0:D], rc[:, 0:1], g_init[:, :], ALU.mult, ALU.mult)\
                            .then_inc(m["hp_ready"], 1)
                if q == 3:
                    if valid(b - 4):
                        need(dve, m["pos_done"], b - 3)
                        dve.tensor_tensor(row_of[:, :], AV[:, 264:264 + E], first_row[:, :], ALU.add).then_inc(m["pos_taken"], 1)
                        dve.tensor_tensor(so_far[:, :], so_far[:, :], mask[:, :], ALU.add).then_inc(m["so_far_ready"], 1)
                        dve.wait_ge(m["pos_taken"], b - 3)
                        dve.tensor_tensor(row_pick[:, :, :], chosen[:, :, :], row_of[:, :].unsqueeze(1).broadcast_to([128, 2, E]),
                                          ALU.mult).then_inc(m["c_row"], 1)
                        dve.wait_ge(m["c_row"], 3 * (b - 4) + 2)
                        dve.tensor_reduce(row_all[:, b - 4, :], row_pick[:, :, :], AX.X, ALU.add).then_inc(m["c_row"], 1)
                        apart(dve, m["c_row"], 3 * (b - 4) + 3)
                        dve.tensor_copy(row_now[:, k % 2, :], row_all[:, b - 4, :]).then_inc(m["row_ready"], 1)
                    if valid(b - 3):
                        need(dve, m["L1_done"], b - 2)
                        dve.scalar_tensor_tensor(x_res[:, b - 3, :], T2[:, 0:D], gates[:, 1:2], x_res[:, b - 3, :],
                                                 ALU.mult, ALU.add).then_inc(m["x4_ready"], 1)
                        stats(b - 3, x_res[:, b - 3, :], raw4, mv4, (raw_sem[4], m["st4"]), m["x4_ready"])
                    if valid(b - 2):
                        need(dve, m["dep_done"], b - 1)
                        need(dve, m["L1_done"], b - 2)
                        dve.tensor_tensor(dep[:, :], T1[0:J, 0:D], b_in[:, :], ALU.add).then_inc(m["dep_ready"], 1)
                        need(dve, m["tanh_ready"], b - 1)
                        need(dve, m["q_ready"], b - 2)
                        step = chain(dve, m["c_conv"], 5 * (b - 2))
                        step(dve.scalar_tensor_tensor(act2, tanh_c, 1.0, conv, ALU.add, ALU.mult))
                        step(dve.tensor_reduce(qs3[:, 0:1], act2, AX.X, ALU.max, apply_absolute_value=True))
                        step(dve.tensor_scalar(qs3[:, 1:2], qs3[:, 0:1], 2 * QUANT_FLOOR, 1.0 / 127.0, ALU.max, ALU.mult))
                        step(dve.reciprocal(qs3[:, 2:3], qs3[:, 1:2]))
                        dve.tensor_scalar(z3, act2, qs3[:, 2:3], MAGIC, ALU.mult, ALU.add).then_inc(m["z_ready"], 1)
                        dve.tensor_scalar(back3[:, k % 2:k % 2 + 1], qs3[:, 1:2], w2_gain[:, :], None, ALU.mult)\
                            .then_inc(m["c_conv"], 1)

            program(dve, slot)

            n = [0]

            def row(ins):
                n[0] += 1
                ins.then_inc(m["c_moe"], 1)
                dve.wait_ge(m["c_moe"], n[0])

            row(dve.tensor_tensor(gp[:, 0, :], best_all[:, :, 1], best_all[:, :, 0], ALU.subtract))
            count, up, tiles, ends = (n_rows[:, i, :] for i in range(4))

            dve.wait_ge(m["n_done"], 1)
            row(dve.tensor_copy(count, AV[:, 264:264 + E]))
            dve.tensor_tensor(pad_row[:, :], n_rows[0:1, 0, :], first_row[0:1, :], ALU.add).then_inc(m["rows_known"], 1)
            row(dve.tensor_scalar(up, count, 1.0 / 128, 63.5 / 128, ALU.mult, ALU.add))
            row(dve.tensor_scalar(tiles, up, MAGIC, None, ALU.add))
            row(dve.tensor_scalar(tiles, tiles, -MAGIC, None, ALU.add))
            row(dve.tensor_tensor_scan(ends, tiles, zero_row[:, 0:E], 0.0, ALU.add, ALU.add))
            dve.wait_ge(m["q_ready"], B)
            dve.wait_ge(m["G_done"], 16 * NG)
            dve.wait_ge(m["V_done"], 4 * B)
            no_of = tile_no[:, :].unsqueeze(2).broadcast_to([1, TILES, E])
            row(dve.tensor_tensor(at_most, n_rows[0:1, 3, :].unsqueeze(1).broadcast_to([1, TILES, E]), no_of, ALU.is_le))
            row(dve.tensor_reduce(tile_f[:, 0, :], at_most, AX.X, ALU.add))
            row(dve.tensor_tensor(at_most_n, at_most, n_rows[0:1, 2, :].unsqueeze(1).broadcast_to([1, TILES, E]), ALU.mult))
            row(dve.tensor_reduce(tile_f[:, 1, :], at_most_n, AX.X, ALU.add))
            row(dve.tensor_tensor(tile_f[:, 2, :], tile_no[:, :], tile_f[:, 1, :], ALU.subtract))
            row(dve.tensor_scalar(tile_f[:, 3, :], tile_f[:, 0, :], float(CAP), None, ALU.mult))
            row(dve.scalar_tensor_tensor(tile_f[:, 4, :], tile_f[:, 2, :], 128.0, tile_f[:, 3, :], ALU.mult, ALU.add))
            row(dve.tensor_scalar(tile_at[:, 0, :], tile_f[:, 4, :], float(E * CAP), None, ALU.min))
            dve.tensor_scalar(tile_at[:, 1, :], tile_f[:, 0, :], float(E - 1), None, ALU.min).then_inc(m["tiles_known"], 1)
            dve.wait_ge(m["tiles_known"], 1)
            row(dve.tensor_tensor(n_rows[:, 4, :], ends, tiles, ALU.subtract))
            row(dve.scalar_tensor_tensor(n_rows[:, 5, :], n_rows[:, 4, :], 128.0, first_row[:, :], ALU.mult, ALU.subtract))
            row(dve.tensor_tensor(move, expert_no[:, :].unsqueeze(1).broadcast_to([128, 2 * B, E]),
                                  at_all[:, :, :].rearrange("p b k -> p (b k)").unsqueeze(2).broadcast_to([128, 2 * B, E]), ALU.is_equal))
            row(dve.tensor_tensor(move, move, n_rows[:, 5, :].unsqueeze(1).broadcast_to([128, 2 * B, E]), ALU.mult))
            row(dve.tensor_reduce(move_by[:, :], move, AX.X, ALU.add))
            all_rows = row_all[:, :, :].rearrange("p b k -> p (b k)")
            row(dve.tensor_tensor(all_rows, all_rows, move_by[:, :], ALU.add))
            dve.wait_ge(m["g_exp"], 1)
            row(dve.tensor_scalar(gp[:, 2, :], gp[:, 1, :], 1.0, None, ALU.add))
            row(dve.reciprocal(gp[:, 3, :], gp[:, 2, :]))
            row(dve.tensor_scalar(gp[:, 3, :], gp[:, 3, :], gates[:, 3:4], None, ALU.mult))
            row(dve.tensor_tensor(gp[:, 4, :], gp[:, 1, :], gp[:, 3, :], ALU.mult))
            dve.wait_ge(ld["moe"], 64)

            def tile(i, j, n=TILES):
                def expert(lag):
                    return dve.value_load(tile_at[0:1, 1, bass.ds(i - lag, 1)] if not isinstance(i, int)
                                          else tile_at[0:1, 1, i - lag:i - lag + 1], min_val=0, max_val=E - 1)

                if valid(i, n):
                    e = expert(0)
                    dve.wait_ge(m["h_out"], i + 1)
                    need(dve, m["hbT_out"], i - 1)
                    dve.tensor_tensor(hb[:, j % 2, :], bank[2 + j % 2][:, :], eb1[:, e, :], ALU.add).then_inc(m["hb_in"], 1)
                if valid(i - 2, n):
                    e = expert(2)
                    dve.wait_ge(m["y_out"], i - 1)
                    if not isinstance(i, int) or i >= 6:
                        dve.wait_ge(m[f"ye_st{(j + 2) % 4}"], 4 * (i - 2 - (j + 2) % 4) if isinstance(i, int) else 4 * (i - j) + (-16 + 16 * (j // 2)))
                    dve.tensor_tensor(ye[:, (j + 2) % 4, :], bank[6 + j % 2][:, 0:D], b2r[:, e, :], ALU.add).then_inc(m["ye_in"], 1)

            for j in range(8):
                tile(j, j)
            with dve.Fori(2, TILES // 4) as u:
                for j in range(4):
                    tile(4 * u + j, j)
            for j in range(2):
                tile(TILES + j, j)

            def index(t, i):
                dve.tensor_copy(row_idx[:, i, :].rearrange("p (b k) -> p b k", b=GB),
                                row_all[:, bass.ds(GB * t, GB), :] if not isinstance(t, int) else row_all[:, GB * t:GB * t + GB, :])\
                    .then_inc(m["idx_ready"], 1)

            def add(u, i, ahead):
                t = 2 * u + i
                dve.wait_ge(m[f"got{i}"], 16 * 2 * GB * (u + 1))
                for kk in range(2):
                    for jb in range(GB):
                        x_at = x_res[:, GB * t + jb, :]
                        dve.scalar_tensor_tensor(x_at, yg[:, i, jb, kk, :], gp[:, 3 + kk, bass.ds(GB * t + jb, 1)]
                                                 if not isinstance(t, int) else gp[:, 3 + kk, GB * t + jb:GB * t + jb + 1],
                                                 x_at, ALU.mult, ALU.add).then_inc(m["moe_sum"], 1)
                    dve.wait_ge(m["moe_sum"], 2 * GB * t + GB * (kk + 1))
                if ahead:
                    index(t + 2, i)

            index(0, 0)
            index(1, 1)
            with dve.Fori(0, NG // 2 - 1) as u:
                for i in range(2):
                    add(u, i, True)
            for i in range(2):
                add(NG // 2 - 1, i, False)


_INS = ["x", "ctx_2048", "mask_BxS2_if0", "g_xattn", "g_ffn", "L0_xattn_Wq", "L0_xattn_Wkv", "L0_xattn_null_kv",
        "L0_xattn_Wout", "L0_xattn_ln_scale", "L0_xattn_ln_bias", "L0_ffn_w1", "L0_ffn_conv_w", "L0_ffn_conv_b",
        "L0_ffn_w2", "L1_xattn_W_in", "L1_xattn_b_in", "L1_xattn_g_res", "L1_xattn_g_init", "L1_ffn_Wg", "L1_ffn_W1",
        "L1_ffn_b1", "L1_ffn_W2", "L1_ffn_b2"]


def kernel(**inputs):
    import concourse.bacc as bacc
    from concourse.bass_utils import run_bass_kernel_spmd

    nc = bacc.Bacc("TRN2", target_bir_lowering=False, num_devices=1)
    arrays, handles = {}, {}
    for name in _INS:
        arr = np.ascontiguousarray(inputs[name])
        arrays[name] = arr
        handles[name] = nc.dram_tensor(name, arr.shape, mybir.dt.from_np(arr.dtype), kind="ExternalInput").ap()
    out = nc.dram_tensor("out", arrays["x"].shape, F32, kind="ExternalOutput").ap()
    build(nc, handles, out)
    r = run_bass_kernel_spmd(nc, [arrays], core_ids=[0])
    return r.results[0]["out"]
```

```python
from contextlib import ExitStack

import numpy as np

import concourse.bass as bass
from concourse import mybir

F32 = mybir.dt.float32
F32R = mybir.dt.float32r
BF16 = mybir.dt.bfloat16
I32 = mybir.dt.int32
U32 = mybir.dt.uint32
ALU = mybir.AluOpType
ACT = mybir.ActivationFunctionType
AX = mybir.AxisListType

MAGIC = 1.5 * 2.0**23
LN_EPS = 1e-5
XATTN_EPS = 1e-6
QUANT_FLOOR = 1e-5
PATCH_CLIP = 65536.0


def need(eng, sem, count):
    if isinstance(count, int) and count <= 0:
        return
    eng.wait_ge(sem, count)


def chain(eng, sem, count):
    done = [0]

    def link(ins, wait=need):
        done[0] += 1
        ins.then_inc(sem, 1)
        wait(eng, sem, count + done[0])

    return link


def build(nc, a, out):
    B, S, D = a["x"].shape
    J, C = a["ctx_2048"].shape[1:]
    INNER = a["L0_xattn_Wq"].shape[1]
    DH = a["L0_xattn_null_kv"].shape[1]
    H = INNER // DH
    F = a["L0_ffn_w1"].shape[0]
    E = a["L1_ffn_Wg"].shape[1]
    FF = a["L1_ffn_W1"].shape[2]
    assert S == 128 and D == 128 and C == 256 and DH == 64 and B % 4 == 0
    GB = 4
    NG = B // GB
    QH = H // 4
    JN = J + 1
    CC = C // 128
    FC = F // 128
    FFC = FF // 128
    SCALE = DH**-0.5
    CAP = B * S + 128
    TILES = 2 * B * S // 128 + E
    PADS = 2 * E
    DX = D + 1
    POWERS = 12
    CT_LAST = 4 * (NG - 2) + 3 + 8 + 1

    logp = np.float32(-0.001)
    dt = np.float32(-np.log(-np.expm1(logp)))
    decay = float(np.exp(-dt))
    gain = float(np.exp(logp))

    ctx = ExitStack()
    with ctx:
        def sb(name, shape, dtype=F32):
            return ctx.enter_context(nc.sbuf_tensor(name, shape, dtype))

        def sem(name):
            return ctx.enter_context(nc.semaphore(name))

        x_res = sb("x_res", [128, B, D])
        G = sb("G", [128, 2, GB, H, JN])
        wv_lo = sb("wv_lo", [128, CC, INNER], F32R)
        ctxT_hi = sb("ctxT_hi", [128, 2, CC, GB * J], F32R)
        ctxT_lo = sb("ctxT_lo", [128, 2, CC, GB * J], F32R)
        ctxv_hi = sb("ctxv_hi", [128, 2, CC, J], F32R)
        ctxv_lo = sb("ctxv_lo", [128, 2, CC, J], F32R)
        tap_hi = sb("tap_hi", [128, 3, F], F32R)
        tap_lo = sb("tap_lo", [128, 3, F], F32R)
        w_out = sb("w_out", [128, INNER // 128, D])
        w2q = sb("w2q", [128, FC, D], BF16)
        w_inT = sb("w_inT", [128, D])
        w_gate = sb("w_gate", [128, E])
        plug_rows = sb("plug_rows", [J, B, S], BF16)
        before = sb("before", [128, 128], BF16)
        ones_bf = sb("ones_bf", [128, 128], BF16)
        ident = sb("ident", [128, 128])
        ident_bf = sb("ident_bf", [128, 128], BF16)
        ones = sb("ones", [128, 128])
        scanT = sb("scanT", [J, J])
        patch_no = sb("patch_no", [J, 1])
        conv_b = sb("conv_b", [128, F])
        ln_gain = sb("ln_gain", [128, D])
        ln_shift = sb("ln_shift", [128, D])
        b_in = sb("b_in", [J, D])
        g_init = sb("g_init", [J, D])
        g_res = sb("g_res", [128, 1])
        gates = sb("gates", [128, 4])
        w2_gain = sb("w2_gain", [128, 1])
        wsum = sb("wsum", [128, 2])
        wmean = sb("wmean", [128, 2])
        winv = sb("winv", [128, 2])
        half = sb("half", [128, 1])
        tap_gain = sb("tap_gain", [128, FC, 3])
        nullk = sb("nullk", [128, 2])
        gnull = sb("gnull", [128, H])
        expert_no = sb("expert_no", [128, E])
        gp = sb("gp", [128, 5, B])

        rows = sb("rows", [J, 2, C])
        patch = sb("patch", [J, 2, C])
        h1 = sb("h1", [128, D])
        hT = sb("hT", [128, 2, S])
        top = sb("top", [128, 2, QH])
        shifted = sb("shifted", [128, 2, QH, JN])
        probs = sb("probs", [128, 2, QH, JN])
        probsT = sb("probsT", [JN, 2, QH, S])
        V = sb("V", [JN, 2, H, DH + 1])
        rden = sb("rden", [128, 2, QH])
        attn = sb("attn", [128, 2, QH * DH])
        attnT = sb("attnT", [128, 2, INNER // 128, S])
        xb = sb("xb", [128, D])
        y1 = sb("y1", [128, D])
        y2 = sb("y2", [128, D])
        h2 = sb("h2", [128, D])
        z2 = sb("z2", [128, D])
        xq = sb("xq", [128, D])
        xqT_hi = sb("xqT_hi", [128, S + 2], F32R)
        xqT_lo = sb("xqT_lo", [128, S + 2], F32R)
        ffn = sb("ffn", [128, 4, F])
        conv, tanh_c, act2, z3 = (ffn[:, i, :] for i in range(4))
        q3 = sb("q3", [128, F], BF16)
        q3T = sb("q3T", [128, FC, S], BF16)
        h3 = sb("h3", [128, D])
        h3T = sb("h3T", [128, S])
        hp = sb("hp", [J, D])
        dep = sb("dep", [J, D])
        pick = sb("pick", [J, S])
        xs = sb("xs", [128, 2, 2, DX])
        result_row = sb("result_row", [128, B, 2])
        xsT = sb("xsT", [128, S])
        raw1, raw2, raw3, raw4, rawy = (sb(f"raw_{n}", [128, 6]) for n in ("x", "x2", "x3", "x4", "y"))
        mv1, mv2, mv3, mv4, mvy = (sb(f"mv_{n}", [128, 2]) for n in ("x", "x2", "x3", "x4", "y"))
        var1, var2, var3, var4, vary = (sb(f"var_{n}", [128, 1]) for n in ("x", "x2", "x3", "x4", "y"))
        r1, r2, r3, r4, ry = (sb(f"rstd_{n}", [128, 1]) for n in ("x", "x2", "x3", "x4", "y"))
        ratio3 = sb("ratio3", [128, 3])
        rawc = sb("raw_c", [J, 6])
        mvc = sb("mv_c", [J, 2])
        msc = sb("ms_c", [J, 2])
        rc = sb("rstd_c", [J, 1])
        qs2 = sb("qs2", [128, 3])
        qs3 = sb("qs3", [128, 3])
        back3 = sb("back3", [128, 2])
        best = sb("best", [128, 8])
        best_at = sb("best_at", [128, 8], U32)
        chosen = sb("chosen", [128, 2, E])
        mask = sb("mask", [128, E], BF16)
        so_far = sb("so_far", [128, E], BF16)
        first_row = sb("first_row", [128, E])
        row_of = sb("row_of", [128, E])
        row_pick = sb("row_pick", [128, 2, E])
        row_now = sb("row_now", [128, 2, 2], U32)
        row_f = sb("row_f", [128, 2])
        row_out = sb("row_out", [128, 4, 1], U32)
        pad_row = sb("pad_row", [1, E], I32)
        tile_no = sb("tile_no", [1, TILES])
        tile_at = sb("tile_at", [1, 2, TILES], I32)
        n_rows = sb("n_rows", [1, 4, E])
        best_all = sb("best_all", [128, B, 2])
        at_all = sb("at_all", [128, B, 2])

        flat = G[:, :, :, :, :].rearrange("p a b h j -> p (a b h j)")
        taken = [0]

        def part(n):
            taken[0] += n
            assert taken[0] <= 2 * GB * H * JN
            return flat[:, taken[0] - n:taken[0]]

        wq = part(INNER)
        wk = part(CC * INNER).rearrange("p (c n) -> p c n", c=CC)
        wqT = part(INNER).rearrange("p (h d) -> p h d", d=D)
        wkT = part(CC * INNER).rearrange("p (h c) -> p h c", c=C)
        w1 = part(FC * D).rearrange("p (c d) -> p c d", c=FC)
        w2 = part(F)
        wtap = part(FC * 3 * D).rearrange("p (c t d) -> p c t d", c=FC, t=3)
        w_in = part(D)
        w2t = part(F // 2).bitcast(BF16)
        eW1 = flat[:, 0:E * (FF + FFC)].rearrange("p (e f) -> p e f", e=E)
        b2r = flat[:, E * (2 * FF + FFC):E * (2 * FF + FFC + D)].rearrange("p (e d) -> p e d", e=E)
        eW2 = flat[:, E * (FF + FFC):E * (2 * FF + FFC)].rearrange("p (e c d) -> p e c d", e=E, c=FFC)
        wv = ffn[:, :, :].rearrange("p (c a) n -> p c (a n)", c=CC)
        eq = attnT[:, :, :, :].rearrange("p a c s -> p (a c s)")[:, 0:16 * J].bitcast(BF16).rearrange(
            "p (t j) -> p t j", t=32)
        at_most = ffn[0:1, :, :].rearrange("p a n -> p (a n)")[:, 0:TILES * E].rearrange("p (t e) -> p t e", e=E)
        at_most_n = ffn[0:1, :, :].rearrange("p a n -> p (a n)")[:, TILES * E:2 * TILES * E].rearrange("p (t e) -> p t e", e=E)
        tile_f = ffn[0:1, :, :].rearrange("p a n -> p (a n)")[:, 2 * TILES * E:2 * TILES * E + 6 * TILES].rearrange("p (i t) -> p i t", i=6)
        len_i = sb("len_i", [128, J], I32)
        len_f = sb("len_f", [128, J])
        len_sum = sb("len_sum", [128, J])
        len_wrap = sb("len_wrap", [128, J])
        token_no = sb("token_no", [128, 32])
        edge = sb("edge", [128, 32])
        edges = sb("edges", [B, S])
        edge_sum = sb("edge_sum", [B, S])
        zero_row = sb("zero_row", [128, 128])
        plug = sb("plug", [B, S], BF16)

        with ExitStack() as first:
            def weights(name, shape):
                return first.enter_context(nc.sbuf_tensor(name, shape, F32R))

            A_hi = weights("A_hi", [128, CC, H, D])
            A_lo = weights("A_lo", [128, CC, H, D])
            wv_hi = weights("wv_hi", [128, CC, INNER])
        w1_now = sb("w1_now", [128, 4, FF + FFC])
        xt = sb("xt", [128, 4, DX])
        xtT = sb("xtT", [128, 2, 128])
        w2_now = sb("w2_now", [128, 2, FFC, D])
        hbT = sb("hbT", [128, 4, FFC, 128])
        ye = sb("ye", [128, 4, D])
        pads = sb("pads", [128, PADS, DX])
        yg = pads[:, :, :].rearrange("p t d -> p (t d)")[:, 0:4 * GB * D].rearrange("p (i b k d) -> p i b k d", i=2, b=GB, k=2)

        bank = [ctx.enter_context(nc.psum_tensor(f"bank{i}", [128, 512], F32)) for i in range(8)]
        SC, PT, AV, YH, GC, VO, T1, T2 = bank

        edge_d = nc.dram_tensor("edge_d", (B, S), F32, kind="Internal").ap()
        xe_d = nc.dram_tensor("xe_d", (E * CAP + 128 * E, DX), F32, kind="Internal").ap()
        ye_d = nc.dram_tensor("ye_d", (2 * B * S + 128 * PADS, D), F32, kind="Internal").ap()
        plug_d = nc.dram_tensor("plug_d", (B, S), BF16, kind="Internal").ap()

        ld_names = ["wq", "wk", "x0", "x1", "wv", "wout", "len", "small", "row", "edge", "plug_st", "plug", "moe"]
        ld = {n: sem(f"loaded_{n}") for n in ld_names}
        ld_rows = [sem(f"loaded_rows{i}") for i in range(2)]
        ld_patch = [sem(f"loaded_patch{i}") for i in range(2)]
        prep_pe = sem("prep_pe")
        prep_act = sem("prep_act")
        prep_dve = sem("prep_dve")
        prep_pool = sem("prep_pool")
        prep_chain = sem("prep_chain")
        prep_split = sem("prep_split")
        edge_ready = sem("edge_ready")
        plug_ready = sem("plug_ready")
        wsum_ready = sem("wsum_ready")
        wtap_ready = sem("wtap_ready")
        w2t_ready = sem("w2t_ready")
        gates_ready = sem("gates_ready")
        shift_ready = sem("shift_ready")
        main_ready = sem("main_ready")
        names = """s_done pT_done av_done oT_done G_done V_done xT_done conv_done qT_done w2_done hT_done
            T3_done L1_done T4_done gate_done dep_done cT_done y_done
            exp_ready oT_ready pT_ready G_ready xThi_ready T3_ready cThi_ready hT_ready tanh_ready qT_ready xsT_ready
            norm_ready sub_ready V_ready h1_ready h3_ready xTlo_ready cTlo_ready pick_ready conv_ready z_ready
            xq_ready x3_ready x4_ready xs_ready hp_ready dep_ready gate_taken y_taken x2_ready
            st1 st2 st3 st4 sty stc rs1 rs2 rs3 rs4 rsy rsc q_ready xb_ready cv_ready
            c_soft c_norm c_y c_h2 c_conv c_gate c_pool1 c_pool2 c_pool3 c_pool4 c_pooly c_poolc
            g_exp stored c_moe moe_sum mask_ready pos_done pos_taken row_ready so_far_ready c_row
            scattered0 scattered1 n_done rows_known tiles_known padded xt_in0 xt_in1 xt_in2 xt_in3 xT_out xT_in
            h_out w1_in w2_in hbT_in y_out ye_in ye_st0 ye_st1 ye_st2 ye_st3 pads_ready id_ready out_id got0 got1""".split()
        m = {n: sem(n) for n in names}

        raw_sem = [sem(f"raw_{n}") for n in ("y", "x", "x2", "x3", "x4", "c")]

        def valid(b, n=B):
            return not isinstance(b, int) or 0 <= b < n

        def apart(eng, sem, count):
            if isinstance(count, int) and count <= 0:
                return
            if not isinstance(count, int):
                at = counts[eng.engine]
                eng.reg_mov(at, count)
                count = at
            eng.wait_ge(main_ready, 1)
            eng.wait_ge(sem, count)

        def pad_experts(eng, experts):
            eng.wait_ge(m["rows_known"], 1)
            for e in experts:
                at = eng.value_load(pad_row[0:1, e:e + 1], min_val=0, max_val=E * CAP - 128)
                eng.dma_start(xe_d[bass.ds(at, 128), :], pads[:, e, :]).then_inc(m["padded"], 16)

        def expert(eng, i, j):
            at = tile_at[0:1, 1, i:i + 1] if isinstance(i, int) else tile_at[0:1, 1, bass.ds(i, 1)]
            e = eng.value_load(at, min_val=0, max_val=E - 1)
            eng.reg_mov(experts[eng.engine][j % 4], e)
            return e

        def expert_before(eng, j, lag):
            return eng.snap(experts[eng.engine][(j - lag) % 4], min_val=0, max_val=E - 1)

        def G_banks(g):
            return (GC, SC, PT, AV) if isinstance(g, int) and g < 0 else (GC,)

        def upto(n, last):
            return min(n, last) if isinstance(n, int) else n

        def back(b, q, k, d):
            return b + (q - d) // 4, (q - d) % 4, (k + (q - d) // 4) % 4

        def program(eng, slot):
            def group(g):
                for j in range(16):
                    slot(g, j // 4, j % 4, 4 * g + j // 4, 16 * g + j)

            for g in (-2, -1, 0, 1):
                group(g)
            with eng.Fori(2, NG - 1) as g:
                group(g)
            for g in (NG - 1, NG):
                group(g)

        counts = {e.engine: e.alloc_register(f"count_{i}") for i, e in enumerate((nc.vector, nc.gpsimd))}
        experts = {e.engine: [e.alloc_register(f"expert_{i}_{j}") for j in range(4)]
                   for i, e in enumerate((nc.vector,))}
        block = ctx.enter_context(nc.Block())

        SMALL = 17
        LEN_LOADS = 4
        NULL_LOADS = 4

        @block.sync
        def _(sp):
            kv = a["L0_xattn_Wkv"].rearrange("(c p) n -> p c n", p=128)
            sp.dma_start(rows[:, 0, :], a["ctx_2048"][0]).then_inc(ld_rows[0], 16)
            sp.dma_start(wq, a["L0_xattn_Wq"]).then_inc(ld["wq"], 16)
            sp.dma_start(wk, kv[:, :, 0:INNER]).then_inc(ld["wk"], 16)
            sp.dma_start(wv, kv[:, :, INNER:2 * INNER]).then_inc(ld["wv"], 16)
            nk = a["L0_xattn_null_kv"]
            sp.wait_ge(prep_pool, 2)
            for i in range(2):
                sp.dma_start(nullk[64 * i:64 * i + 64, i:i + 1], nk[0:1, :].rearrange("o d -> d o")).then_inc(ld["small"], 16)
                sp.dma_start(V[J:JN, i, :, 0:DH], nk[1:2, :].unsqueeze(1).broadcast_to([1, H, DH])).then_inc(ld["small"], 16)
            n = NULL_LOADS + 2
            for dst, src in (
                (tap_gain[:, :, :], a["L0_ffn_conv_w"].rearrange("(c p) o t -> p c (o t)", p=128)),
                (gates[:, 0:2], a["g_xattn"].partition_broadcast(128)),
                (gates[:, 2:4], a["g_ffn"].partition_broadcast(128)),
                (w_in, a["L1_xattn_W_in"]),
                (g_res[:, :], a["L1_xattn_g_res"].rearrange("(p o) -> p o", o=1)),
                (ln_gain[:, :], a["L0_xattn_ln_scale"].partition_broadcast(128)),
                (ln_shift[:, :], a["L0_xattn_ln_bias"].partition_broadcast(128)),
                (w_gate[:, :], a["L1_ffn_Wg"]),
                (conv_b[:, :], a["L0_ffn_conv_b"].partition_broadcast(128)),
                (b_in[:, :], a["L1_xattn_b_in"].partition_broadcast(J)),
                (g_init[:, :], a["L1_xattn_g_init"][0:D].partition_broadcast(J)),
            ):
                sp.dma_start(dst, src).then_inc(ld["small"], 16)
                n += 1
            assert n == SMALL
            sp.dma_start(x_res[:, 0:8, :], a["x"][0:8].rearrange("b s d -> s b d")).then_inc(ld["x0"], 16)
            sp.dma_start(w_out[:, :, :], a["L0_xattn_Wout"].rearrange("(c p) n -> p c n", p=128)).then_inc(ld["wout"], 16)
            sp.dma_start(x_res[:, 8:B, :], a["x"][8:B].rearrange("b s d -> s b d")).then_inc(ld["x1"], 16)

            def collect_edges():
                sp.wait_ge(edge_ready, 1)
                for i in range(4):
                    sp.dma_start(edge_d[:, 32 * i:32 * i + 32], edge[B * i:B * i + B, :]).then_inc(ld["edge"], 16)
                sp.wait_ge(ld["edge"], 64)
                sp.dma_start(edges[:, :], edge_d).then_inc(ld["row"], 16)

            def spread_patches():
                sp.wait_ge(plug_ready, 1)
                sp.dma_start(plug_d, plug[:, :]).then_inc(ld["plug_st"], 16)
                sp.wait_ge(ld["plug_st"], 16)
                sp.dma_start(plug_rows[:, :, :], plug_d.partition_broadcast(J)).then_inc(ld["plug"], 16)

            def slot(g, k, q, b, s):
                if isinstance(b, int) and q == 1:
                    if b == -3:
                        collect_edges()
                    if b == -1:
                        spread_patches()
                if q == 0:
                    if not isinstance(b, int) or 0 <= b + 9 < CT_LAST:
                        need(sp, m["cT_done"], b + 8)
                        sp.dma_start(rows[:, (k + 1) % 2, :], a["ctx_2048"][(b + 9) % B]).then_inc(ld_rows[(k + 1) % 2], 16)
                    if valid(b - 1):
                        need(sp, m["hp_ready"], b - 2)
                        sp.dma_start(patch[:, (k + 1) % 2, :], a["ctx_2048"][b - 1]).then_inc(ld_patch[(k + 1) % 2], 16)

            program(sp, slot)
            for i in range(2):
                sp.wait_ge(ld_rows[i], 16 * ((CT_LAST + 2 - i) // 2))
            sp.wait_ge(m["s_done"], 4 * B)
            sp.dma_start(eW1[:, :, 0:FF], a["L1_ffn_W1"].rearrange("e p f -> p e f")).then_inc(ld["moe"], 16)
            sp.dma_start(eW2, a["L1_ffn_W2"].rearrange("e (c p) d -> p e c d", p=128)).then_inc(ld["moe"], 16)
            sp.dma_start(b2r, a["L1_ffn_b2"].partition_broadcast(128)).then_inc(ld["moe"], 16)
            for e in range(E):
                sp.dma_start(eW1[:, e, FF:FF + FFC], a["L1_ffn_b1"][e].rearrange("(c p) -> p c", p=128),
                             allow_slow_non_contiguous=True).then_inc(ld["moe"], 16)
            sp.wait_ge(m["pads_ready"], 2)
            sp.dma_start(xe_d[E * CAP:E * CAP + 128 * E, :].rearrange("(t p) d -> p t d", p=128), pads[:, E:PADS, :])\
                .then_inc(m["padded"], 16)
            pad_experts(sp, range(0, E // 2))
            for i in range(2):
                sp.wait_ge(m[f"scattered{i}"], 16 * B)
            sp.wait_ge(m["tiles_known"], 1)
            sp.wait_ge(m["padded"], 16 * (E + 1))

            def load_tile(u, j):
                at = sp.value_load(tile_at[0:1, 0, bass.ds(4 * u + j, 1)], min_val=0, max_val=E * CAP + 128 * (E - 1))
                need(sp, m["xT_out"], 4 * u - 3 + j)
                need(sp, m["out_id"], 4 * u - 3 + j)
                sp.dma_start(xt[:, j, :], xe_d[bass.ds(at, 128), :]).then_inc(m[f"xt_in{j}"], 16)

            for j in range(4):
                load_tile(0, j)
            with sp.Fori(1, TILES // 4) as u:
                for j in range(4):
                    load_tile(u, j)

            out_v = out.rearrange("(t b) s d -> t s b d", b=GB)
            with sp.Fori(0, NG) as t:
                sp.wait_ge(m["moe_sum"], 2 * GB * (t + 1))
                sp.dma_start(out_v[t], x_res[:, bass.ds(GB * t, GB), :]).then_inc(m["stored"], 16)
            sp.wait_ge(m["stored"], 16 * NG)

        @block.gpsimd
        def _(pool):
            pool.memset(nullk[:, :], 0.0).then_inc(prep_pool, 1)
            pool.memset(V[:, :, :, :], 1.0).then_inc(prep_pool, 1)
            pool.memset(ident[:, :], 0.0).then_inc(prep_pool, 1)
            pool.memset(ones[:, :], 1.0).then_inc(prep_pool, 1)
            pool.memset(half[:, :], -0.5).then_inc(prep_pool, 1)
            pool.memset(xqT_hi[:, :].bitcast(F32), 0.0).then_inc(prep_pool, 1)
            pool.memset(xqT_lo[:, :].bitcast(F32), 0.0).then_inc(prep_pool, 1)
            pool.memset(scanT[:, :], 0.0).then_inc(prep_pool, 1)
            pool.memset(zero_row[:, :], 0.0).then_inc(prep_pool, 1)
            pool.wait_ge(prep_pool, 9)
            step = chain(pool, prep_pool, 9)
            step(pool.affine_select(out=ident[:, :], in_=ident[:, :], compare_op=ALU.not_equal, fill=1.0, base=0,
                                    pattern=[[-1, 128]], channel_multiplier=1))
            for i in range(4):
                step(pool.iota(token_no[32 * i:32 * i + 32, :], pattern=[[1, 32]], base=32 * i, channel_multiplier=0,
                               allow_small_or_imprecise_dtypes=True))
            step(pool.iota(patch_no[:, :], pattern=[[0, 1]], base=1, channel_multiplier=1,
                           allow_small_or_imprecise_dtypes=True))
            step(pool.iota(expert_no[:, :], pattern=[[1, E]], base=0, channel_multiplier=0,
                           allow_small_or_imprecise_dtypes=True))
            step(pool.tensor_copy(ident_bf[:, :], ident[:, :]))
            k = 0
            while k < POWERS:
                step(pool.affine_select(out=scanT[:, :], in_=scanT[:, :], compare_op=ALU.not_equal,
                                        fill=gain * decay**k, base=k, pattern=[[-1, J]], channel_multiplier=1))
                k += 1
            step(pool.memset(so_far[:, :], 0.0))
            step(pool.memset(ones_bf[:, :], 1.0))
            step(pool.affine_select(out=before[:, :], in_=ones_bf[:, :], compare_op=ALU.is_ge, fill=0.0, base=-1,
                                    pattern=[[1, 128]], channel_multiplier=-1))
            step(pool.iota(first_row[:, :], pattern=[[CAP, E]], base=0, channel_multiplier=0,
                           allow_small_or_imprecise_dtypes=True))
            step(pool.iota(result_row[:, :, :], pattern=[[2 * S, B], [1, 2]], base=0, channel_multiplier=2,
                           allow_small_or_imprecise_dtypes=True))
            step(pool.iota(tile_no[:, :], pattern=[[1, TILES]], base=0, channel_multiplier=0,
                           allow_small_or_imprecise_dtypes=True))

            def rstd(b, var, root, ready, sem_c, src, eps, stat):
                apart(pool, stat, b + 1)
                step = chain(pool, sem_c, b)
                step(pool.tensor_scalar(var[:, :], src, eps, None, ALU.add))
                pool.tensor_tensor(root[:, :], var[:, :], half[0:root.shape[0], :], ALU.pow).then_inc(ready, 1)

            def slot(g, k, q, b, s):
                if isinstance(b, int) and b == B + 1 and q == 0:
                    pool.wait_ge(m["V_done"], 4 * B)
                    pool.wait_ge(m["G_done"], 16 * NG)
                    pool.memset(pads[:, :, :], 0.0).then_inc(m["pads_ready"], 1)
                    pool.wait_ge(m["pads_ready"], 1)
                    pool.iota(pads[:, :, D], pattern=[[128, PADS]], base=2 * B * S, channel_multiplier=1,
                              allow_small_or_imprecise_dtypes=True).then_inc(m["pads_ready"], 1)
                if q == 0:
                    if valid(b - 2):
                        rstd(b - 2, vary, ry, m["rsy"], m["c_pooly"], mvy[:, 1:2], XATTN_EPS, m["sty"])
                    if valid(b + 1):
                        rstd(b + 1, var1, r1, m["rs1"], m["c_pool1"], mv1[:, 1:2], LN_EPS, m["st1"])
                if q == 1:
                    if valid(b - 2):
                        rstd(b - 2, var2, r2, m["rs2"], m["c_pool2"], mv2[:, 1:2], LN_EPS, m["st2"])
                    if valid(b - 1):
                        need(pool, m["x2_ready"], b - 1)
                        pool.tensor_tensor(xb[:, :], x_res[:, b - 1, :], ln_shift[:, :], ALU.add)\
                            .then_inc(m["xb_ready"], 1)
                    if valid(b + 2):
                        grp = g + (k + 2) // 4
                        kk = (k + 2) % 4
                        need(pool, m["cThi_ready"], b + 3)
                        need(pool, m["cTlo_ready"], b + 3)
                        need(pool, m["V_done"], 4 * (b + 1))
                        for to, of in ((ctxv_hi, ctxT_hi), (ctxv_lo, ctxT_lo)):
                            pool.tensor_copy(to[:, k % 2, :, :], of[:, grp % 2, :, kk * J:kk * J + J].bitcast(F32))\
                                .then_inc(m["cv_ready"], 1)
                if q == 2:
                    if valid(b - 3):
                        apart(pool, m["st3"], b - 2)
                        step = chain(pool, m["c_pool3"], 5 * (b - 3))
                        step(pool.tensor_scalar(var3[:, :], mv3[:, 1:2], LN_EPS, None, ALU.add))
                        step(pool.tensor_tensor(ratio3[:, 0:1], var3[:, :], half[:, :], ALU.pow))
                        step(pool.tensor_tensor(ratio3[:, 1:2], ratio3[:, 0:1], ratio3[:, 0:1], ALU.mult), apart)
                        step(pool.tensor_scalar(ratio3[:, 2:3], ratio3[:, 1:2], mv3[:, 1:2], LN_EPS, ALU.mult, ALU.add))
                        step(pool.tensor_tensor(var3[:, :], ratio3[:, 2:3], half[:, :], ALU.pow))
                        pool.tensor_tensor(r3[:, :], var3[:, :], ratio3[:, 0:1], ALU.mult).then_inc(m["rs3"], 1)
                if q == 3:
                    if valid(b - 3):
                        rstd(b - 3, var4, r4, m["rs4"], m["c_pool4"], mv4[:, 1:2], LN_EPS, m["st4"])
                    if valid(b - 1):
                        need(pool, m["stc"], b)
                        step = chain(pool, m["c_poolc"], 3 * (b - 1))
                        step(pool.tensor_tensor(msc[:, 0:1], mvc[:, 0:1], mvc[:, 0:1], ALU.mult))
                        step(pool.tensor_tensor(msc[:, 1:2], msc[:, 0:1], mvc[:, 1:2], ALU.add), apart)
                        step(pool.tensor_scalar(msc[:, 0:1], msc[:, 1:2], LN_EPS, None, ALU.add))
                        pool.tensor_tensor(rc[:, :], msc[:, 0:1], half[0:J, :], ALU.pow).then_inc(m["rsc"], 1)
                if q == 3 and valid(b - 4):
                    apart(pool, m["id_ready"], b - 3)
                    apart(pool, m["row_ready"], b - 3)
                    for i in range(2):
                        pool.indirect_dma_start(xe_d, bass.IndirectOffsetOnAxis(ap=row_now[:, k % 2, i:i + 1], axis=0),
                                                xs[:, k % 2, i, :], None).then_inc(m[f"scattered{k % 2}"], 16)

            pool.wait_ge(ld["x0"], 16)
            pool.wait_ge(ld["x1"], 16)
            pool.wait_ge(shift_ready, 1)
            program(pool, slot)

            def put(u, j):
                i = 4 * u + j
                apart(pool, m["ye_in"], i + 1)
                apart(pool, m["out_id"], i + 1)
                pool.indirect_dma_start(ye_d, bass.IndirectOffsetOnAxis(ap=row_out[:, j, :], axis=0), ye[:, j, :], None)\
                    .then_inc(m[f"ye_st{j}"], 16)

            for j in range(4):
                put(0, j)
            with pool.Fori(1, TILES // 4) as u:
                for j in range(4):
                    put(u, j)
            for j in range(4):
                pool.wait_ge(m[f"ye_st{j}"], 16 * (TILES // 4))

        JOBS = 21
        A_JOBS = range(6, 14)
        TAP_JOBS = range(17, 20)

        def a_job(n):
            r = (n - 6) % 4
            return (n - 6) // 4, 8 * (r // 2) + r % 2

        def low_parts(n):
            return sum(j in A_JOBS or j in TAP_JOBS for j in range(n))

        @block.tensor
        def _(pe):
            for n in range(JOBS):
                b8 = bank[n % 8]
                need(pe, prep_act, n - 7)
                need(pe, prep_dve, low_parts(max(n - 7, 0)))
                if n < 2:
                    if n == 0:
                        pe.wait_ge(prep_pool, 17)
                        pe.wait_ge(ld["wq"], 16)
                    for i in range(4):
                        mm = pe.transpose(b8[:, 128 * i:128 * i + 128], wq[:, 128 * (4 * n + i):128 * (4 * n + i) + 128], ident[:, :])
                elif n < 6:
                    if n == 2:
                        pe.wait_ge(ld["wk"], 16)
                    for i in range(4):
                        h2_, c = 2 * (n - 2) + i // 2, i % 2
                        mm = pe.transpose(b8[:, 128 * i:128 * i + 128], wk[:, c, 128 * h2_:128 * h2_ + 128], ident[:, :])
                elif n < 14:
                    if n == 6:
                        pe.wait_ge(prep_act, 6)
                    c, h0 = a_job(n)
                    r = 64 * (h0 % 2)
                    for i in range(4):
                        h = h0 + 2 * i
                        mm = pe.matmul(b8[:, 128 * i:128 * i + 128], wkT[r:r + 64, h // 2, 128 * c:128 * c + 128],
                                       wqT[r:r + 64, h // 2, :], start=True, stop=True)
                elif n == 14:
                    pe.wait_ge(ld["small"], 16 * SMALL)
                    for i in range(H // 2):
                        mm = pe.matmul(b8[:, 2 * i:2 * i + 2], wqT[:, i, :], nullk[:, :], start=True, stop=True)
                elif n == 15:
                    pe.wait_ge(wsum_ready, 2)
                    mm = pe.matmul(b8[:, 0:2], ones[:, :], wsum[:, :], start=True, stop=True)
                elif n == 16:
                    mm = pe.transpose(b8[:, 0:128], w_in, ident[:, :])
                elif n < 20:
                    if n == 17:
                        pe.wait_ge(wtap_ready, 3 * FC)
                    for i in range(FC):
                        mm = pe.transpose(b8[:, 128 * i:128 * i + 128], wtap[:, i, n - 17, :], ident[:, :])
                else:
                    pe.wait_ge(w2t_ready, 1)
                    for i in range(FC):
                        mm = pe.transpose(b8[:, 64 * i:64 * i + 64].bitcast(BF16), w2t[:, 128 * i:128 * i + 128], ident_bf[:, :])
                mm.then_inc(prep_pe, 1)
            pe.wait_ge(prep_act, JOBS)
            pe.wait_ge(prep_dve, low_parts(JOBS))
            pe.wait_ge(ld["wout"], 16)
            pe.wait_ge(prep_split, 2)
            pe.wait_ge(main_ready, 1)
            pe.wait_ge(prep_pool, 17 + POWERS + 6)

            def split3(o, w_hi, w_lo, x_hi, x_lo, first, last):
                pe.matmul(o, w_lo, x_hi, start=first, stop=False)
                pe.matmul(o, w_hi, x_lo, start=False, stop=False)
                return pe.matmul(o, w_hi, x_hi, start=False, stop=last)

            def slot(g, k, q, b, s):
                if q == 3 and valid(b - 4):
                    need(pe, m["mask_ready"], b - 3)
                    need(pe, m["so_far_ready"], b - 4)
                    need(pe, m["norm_ready"], upto(s - 2, 4 * B))
                    pe.matmul(AV[:, 264:264 + E], before[:, :], mask[:, :], start=True, stop=False)
                    pe.matmul(AV[:, 264:264 + E], ones_bf[:, :], so_far[:, :], start=False, stop=True).then_inc(m["pos_done"], 1)
                if valid(s - 2, 4 * B):
                    t = s - 2
                    if q == 0 and valid(b - 5):
                        need(pe, m["pos_taken"], b - 4)
                    bt, qt, kt = back(b, q, k, 2)
                    need(pe, m["pT_ready"], t + 1)
                    need(pe, m["V_ready"], t + 1)
                    need(pe, m["norm_ready"], t)
                    for i in range(QH):
                        mm = pe.matmul(AV[:, i * (DH + 1):(i + 1) * (DH + 1)], probsT[:, qt % 2, i, :],
                                       V[:, kt % 2, QH * qt + i, :], start=True, stop=True)
                    mm.then_inc(m["av_done"], 1)
                if isinstance(s, int) and s == 0:
                    pe.wait_ge(m["G_ready"], 16)
                if valid(b):
                    need(pe, m["G_ready"], 16 * g + QH * (q + 1))
                    need(pe, m["hT_ready"], b + 1)
                    need(pe, m["sub_ready"], s)
                    pe.matmul(SC[:, 0:QH * JN], hT[:, k % 2, :],
                              G[:, g % 2, k, QH * q:QH * q + QH, :].rearrange("p h j -> p (h j)"),
                              start=True, stop=True).then_inc(m["s_done"], 1)
                if valid(b + 1):
                    need(pe, m["cv_ready"], 2 * (b + 2))
                    need(pe, m["V_ready"], s + 4)
                    need(pe, m["oT_ready"], s - 3)
                    for c in range(CC):
                        mm = split3(VO[0:J, 0:QH * DH], ctxv_hi[:, (k + 1) % 2, c, :], ctxv_lo[:, (k + 1) % 2, c, :],
                                    wv_hi[:, c, QH * DH * q:QH * DH * (q + 1)], wv_lo[:, c, QH * DH * q:QH * DH * (q + 1)],
                                    c == 0, c == CC - 1)
                    mm.then_inc(m["V_done"], 1)
                if q == 1 and valid(b - 4):
                    need(pe, m["xs_ready"], b - 3)
                    need(pe, m["x4_ready"], b - 3)
                    pe.transpose(T2[:, 0:S], xs[:, k % 2, 0, 0:D], ident[:, :]).then_inc(m["T4_done"], 1)
                if q == 1 and valid(b - 3):
                    need(pe, m["qT_ready"], b - 2)
                    for i in range(FC):
                        mm = pe.matmul(T1[:, 0:D], q3T[:, i, :], w2q[:, i, :], start=(i == 0), stop=(i == FC - 1))
                    mm.then_inc(m["w2_done"], 1)
                if q == 2 and valid(b - 2):
                    need(pe, m["xq_ready"], b - 1)
                    need(pe, m["x3_ready"], b - 2)
                    pe.transpose(T1[:, 0:S], xq[:, :], ident[:, :]).then_inc(m["xT_done"], 1)
                if q == 3:
                    if valid(b - 3):
                        need(pe, m["T3_ready"], b - 2)
                        need(pe, m["pick_ready"], b - 2)
                        need(pe, m["dep_ready"], b - 2)
                        pe.matmul(T2[:, 0:D], h3T[:, :], w_inT[:, :], start=True, stop=False)
                        pe.matmul(T2[:, 0:D], pick[:, :], dep[:, :], start=False, stop=True).then_inc(m["L1_done"], 1)
                    if valid(b - 2):
                        need(pe, m["hp_ready"], b - 1)
                        need(pe, m["conv_ready"], b - 1)
                        pe.matmul(T1[0:J, 0:D], scanT[:, :], hp[:, :], start=True, stop=True).then_inc(m["dep_done"], 1)
                if valid(s - 1, 4 * B):
                    t = s - 1
                    bt, qt, kt = back(b, q, k, 1)
                    need(pe, m["exp_ready"], t + 1)
                    need(pe, m["pT_ready"], t)
                    for i in range(QH):
                        mm = pe.transpose(PT[0:JN, 128 * i:128 * i + 128], probs[:, qt % 2, i, :], ident[:, :])
                    mm.then_inc(m["pT_done"], 1)
                if valid(g + 1, NG):
                    h = 4 * k + q
                    n = 16 * (g + 1) + h
                    to = G_banks(g)[h % len(G_banks(g))]
                    need(pe, m["G_ready"], n + 1 - len(G_banks(g)))
                    need(pe, m["cThi_ready"], 4 * (g + 2))
                    need(pe, m["cTlo_ready"], 4 * (g + 2))
                    for c in range(CC):
                        mm = split3(to[:, 0:GB * J], A_hi[:, c, h, :], A_lo[:, c, h, :],
                                    ctxT_hi[:, (g + 1) % 2, c, :], ctxT_lo[:, (g + 1) % 2, c, :], c == 0, c == CC - 1)
                    mm.then_inc(m["G_done"], 1)
                if q == 0 and valid(b - 3):
                    need(pe, m["q_ready"], b - 2)
                    need(pe, m["dep_ready"], b - 2)
                    for i in range(FC):
                        mm = pe.transpose(T1[:, 64 * i:64 * i + 64].bitcast(BF16), q3[:, 128 * i:128 * i + 128], ident_bf[:, :])
                    mm.then_inc(m["qT_done"], 1)
                if q == 1:
                    if valid(b - 4):
                        need(pe, m["xsT_ready"], b - 3)
                        pe.matmul(T2[:, 0:E], xsT[:, :], w_gate[:, :], start=True, stop=True).then_inc(m["gate_done"], 1)
                    if not isinstance(b, int) or 0 <= b + 8 < CT_LAST:
                        need(pe, ld_rows[k % 2], 16 * (2 * g + (k + 8) // 2 + 1))
                        need(pe, m["y_taken"], b - 1)
                        need(pe, m["hT_ready"], b + 1)
                        need(pe, m["cThi_ready"], b + 8)
                        need(pe, m["cTlo_ready"], b + 8)
                        for c in range(CC):
                            mm = pe.transpose(YH[:, J * c:J * c + J], rows[:, k % 2, 128 * c:128 * c + 128], ident[0:J, 0:J])
                        mm.then_inc(m["cT_done"], 1)
                if q == 2:
                    if valid(b + 1):
                        need(pe, m["h1_ready"], b + 2)
                        need(pe, m["cThi_ready"], upto(b + 9, CT_LAST))
                        need(pe, m["cTlo_ready"], upto(b + 9, CT_LAST))
                        need(pe, m["y_taken"], b - 1)
                        pe.transpose(YH[:, 0:S], h1[:, :], ident[:, :]).then_inc(m["hT_done"], 1)
                    if valid(b - 2):
                        need(pe, m["xThi_ready"], b - 1)
                        need(pe, m["xTlo_ready"], b - 1)
                        for i in range(3):
                            mm = split3(T1[:, :], xqT_hi[:, i:i + S], xqT_lo[:, i:i + S], tap_hi[:, i, :], tap_lo[:, i, :],
                                        i == 0, i == 2)
                        mm.then_inc(m["conv_done"], 1)
                    if valid(b - 3):
                        need(pe, m["h3_ready"], b - 2)
                        need(pe, m["gate_taken"], b - 3)
                        pe.transpose(T2[:, 0:S], h3[:, :], ident[:, :]).then_inc(m["T3_done"], 1)
                if q == 3 and valid(b - 1):
                    need(pe, m["oT_ready"], 4 * b)
                    need(pe, m["hT_ready"], upto(b + 2, B))
                    need(pe, m["y_taken"], b - 1)
                    for i in range(INNER // 128):
                        mm = pe.matmul(YH[:, 0:D], attnT[:, (k + 1) % 2, i, :], w_out[:, i, :],
                                       start=(i == 0), stop=(i == INNER // 128 - 1))
                    mm.then_inc(m["y_done"], 1)
                if valid(s - 3, 4 * B):
                    t = s - 3
                    bt, qt, kt = back(b, q, k, 3)
                    need(pe, m["norm_ready"], t + 1)
                    need(pe, m["oT_ready"], t)
                    need(pe, m["V_ready"], upto(s + 5, 4 * B))
                    for i in range(2):
                        mm = pe.transpose(VO[:, 256 + 128 * i:384 + 128 * i], attn[:, qt % 2, 128 * i:128 * i + 128], ident[:, :])
                    mm.then_inc(m["oT_done"], 1)

            program(pe, slot)

            pe.wait_ge(m["so_far_ready"], B)
            pe.wait_ge(m["pos_taken"], B)
            pe.matmul(AV[:, 264:264 + E], ones_bf[:, :], so_far[:, :], start=True, stop=True).then_inc(m["n_done"], 1)
            pe.wait_ge(ld["moe"], 16 * (3 + E))
            pe.wait_ge(m["tiles_known"], 1)

            def transpose_rows(i, j):
                pe.wait_ge(m[f"xt_in{j % 4}"], 4 * (i - j % 4) + 16)
                need(pe, m["xT_in"], i - 1)
                pe.transpose(bank[j % 2][:, 0:128], xt[:, j % 4, 0:D], ident[:, :]).then_inc(m["xT_out"], 1)

            def tile(i, j, n=TILES):
                if valid(i, n):
                    pe.wait_ge(m["xT_in"], i + 1)
                    pe.wait_ge(m["w1_in"], i + 1)
                    need(pe, m["hbT_in"], i - 1)
                    for c in range(FFC):
                        mm = pe.matmul(bank[2 + j % 2][:, 128 * c:128 * c + 128], w1_now[:, j % 4, 128 * c:128 * c + 128],
                                       xtT[:, j % 2, :], start=True, stop=True)
                    mm.then_inc(m["h_out"], 1)
                if valid(i + 1, n):
                    transpose_rows(i + 1, j + 1)
                if valid(i - 2, n):
                    pe.wait_ge(m["hbT_in"], i - 1)
                    pe.wait_ge(m["w2_in"], i - 1)
                    need(pe, m["ye_in"], i - 3)
                    for c in range(FFC):
                        mm = pe.matmul(bank[6 + j % 2][:, 0:D], hbT[:, (j + 2) % 4, c, :], w2_now[:, j % 2, c, :], start=(c == 0), stop=(c == FFC - 1))
                    mm.then_inc(m["y_out"], 1)
            transpose_rows(0, 0)
            for j in range(4):
                tile(j, j)
            with pe.Fori(1, TILES // 4 - 1) as u:
                for j in range(4):
                    tile(4 * u + j, j)
            for j in range(6):
                tile(TILES - 4 + j, j)

        @block.scalar
        def _(act):
            for i in range(LEN_LOADS):
                act.dma_start(len_i[B * i:B * i + B, :], a["mask_BxS2_if0"]).then_inc(ld["len"], 16)
            act.dma_start(w1, a["L0_ffn_w1"].rearrange("(c p) d -> p c d", p=128)).then_inc(ld["small"], 16)
            act.dma_start(w2, a["L0_ffn_w2"]).then_inc(ld["small"], 16)
            for n in range(JOBS):
                b8 = bank[n % 8]
                act.wait_ge(prep_pe, n + 1)
                if n < 2:
                    ins = act.activation(wqT[:, 4 * n:4 * n + 4, :].rearrange("p h d -> p (h d)"), b8[:, :], ACT.Copy, scale=SCALE)
                elif n < 6:
                    ins = act.activation(wkT[:, 2 * (n - 2):2 * (n - 2) + 2, :].rearrange("p h c -> p (h c)"), b8[:, :], ACT.Copy)
                elif n < 14:
                    c, h0 = a_job(n)
                    ins = act.activation(A_hi[:, c, h0:h0 + 7:2, :], b8[:, :].rearrange("p (h d) -> p h d", h=4), ACT.Copy)
                elif n == 14:
                    ins = act.activation(gnull[:, :], b8[:, 0:H], ACT.Copy)
                elif n == 15:
                    ins = act.activation(wmean[:, :], b8[:, 0:2], ACT.Copy, scale=1.0 / (F * D))
                elif n == 16:
                    ins = act.activation(w_inT[:, :], b8[:, 0:128], ACT.Copy, scale=g_res[:, :])
                elif n < 20:
                    ins = act.activation(tap_hi[:, n - 17, :], b8[:, :], ACT.Copy)
                else:
                    ins = act.activation(w2q[:, :, :].rearrange("p c d -> p (c d)"), b8[:, 0:256].bitcast(BF16), ACT.Copy)
                ins.then_inc(prep_act, 1)
                if n == 13:
                    act.wait_ge(ld["wv"], 16)
                    act.activation(wv_hi[:, :, :], wv, ACT.Copy).then_inc(prep_split, 1)
                    act.wait_ge(ld["small"], 16 * SMALL)
                    act.activation(gates[:, :], gates[:, :], ACT.Tanh).then_inc(gates_ready, 1)
            act.wait_ge(main_ready, 1)

            def slot(g, k, q, b, s):
                if valid(s - 4, 4 * B):
                    t = s - 4
                    bt, qt, kt = back(b, q, k, 4)
                    need(act, m["oT_done"], t + 1)
                    need(act, m["y_done"], bt - 1)
                    act.activation(attnT[:, kt % 2, 2 * qt:2 * qt + 2, :].rearrange("p c s -> p (c s)"), VO[:, 256:512], ACT.Copy)\
                        .then_inc(m["oT_ready"], 1)
                if valid(b + 1):
                    need(act, m["V_done"], s + 5)
                    need(act, m["av_done"], s - 3)
                    act.activation(V[0:J, (k + 1) % 2, QH * q:QH * q + QH, 0:DH],
                                   VO[0:J, 0:QH * DH].rearrange("p (h d) -> p h d", h=QH), ACT.Copy).then_inc(m["V_ready"], 1)
                if q == 2 and valid(b - 2):
                    need(act, m["xT_done"], b - 1)
                    need(act, m["conv_done"], b - 2)
                    act.activation(xqT_hi[:, 1:S + 1], T1[:, 0:S], ACT.Copy).then_inc(m["xThi_ready"], 1)
                if q == 0 and valid(b - 3):
                    need(act, m["z_ready"], b - 2)
                    need(act, m["qT_done"], b - 3)
                    act.activation(q3[:, :], z3, ACT.Copy, bias=-MAGIC).then_inc(m["q_ready"], 1)
                if valid(b):
                    need(act, m["sub_ready"], s + 1)
                    need(act, m["pT_done"], s - 1)
                    act.activation(probs[:, q % 2, :, :], shifted[:, q % 2, :, :], ACT.Exp).then_inc(m["exp_ready"], 1)
                if q == 1 and valid(b - 4):
                    need(act, m["T4_done"], b - 3)
                    need(act, m["gate_done"], b - 4)
                    act.activation(xsT[:, :], T2[:, 0:S], ACT.Copy).then_inc(m["xsT_ready"], 1)
                if q == 3 and valid(b - 2):
                    need(act, m["conv_ready"], b - 1)
                    need(act, m["c_conv"], 5 * (b - 2))
                    act.activation(tanh_c, conv, ACT.Tanh, scale=0.5).then_inc(m["tanh_ready"], 1)
                if valid(s - 1, 4 * B):
                    t = s - 1
                    bt, qt, kt = back(b, q, k, 1)
                    need(act, m["pT_done"], t + 1)
                    need(act, m["av_done"], t - 1)
                    act.activation(probsT[:, qt % 2, :, :].rearrange("p h s -> p (h s)"), PT[0:JN, :], ACT.Copy)\
                        .then_inc(m["pT_ready"], 1)
                if valid(g + 1, NG):
                    h = 4 * k + q
                    n = 16 * (g + 1) + h
                    need(act, m["G_done"], n + 1)
                    need(act, m["s_done"], 16 * g)
                    act.activation(G[:, (g + 1) % 2, :, h, 0:J], G_banks(g)[h % len(G_banks(g))][:, 0:GB * J].rearrange("p (b j) -> p b j", b=GB), ACT.Copy)\
                        .then_inc(m["G_ready"], 1)
                if q == 0 and valid(b - 3):
                    need(act, m["qT_done"], b - 2)
                    need(act, m["w2_done"], b - 3)
                    act.activation(q3T[:, :, :].rearrange("p c s -> p (c s)"), T1[:, 0:256].bitcast(BF16), ACT.Copy)\
                        .then_inc(m["qT_ready"], 1)
                if q == 1 and (not isinstance(b, int) or 0 <= b + 8 < CT_LAST):
                    need(act, m["cT_done"], b + 9)
                    need(act, m["G_done"], 16 * (g + 1))
                    need(act, m["cv_ready"], upto(2 * (b + 1), 2 * B))
                    act.activation(ctxT_hi[:, g % 2, :, k * J:k * J + J], YH[:, 0:CC * J].rearrange("p (c j) -> p c j", c=CC), ACT.Copy)\
                        .then_inc(m["cThi_ready"], 1)
                if q == 2:
                    if valid(b + 1):
                        need(act, m["hT_done"], b + 2)
                        need(act, m["s_done"], 4 * b)
                        act.activation(hT[:, (k + 1) % 2, :], YH[:, 0:S], ACT.Copy).then_inc(m["hT_ready"], 1)
                    if valid(b - 3):
                        need(act, m["T3_done"], b - 2)
                        need(act, m["L1_done"], b - 3)
                        act.activation(h3T[:, :], T2[:, 0:S], ACT.Copy).then_inc(m["T3_ready"], 1)

            program(act, slot)
            act.wait_ge(m["c_moe"], 1)
            act.activation(gp[:, 1, :], gp[:, 0, :], ACT.Exp).then_inc(m["g_exp"], 1)
            act.wait_ge(m["pads_ready"], 2)
            pad_experts(act, range(E // 2, E))


            def tile(i, j, n=TILES):
                if valid(i, n):
                    act.wait_ge(m["xT_out"], i + 1)
                    need(act, m["h_out"], i - 1)
                    act.activation(xtT[:, j % 2, :], bank[j % 2][:, 0:128], ACT.Copy).then_inc(m["xT_in"], 1)
                if valid(i - 1, n):
                    act.wait_ge(m["h_out"], i)
                    act.wait_ge(m["w1_in"], i)
                    need(act, m["y_out"], i - 4)
                    for c in range(FFC):
                        ins = act.activation(hbT[:, (j + 3) % 4, c, :], bank[2 + (j + 1) % 2][:, 128 * c:128 * c + 128], ACT.Relu,
                                             bias=w1_now[:, (j + 3) % 4, FF + c:FF + c + 1])
                    ins.then_inc(m["hbT_in"], 1)

            for j in range(8):
                tile(j, j)
            with act.Fori(2, TILES // 4) as u:
                for j in range(4):
                    tile(4 * u + j, j)
            tile(TILES, 0)

            for j in range(4):
                act.wait_ge(m[f"ye_st{j}"], 16 * (TILES // 4))
            y_v = ye_d[0:2 * B * S, :].rearrange("(t b p k) d -> t p b k d", b=GB, p=S, k=2)
            for i in range(2):
                act.dma_start(yg[:, i, :, :, :], y_v[i]).then_inc(m[f"got{i}"], 16)
            with act.Fori(1, NG // 2) as u:
                for i in range(2):
                    act.wait_ge(m["moe_sum"], 2 * GB * (2 * u + i - 1))
                    act.dma_start(yg[:, i, :, :, :], y_v[2 * u + i]).then_inc(m[f"got{i}"], 16)

        @block.vector
        def _(dve):
            step = chain(dve, prep_chain, 0)
            dve.wait_ge(ld["small"], 16 * SMALL)
            dve.tensor_reduce(wsum[:, 0:1], w1, AX.XY, ALU.add, apply_absolute_value=True).then_inc(wsum_ready, 1)
            dve.tensor_reduce(wsum[:, 1:2], w2, AX.X, ALU.add, apply_absolute_value=True).then_inc(wsum_ready, 1)
            for n in A_JOBS:
                c, h0 = a_job(n)
                dve.wait_ge(prep_act, n + 1)
                dve.tensor_tensor(A_lo[:, c, h0:h0 + 7:2, :], bank[n % 8][:, :].rearrange("p (h d) -> p h d", h=4),
                                  A_hi[:, c, h0:h0 + 7:2, :].bitcast(F32), ALU.subtract).then_inc(prep_dve, 1)
            dve.wait_ge(prep_act, 16)
            dve.wait_ge(gates_ready, 1)
            step(dve.tensor_scalar(wsum[:, :], wmean[:, :], QUANT_FLOOR, None, ALU.max))
            step(dve.reciprocal(winv[:, :], wsum[:, :]))
            step(dve.tensor_scalar(w1, w1, winv[:, 0:1], -1.0, ALU.mult, ALU.max))
            step(dve.tensor_scalar(w1, w1, 1.0, MAGIC, ALU.min, ALU.add))
            step(dve.tensor_scalar(w1, w1, -MAGIC, wsum[:, 0:1], ALU.add, ALU.mult))
            for c in range(FC):
                for t in range(3):
                    dve.tensor_scalar(wtap[:, c, t, :], w1[:, c, :], tap_gain[:, c, t:t + 1], None, ALU.mult).then_inc(wtap_ready, 1)
            step(dve.tensor_scalar(w2, w2, winv[:, 1:2], -1.0, ALU.mult, ALU.max))
            step(dve.tensor_scalar(w2, w2, 1.0, MAGIC, ALU.min, ALU.add))
            dve.tensor_scalar(w2t, w2, -MAGIC, None, ALU.add).then_inc(w2t_ready, 1)
            step(dve.tensor_scalar(w2_gain[:, :], wsum[:, 1:2], gates[:, 2:3], 0.5, ALU.mult, ALU.mult))
            step(dve.tensor_scalar(ln_gain[:, :], ln_gain[:, :], gates[:, 0:1], None, ALU.mult))
            dve.tensor_scalar(ln_shift[:, :], ln_shift[:, :], gates[:, 0:1], None, ALU.mult).then_inc(shift_ready, 1)
            dve.wait_ge(prep_split, 1)
            dve.tensor_tensor(wv_lo[:, :, :], wv, wv_hi[:, :, :].bitcast(F32), ALU.subtract).then_inc(prep_split, 1)
            for n in TAP_JOBS:
                dve.wait_ge(prep_act, n + 1)
                dve.tensor_tensor(tap_lo[:, n - 17, :], bank[n % 8][:, :], tap_hi[:, n - 17, :].bitcast(F32), ALU.subtract)\
                    .then_inc(prep_dve, 1)
            dve.wait_ge(prep_act, JOBS)
            for i in range(2):
                ins = dve.tensor_copy(G[:, i, :, :, J], gnull[:, :].unsqueeze(1).broadcast_to([128, GB, H]))
            ins.then_inc(main_ready, 1)
            dve.wait_ge(ld["x0"], 16)
            dve.wait_ge(ld["x1"], 16)
            dve.wait_ge(prep_pool, 17)

            def patch_edges():
                dve.wait_ge(ld["len"], 16 * LEN_LOADS)
                dve.wait_ge(prep_pool, 16)
                step(dve.tensor_scalar(len_f[:, :], len_i[:, :], PATCH_CLIP, -PATCH_CLIP, ALU.min, ALU.max))
                step(dve.tensor_tensor_scan(len_sum[:, :], len_f[:, :], zero_row[:, 0:J], 0.0, ALU.add, ALU.add))
                step(dve.tensor_scalar(len_f[:, :], len_sum[:, :], -1.0, None, ALU.add))
                step(dve.tensor_scalar(len_wrap[:, :], len_f[:, :], 0.0, float(S), ALU.is_lt, ALU.mult))
                step(dve.tensor_tensor(len_sum[:, :], len_f[:, :], len_wrap[:, :], ALU.add))
                step(dve.tensor_tensor(eq, len_sum[:, :].unsqueeze(1).broadcast_to([128, 32, J]),
                                       token_no[:, :].unsqueeze(2).broadcast_to([128, 32, J]), ALU.is_equal))
                dve.tensor_reduce(edge[:, :], eq, AX.X, ALU.max).then_inc(edge_ready, 1)

            def patch_numbers():
                dve.wait_ge(ld["row"], 16)
                step(dve.tensor_tensor_scan(edge_sum[:, :], edges[:, :], zero_row[0:B, :], 0.0, ALU.add, ALU.add))
                dve.tensor_scalar(plug[:, :], edge_sum[:, :], 1.0, None, ALU.max).then_inc(plug_ready, 1)

            def stats(b, src, raw, ready, written=None):
                if written:
                    apart(dve, written, b + 1)
                dve.bn_stats(raw[:, :], src).then_inc(ready, 1)

            def moments(b, raw, mv, ready, done):
                apart(dve, ready, b + 1)
                dve.bn_aggr(mv[:, :], raw[:, :]).then_inc(done, 1)

            def norm_by(dst, src, mv, root):
                return dve.tensor_scalar(dst, src, mv[:, 0:1], root[:, 0:1], ALU.subtract, ALU.mult)

            def slot(g, k, q, b, s):
                t = s - 2
                bt, qt, kt = back(b, q, k, 2)
                av = AV[:, 0:QH * (DH + 1)].rearrange("p (h d) -> p h d", h=QH)
                sc = SC[:, 0:QH * JN].rearrange("p (h j) -> p h j", h=QH)
                if isinstance(b, int) and q == 0:
                    if b == -4:
                        patch_edges()
                    if b == -2:
                        patch_numbers()
                    if b == 2:
                        dve.wait_ge(ld["plug"], 16)
                if q == 0 and valid(b - 2):
                    stats(b - 2, YH[:, 0:D], rawy, raw_sem[0], m["y_done"])
                if q == 3 and valid(b - 2):
                    need(dve, m["conv_done"], b - 1)
                    dve.tensor_tensor(conv, T1[:, :], conv_b[:, :], ALU.add).then_inc(m["conv_ready"], 1)
                if valid(t, 4 * B):
                    need(dve, m["av_done"], t + 1)
                    need(dve, m["oT_done"], t - 1)
                    dve.reciprocal(rden[:, qt % 2, :], av[:, :, DH]).then_inc(m["c_norm"], 1)
                if q == 0 and valid(b - 2):
                    moments(b - 2, rawy, mvy, raw_sem[0], m["sty"])
                if valid(b):
                    need(dve, m["s_done"], s + 1)
                    need(dve, m["exp_ready"], s - 1)
                    dve.tensor_reduce(top[:, q % 2, :], sc, AX.X, ALU.max).then_inc(m["c_soft"], 1)
                if valid(t, 4 * B):
                    dve.wait_ge(m["c_norm"], t + 1)
                    dve.tensor_tensor(attn[:, qt % 2, :].rearrange("p (h d) -> p h d", h=QH), av[:, :, 0:DH],
                                      rden[:, qt % 2, :].unsqueeze(2).broadcast_to([128, QH, DH]), ALU.mult)\
                        .then_inc(m["norm_ready"], 1)
                if valid(b):
                    dve.wait_ge(m["c_soft"], s + 1)
                    dve.tensor_tensor(shifted[:, q % 2, :, :], sc, top[:, q % 2, :].unsqueeze(2).broadcast_to([128, QH, JN]),
                                      ALU.subtract).then_inc(m["sub_ready"], 1)
                if q == 0:
                    if valid(b + 1):
                        stats(b + 1, x_res[:, b + 1, :], raw1, raw_sem[1])
                    if valid(b - 2):
                        need(dve, m["rsy"], b - 1)
                        need(dve, m["xb_ready"], b - 1)
                        norm_by(y1[:, :], YH[:, 0:D], mvy, ry).then_inc(m["y_taken"], 1)
                    if valid(b + 1):
                        moments(b + 1, raw1, mv1, raw_sem[1], m["st1"])
                    if valid(b - 2):
                        dve.wait_ge(m["y_taken"], b - 1)
                        dve.tensor_tensor(y2[:, :], y1[:, :], ln_gain[:, :], ALU.mult).then_inc(m["c_y"], 1)
                    if valid(b - 4):
                        need(dve, m["rs4"], b - 3)
                        need(dve, m["T4_done"], b - 5)
                        need(dve, m[f"scattered{k % 2}"], 32 * (2 * g + k // 2 - 2))
                        norm_by(xs[:, k % 2, :, 0:D], x_res[:, b - 4, :].unsqueeze(1).broadcast_to([128, 2, D]), mv4, r4)\
                            .then_inc(m["xs_ready"], 1)
                    if valid(b - 2):
                        dve.wait_ge(m["c_y"], b - 1)
                        dve.tensor_tensor(x_res[:, b - 2, :], y2[:, :], xb[:, :], ALU.add).then_inc(m["x2_ready"], 1)
                    if valid(b - 4):
                        dve.tensor_copy(xs[:, k % 2, :, D], result_row[:, b - 4, :]).then_inc(m["id_ready"], 1)
                    if valid(b - 2):
                        stats(b - 2, x_res[:, b - 2, :], raw2, raw_sem[2], m["x2_ready"])
                        moments(b - 2, raw2, mv2, raw_sem[2], m["st2"])
                if q == 1:
                    if valid(b - 3):
                        need(dve, m["w2_done"], b - 2)
                        need(dve, m["c_conv"], 5 * (b - 2))
                        dve.scalar_tensor_tensor(x_res[:, b - 3, :], T1[:, 0:D], back3[:, (k + 1) % 2:(k + 1) % 2 + 1],
                                                 x_res[:, b - 3, :], ALU.mult, ALU.add).then_inc(m["x3_ready"], 1)
                    if valid(b + 1):
                        need(dve, m["rs1"], b + 2)
                        need(dve, m["hT_done"], b + 1)
                        norm_by(h1[:, :], x_res[:, b + 1, :], mv1, r1).then_inc(m["h1_ready"], 1)
                    if valid(b - 3):
                        stats(b - 3, x_res[:, b - 3, :], raw3, raw_sem[3], m["x3_ready"])
                    if valid(b - 2):
                        need(dve, m["rs2"], b - 1)
                        need(dve, m["xT_done"], b - 2)
                        norm_by(h2[:, :], x_res[:, b - 2, :], mv2, r2).then_inc(m["c_h2"], 1)
                    if valid(b - 3):
                        moments(b - 3, raw3, mv3, raw_sem[3], m["st3"])
                    if valid(b - 2):
                        step = chain(dve, m["c_h2"], 5 * (b - 2) + 1)
                        dve.wait_ge(m["c_h2"], 5 * (b - 2) + 1)
                        step(dve.tensor_reduce(qs2[:, 0:1], h2[:, :], AX.X, ALU.max, apply_absolute_value=True))
                        step(dve.tensor_scalar(qs2[:, 1:2], qs2[:, 0:1], QUANT_FLOOR, 1.0 / 127.0, ALU.max, ALU.mult))
                        step(dve.reciprocal(qs2[:, 2:3], qs2[:, 1:2]))
                        step(dve.tensor_scalar(z2[:, :], h2[:, :], qs2[:, 2:3], MAGIC, ALU.mult, ALU.add))
                        dve.tensor_scalar(xq[:, :], z2[:, :], -MAGIC, qs2[:, 1:2], ALU.add, ALU.mult).then_inc(m["xq_ready"], 1)
                    if not isinstance(b, int) or 0 <= b + 8 < CT_LAST:
                        need(dve, m["cThi_ready"], b + 9)
                        dve.tensor_tensor(ctxT_lo[:, g % 2, :, k * J:k * J + J], YH[:, 0:CC * J].rearrange("p (c j) -> p c j", c=CC),
                                          ctxT_hi[:, g % 2, :, k * J:k * J + J].bitcast(F32), ALU.subtract).then_inc(m["cTlo_ready"], 1)
                if q == 2:
                    if valid(b - 2):
                        need(dve, m["xThi_ready"], b - 1)
                        dve.tensor_tensor(xqT_lo[:, 1:S + 1], T1[:, 0:S], xqT_hi[:, 1:S + 1].bitcast(F32), ALU.subtract)\
                            .then_inc(m["xTlo_ready"], 1)
                    if valid(b - 4):
                        apart(dve, m["gate_done"], b - 3)
                        dve.max(best[:, :], T2[:, 0:E]).then_inc(m["c_gate"], 1)
                    if valid(b - 3):
                        need(dve, m["rs3"], b - 2)
                        need(dve, m["T3_done"], b - 3)
                        norm_by(h3[:, :], x_res[:, b - 3, :], mv3, r3).then_inc(m["h3_ready"], 1)
                    if valid(b - 4):
                        apart(dve, m["c_gate"], 3 * (b - 4) + 1)
                        dve.max_index(best_at[:, :], best[:, :], T2[:, 0:E]).then_inc(m["gate_taken"], 1)
                        dve.tensor_copy(best_all[:, b - 4, :], best[:, 0:2]).then_inc(m["c_gate"], 1)
                    if valid(b - 1):
                        apart(dve, ld_patch[(k + 1) % 2], 16 * (2 * g + (k - 1 - (k + 1) % 2) // 2 + 1))
                        dve.bn_stats(rawc[:, :], patch[:, (k + 1) % 2, :]).then_inc(raw_sem[5], 1)
                    if valid(b - 4):
                        dve.wait_ge(m["gate_taken"], b - 3)
                        dve.tensor_copy(at_all[:, b - 4, :], best_at[:, 0:2]).then_inc(m["c_gate"], 1)
                    if valid(b - 2):
                        need(dve, m["rsc"], b - 1)
                        need(dve, m["dep_done"], b - 2)
                        dve.scalar_tensor_tensor(hp[:, :], patch[:, k % 2, 0:D], rc[:, 0:1], g_init[:, :], ALU.mult, ALU.mult)\
                            .then_inc(m["hp_ready"], 1)
                    if valid(b - 4):
                        dve.wait_ge(m["c_gate"], 3 * (b - 4) + 3)
                        dve.tensor_tensor(chosen[:, :, :], expert_no[:, :].unsqueeze(1).broadcast_to([128, 2, E]),
                                          at_all[:, b - 4, :].unsqueeze(2).broadcast_to([128, 2, E]), ALU.is_equal)\
                            .then_inc(m["c_row"], 1)
                    if valid(b - 3):
                        need(dve, m["L1_done"], b - 3)
                        dve.tensor_scalar(pick[:, :], plug_rows[:, b - 3, :], patch_no[:, :], None, ALU.is_equal)\
                            .then_inc(m["pick_ready"], 1)
                    if valid(b - 4):
                        dve.wait_ge(m["c_row"], 3 * (b - 4) + 1)
                        need(dve, m["pos_done"], b - 4)
                        dve.tensor_tensor(mask[:, :], chosen[:, 0, :], chosen[:, 1, :], ALU.add).then_inc(m["mask_ready"], 1)
                    if valid(b - 1):
                        apart(dve, raw_sem[5], b)
                        dve.bn_aggr(mvc[:, :], rawc[:, :]).then_inc(m["stc"], 1)
                if q == 3:
                    if valid(b - 4):
                        need(dve, m["pos_done"], b - 3)
                        dve.tensor_tensor(row_of[:, :], AV[:, 264:264 + E], first_row[:, :], ALU.add).then_inc(m["pos_taken"], 1)
                        dve.tensor_tensor(so_far[:, :], so_far[:, :], mask[:, :], ALU.add).then_inc(m["so_far_ready"], 1)
                    if valid(b - 3):
                        need(dve, m["L1_done"], b - 2)
                        dve.scalar_tensor_tensor(x_res[:, b - 3, :], T2[:, 0:D], gates[:, 1:2], x_res[:, b - 3, :],
                                                 ALU.mult, ALU.add).then_inc(m["x4_ready"], 1)
                    if valid(b - 4):
                        dve.wait_ge(m["pos_taken"], b - 3)
                        dve.tensor_tensor(row_pick[:, :, :], chosen[:, :, :], row_of[:, :].unsqueeze(1).broadcast_to([128, 2, E]),
                                          ALU.mult).then_inc(m["c_row"], 1)
                    if valid(b - 3):
                        stats(b - 3, x_res[:, b - 3, :], raw4, raw_sem[4], m["x4_ready"])
                    if valid(b - 4):
                        dve.wait_ge(m["c_row"], 3 * (b - 4) + 2)
                        dve.tensor_reduce(row_f[:, :], row_pick[:, :, :], AX.X, ALU.add).then_inc(m["c_row"], 1)
                    if valid(b - 2):
                        need(dve, m["dep_done"], b - 1)
                        need(dve, m["L1_done"], b - 2)
                        dve.tensor_tensor(dep[:, :], T1[0:J, 0:D], b_in[:, :], ALU.add).then_inc(m["dep_ready"], 1)
                    if valid(b - 4):
                        apart(dve, m["c_row"], 3 * (b - 4) + 3)
                        dve.tensor_copy(row_now[:, k % 2, :], row_f[:, :]).then_inc(m["row_ready"], 1)
                    if valid(b - 3):
                        moments(b - 3, raw4, mv4, raw_sem[4], m["st4"])
                    if valid(b - 2):
                        need(dve, m["tanh_ready"], b - 1)
                        need(dve, m["q_ready"], b - 2)
                        step = chain(dve, m["c_conv"], 5 * (b - 2))
                        step(dve.scalar_tensor_tensor(act2, tanh_c, 1.0, conv, ALU.add, ALU.mult))
                        step(dve.tensor_reduce(qs3[:, 0:1], act2, AX.X, ALU.max, apply_absolute_value=True))
                        step(dve.tensor_scalar(qs3[:, 1:2], qs3[:, 0:1], 2 * QUANT_FLOOR, 1.0 / 127.0, ALU.max, ALU.mult))
                        step(dve.reciprocal(qs3[:, 2:3], qs3[:, 1:2]))
                        dve.tensor_scalar(z3, act2, qs3[:, 2:3], MAGIC, ALU.mult, ALU.add).then_inc(m["z_ready"], 1)
                        dve.tensor_scalar(back3[:, k % 2:k % 2 + 1], qs3[:, 1:2], w2_gain[:, :], None, ALU.mult)\
                            .then_inc(m["c_conv"], 1)

            program(dve, slot)

            n = [0]

            def row(ins):
                n[0] += 1
                ins.then_inc(m["c_moe"], 1)
                dve.wait_ge(m["c_moe"], n[0])

            row(dve.tensor_tensor(gp[:, 0, :], best_all[:, :, 1], best_all[:, :, 0], ALU.subtract))
            count, up, tiles, ends = (n_rows[:, i, :] for i in range(4))

            dve.wait_ge(m["n_done"], 1)
            row(dve.tensor_copy(count, AV[0:1, 264:264 + E]))
            dve.tensor_tensor(pad_row[:, :], n_rows[0:1, 0, :], first_row[0:1, :], ALU.add).then_inc(m["rows_known"], 1)
            row(dve.tensor_scalar(up, count, 1.0 / 128, 63.5 / 128, ALU.mult, ALU.add))
            row(dve.tensor_scalar(tiles, up, MAGIC, None, ALU.add))
            row(dve.tensor_scalar(tiles, tiles, -MAGIC, None, ALU.add))
            row(dve.tensor_tensor_scan(ends, tiles, zero_row[0:1, 0:E], 0.0, ALU.add, ALU.add))
            dve.wait_ge(m["q_ready"], B)
            dve.wait_ge(m["G_done"], 16 * NG)
            dve.wait_ge(m["V_done"], 4 * B)
            no_of = tile_no[:, :].unsqueeze(2).broadcast_to([1, TILES, E])
            row(dve.tensor_tensor(at_most, n_rows[0:1, 3, :].unsqueeze(1).broadcast_to([1, TILES, E]), no_of, ALU.is_le))
            row(dve.tensor_reduce(tile_f[:, 0, :], at_most, AX.X, ALU.add))
            row(dve.tensor_tensor(at_most_n, at_most, n_rows[0:1, 2, :].unsqueeze(1).broadcast_to([1, TILES, E]), ALU.mult))
            row(dve.tensor_reduce(tile_f[:, 1, :], at_most_n, AX.X, ALU.add))
            row(dve.tensor_tensor(tile_f[:, 2, :], tile_no[:, :], tile_f[:, 1, :], ALU.subtract))
            row(dve.tensor_scalar(tile_f[:, 3, :], tile_f[:, 0, :], float(CAP), None, ALU.mult))
            row(dve.scalar_tensor_tensor(tile_f[:, 4, :], tile_f[:, 2, :], 128.0, tile_f[:, 3, :], ALU.mult, ALU.add))
            row(dve.tensor_copy(tile_at[:, 0, :], tile_f[:, 4, :]))
            dve.tensor_scalar(tile_at[:, 1, :], tile_f[:, 0, :], float(E - 1), None, ALU.min).then_inc(m["tiles_known"], 1)
            dve.wait_ge(m["tiles_known"], 1)
            dve.wait_ge(m["g_exp"], 1)
            row(dve.tensor_scalar(gp[:, 2, :], gp[:, 1, :], 1.0, None, ALU.add))
            row(dve.reciprocal(gp[:, 3, :], gp[:, 2, :]))
            row(dve.tensor_scalar(gp[:, 3, :], gp[:, 3, :], gates[:, 3:4], None, ALU.mult))
            row(dve.tensor_tensor(gp[:, 4, :], gp[:, 1, :], gp[:, 3, :], ALU.mult))
            dve.wait_ge(ld["moe"], 16 * (3 + E))

            def take_weight(i, j):
                e = expert(dve, i, j)
                need(dve, m["h_out"], i - 3)
                need(dve, m["hbT_in"], i - 3)
                dve.tensor_copy(w1_now[:, j % 4, :], eW1[:, e, :]).then_inc(m["w1_in"], 1)

            def tile(i, j, n=TILES):
                if valid(i + 1, n):
                    take_weight(i + 1, j + 1)
                if valid(i - 1, n):
                    e = expert_before(dve, j, 1)
                    need(dve, m["y_out"], i - 2)
                    dve.tensor_copy(w2_now[:, (j + 1) % 2, :, :], eW2[:, e, :, :]).then_inc(m["w2_in"], 1)
                if valid(i - 2, n):
                    e = expert_before(dve, j, 2)
                    dve.wait_ge(m["y_out"], i - 1)
                    if not isinstance(i, int) or i >= 6:
                        dve.wait_ge(m[f"ye_st{(j + 2) % 4}"], 4 * (i - 2 - (j + 2) % 4) if isinstance(i, int) else 4 * (i - j) + (-16 + 16 * (j // 2)))
                    dve.tensor_tensor(ye[:, (j + 2) % 4, :], bank[6 + j % 2][:, 0:D], b2r[:, e, :], ALU.add).then_inc(m["ye_in"], 1)
                if valid(i - 1, n):
                    dve.wait_ge(m["xT_out"], i)
                    if not isinstance(i, int) or i >= 5:
                        dve.wait_ge(m[f"ye_st{(j + 3) % 4}"], 4 * (i - 1 - (j + 3) % 4) if isinstance(i, int) else 4 * (i - j) - (16 if j == 0 else 0))
                    dve.tensor_copy(row_out[:, (j + 3) % 4, :], xt[:, (j + 3) % 4, D:DX]).then_inc(m["out_id"], 1)

            take_weight(0, 0)
            for j in range(8):
                tile(j, j)
            with dve.Fori(2, TILES // 4 - 1) as u:
                for j in range(4):
                    tile(4 * u + j, j)
            for j in range(6):
                tile(TILES - 4 + j, j)

            def add(u, i):
                t = 2 * u + i
                dve.wait_ge(m[f"got{i}"], 16 * (u + 1))
                for kk in range(2):
                    for jb in range(GB):
                        x_at = x_res[:, GB * t + jb, :]
                        dve.scalar_tensor_tensor(x_at, yg[:, i, jb, kk, :], gp[:, 3 + kk, bass.ds(GB * t + jb, 1)],
                                                 x_at, ALU.mult, ALU.add).then_inc(m["moe_sum"], 1)
                    dve.wait_ge(m["moe_sum"], 2 * GB * t + GB * (kk + 1))

            with dve.Fori(0, NG // 2) as u:
                for i in range(2):
                    add(u, i)


_INS = ["x", "ctx_2048", "mask_BxS2_if0", "g_xattn", "g_ffn", "L0_xattn_Wq", "L0_xattn_Wkv", "L0_xattn_null_kv",
        "L0_xattn_Wout", "L0_xattn_ln_scale", "L0_xattn_ln_bias", "L0_ffn_w1", "L0_ffn_conv_w", "L0_ffn_conv_b",
        "L0_ffn_w2", "L1_xattn_W_in", "L1_xattn_b_in", "L1_xattn_g_res", "L1_xattn_g_init", "L1_ffn_Wg", "L1_ffn_W1",
        "L1_ffn_b1", "L1_ffn_W2", "L1_ffn_b2"]


def kernel(**inputs):
    import concourse.bacc as bacc
    from concourse.bass_utils import run_bass_kernel_spmd

    nc = bacc.Bacc("TRN2", target_bir_lowering=False, num_devices=1)
    arrays, handles = {}, {}
    for name in _INS:
        arr = np.ascontiguousarray(inputs[name])
        arrays[name] = arr
        handles[name] = nc.dram_tensor(name, arr.shape, mybir.dt.from_np(arr.dtype), kind="ExternalInput").ap()
    out = nc.dram_tensor("out", arrays["x"].shape, F32, kind="ExternalOutput").ap()
    build(nc, handles, out)
    r = run_bass_kernel_spmd(nc, [arrays], core_ids=[0])
    return r.results[0]["out"]
```
